# Optimizing a Trainium2 kernel written in Bass

```python
import numpy as np
import jax
import jax.numpy as jnp

def _softmax(x, axis=-1):
    return jax.nn.softmax(x, axis=axis)

def _gelu(x):
    return jax.nn.gelu(x, approximate=True)

def _silu(x):
    return jax.nn.silu(x)

def _sigmoid(x):
    return jax.nn.sigmoid(x)

def _layernorm(x, axis=-1, eps=1e-05):
    m = jnp.mean(x, axis=axis, keepdims=True)
    v = jnp.var(x, axis=axis, keepdims=True)
    return (x - m) / jnp.sqrt(v + eps)

def _scatter_add(tgt, idx, src, axis=0):
    return tgt.at[idx].add(src)

def _segment_sum(src, seg, n):
    return jax.ops.segment_sum(src, seg, n)
kernel_name = 'mk_flamingo_gated_d1_seqx_r8_ae7b15'

def setup_inputs(seed: int=0):
    np.random.seed(seed)
    _w = jnp.asarray

    def _rec_inputs():
        import jax
        import jax.numpy as jnp
        _rk = jax.random.key(seed)
        x = -0.0003929 + 0.9999 * jax.random.normal(jax.random.fold_in(_rk, 1), (8, 256, 256), jnp.float32)
        _lenS = 256 - jax.random.randint(jax.random.fold_in(_rk, 7), (8,), 0, max(1, 256 // 4) + 1, jnp.int32)
        _lenS2 = 1601 - jax.random.randint(jax.random.fold_in(_rk, 8), (8,), 0, max(1, 1601 // 4) + 1, jnp.int32)
        _ctx_1024P = jax.random.normal(jax.random.fold_in(_rk, 11), (8, 16, 128), jnp.float32)
        _ctx_1024c = jax.random.dirichlet(jax.random.fold_in(_rk, 511), 0.3 * jnp.ones((16,), jnp.float32), (8, 1601))
        _ctx_1024t = jnp.einsum('bsk,bkd->bsd', _ctx_1024c, _ctx_1024P)
        _ctx_1024t = _ctx_1024t * jax.lax.rsqrt(jnp.mean(jnp.square(_ctx_1024t)) + 1e-12) * 0.953939
        ctx_1024 = 0.000227908 + 0.99994 * (_ctx_1024t + 0.3 * jax.random.normal(jax.random.fold_in(_rk, 611), (8, 1601, 128), jnp.float32))
        _g = jax.random.normal(jax.random.fold_in(_rk, 9001), (2, 1), jnp.float32)
        _g = jnp.sign(_g) * jnp.maximum(jnp.abs(_g), 1.0) + (_g == 0) * 1.0
        g_xattn = _g[0]
        g_ffn = _g[1]
        return (x, ctx_1024, g_xattn, g_ffn)
    x, ctx_1024, g_xattn, g_ffn = _rec_inputs()

    def _L0_xattn_setup():
        import jax, jax.numpy as jnp
        import numpy as np
        EPS = 1e-05

        def rmsnorm(x, g, eps=EPS):
            var = jnp.mean(jnp.square(x), axis=-1, keepdims=True)
            return x * jax.lax.rsqrt(var + eps) * g
        key = jax.random.key(seed)
        ks = jax.random.split(key, 8)
        B, Sq, Skv = (2, 512, 64)
        dim, cdim, H, D = (256, 128, 16, 128)
        inner = H * D
        s = lambda f: 1.0 / np.sqrt(f)
        return {'hidden_states': jax.random.normal(ks[0], (B, Sq, dim), jnp.float32), 'encoder_hidden_states': jax.random.normal(ks[1], (B, Skv, cdim), jnp.float32), 'Wq': jax.random.normal(ks[2], (dim, inner), jnp.float32) * s(dim), 'Wk': jax.random.normal(ks[3], (cdim, inner), jnp.float32) * s(cdim), 'Wv': jax.random.normal(ks[4], (cdim, inner), jnp.float32) * s(cdim), 'Wo': jax.random.normal(ks[5], (inner, dim), jnp.float32) * s(inner), 'gq': jnp.ones((D,), jnp.float32), 'gk': jnp.ones((D,), jnp.float32)}
    _L0_xattn_all = _L0_xattn_setup()
    _L0_xattn_in = {k: v for k, v in _L0_xattn_all.items() if k in ('Wq', 'Wk', 'Wv', 'Wo', 'gq', 'gk')}
    del _L0_xattn_all

    def _L0_ffn_setup():
        import jax, jax.numpy as jnp
        import numpy as np
        E, H, I = (8, 256, 512)
        TOP_K = 1
        B, S = (1, 256)
        key = jax.random.key(seed)
        ks = jax.random.split(key, 7)
        std = 0.02
        return {'hidden_states': jax.random.normal(ks[0], (B, S, H), dtype=jnp.float32), 'router_w': jax.random.normal(ks[1], (E, H), dtype=jnp.float32) * std, 'gate_up_proj': jax.random.normal(ks[2], (E, H, 2 * I), dtype=jnp.float32) * std, 'down_proj': jax.random.normal(ks[3], (E, I, H), dtype=jnp.float32) * std, 'shared_gate_w': jax.random.normal(ks[4], (H, I), dtype=jnp.float32) * std, 'shared_up_w': jax.random.normal(ks[5], (H, I), dtype=jnp.float32) * std, 'shared_down_w': jax.random.normal(ks[6], (I, H), dtype=jnp.float32) * std}
    _L0_ffn_all = _L0_ffn_setup()
    _L0_ffn_in = {k: v for k, v in _L0_ffn_all.items() if k in ('router_w', 'gate_up_proj', 'down_proj', 'shared_gate_w', 'shared_up_w', 'shared_down_w')}
    del _L0_ffn_all
    return {'x': x, 'ctx_1024': ctx_1024, 'g_xattn': g_xattn, 'g_ffn': g_ffn, 'L0_xattn_Wq': _L0_xattn_in['Wq'], 'L0_xattn_Wk': _L0_xattn_in['Wk'], 'L0_xattn_Wv': _L0_xattn_in['Wv'], 'L0_xattn_Wo': _L0_xattn_in['Wo'], 'L0_xattn_gq': _L0_xattn_in['gq'], 'L0_xattn_gk': _L0_xattn_in['gk'], 'L0_ffn_router_w': _L0_ffn_in['router_w'], 'L0_ffn_gate_up_proj': _L0_ffn_in['gate_up_proj'], 'L0_ffn_down_proj': _L0_ffn_in['down_proj'], 'L0_ffn_shared_gate_w': _L0_ffn_in['shared_gate_w'], 'L0_ffn_shared_up_w': _L0_ffn_in['shared_up_w'], 'L0_ffn_shared_down_w': _L0_ffn_in['shared_down_w']}

def reference(x, ctx_1024, g_xattn, g_ffn, L0_xattn_Wq, L0_xattn_Wk, L0_xattn_Wv, L0_xattn_Wo, L0_xattn_gq, L0_xattn_gk, L0_ffn_router_w, L0_ffn_gate_up_proj, L0_ffn_down_proj, L0_ffn_shared_gate_w, L0_ffn_shared_up_w, L0_ffn_shared_down_w):
    import jax
    import jax.numpy as jnp

    def _L0_xattn_ref(hidden_states, encoder_hidden_states, Wq, Wk, Wv, Wo, gq, gk):
        import jax, jax.numpy as jnp
        import numpy as np
        EPS = 1e-05

        def rmsnorm(x, g, eps=EPS):
            var = jnp.mean(jnp.square(x), axis=-1, keepdims=True)
            return x * jax.lax.rsqrt(var + eps) * g
        B, Sq, _ = hidden_states.shape
        Skv = encoder_hidden_states.shape[1]
        D = gq.shape[0]
        H = Wq.shape[1] // D
        scale = 1.0 / np.sqrt(D)
        q = (hidden_states @ Wq).reshape(B, Sq, H, D)
        k = (encoder_hidden_states @ Wk).reshape(B, Skv, H, D)
        v = (encoder_hidden_states @ Wv).reshape(B, Skv, H, D)
        q = rmsnorm(q, gq)
        k = rmsnorm(k, gk)
        scores = jnp.einsum('bqhd,bkhd->bhqk', q, k) * scale
        attn = jax.nn.softmax(scores, axis=-1)
        out = jnp.einsum('bhqk,bkhd->bqhd', attn, v)
        out = out.reshape(B, Sq, H * D)
        return out @ Wo

    def _L0_ffn_ref(hidden_states, router_w, gate_up_proj, down_proj, shared_gate_w, shared_up_w, shared_down_w):
        import jax, jax.numpy as jnp
        import numpy as np
        E, H, I = (8, 256, 512)
        TOP_K = 1
        B, S = (1, 256)
        orig_shape = hidden_states.shape
        x = hidden_states.reshape(-1, H)
        T = x.shape[0]
        logits = x @ router_w.T
        top_vals, top_idx = jax.lax.top_k(logits, TOP_K)
        scores = jnp.full_like(logits, -jnp.inf)
        scores = scores.at[jnp.arange(T)[:, None], top_idx].set(top_vals)
        scores = jax.nn.sigmoid(scores.astype(jnp.float32)).astype(logits.dtype)
        xr = x[None, :, :] * scores.T[:, :, None]
        gate_up = jnp.einsum('eth,ehf->etf', xr, gate_up_proj)
        gate, up = jnp.split(gate_up, 2, axis=-1)
        routed = jnp.einsum('etf,efh->eth', up * jax.nn.silu(gate), down_proj)
        routed_sum = routed.sum(axis=0)
        shared = jax.nn.silu(x @ shared_gate_w) * (x @ shared_up_w) @ shared_down_w
        return (shared + routed_sum).reshape(orig_shape)
    x = x + jnp.tanh(g_xattn[0]) * _L0_xattn_ref(_layernorm(x, axis=-1), ctx_1024, L0_xattn_Wq, L0_xattn_Wk, L0_xattn_Wv, L0_xattn_Wo, L0_xattn_gq, L0_xattn_gk)
    x = x + jnp.tanh(g_ffn[0]) * _L0_ffn_ref(_layernorm(x, axis=-1), L0_ffn_router_w, L0_ffn_gate_up_proj, L0_ffn_down_proj, L0_ffn_shared_gate_w, L0_ffn_shared_up_w, L0_ffn_shared_down_w)
    return x

_drawn_inputs = setup_inputs


def setup_inputs(seed=0):
    import zlib

    import numpy as np

    out = dict(_drawn_inputs(seed))
    spreads = {'L0_xattn_gq': (1.0, 0.536), 'L0_xattn_gk': (1.0, 0.6)}
    factors = {'L0_ffn_router_w': 7.479,
     'L0_ffn_gate_up_proj': 6.932,
     'L0_ffn_down_proj': 6.918,
     'L0_ffn_shared_gate_w': 2.739,
     'L0_ffn_shared_up_w': 2.712,
     'L0_ffn_shared_down_w': 2.694}
    for name, (base, spread) in spreads.items():
        noise = np.random.default_rng([zlib.crc32(name.encode()), seed]).standard_normal(out[name].shape)
        drawn = base * np.exp(spread * noise) if base else spread * noise
        out[name] = jnp.asarray(drawn.astype(out[name].dtype))
    for name, factor in factors.items():
        out[name] = (out[name] * factor).astype(out[name].dtype)
    return out
```

```python
from contextlib import ExitStack

import concourse.bass as bass
from concourse import mybir

F32 = mybir.dt.float32
F16 = mybir.dt.float16
BF16 = mybir.dt.bfloat16
I32 = mybir.dt.int32
ALU = mybir.AluOpType
ACT = mybir.ActivationFunctionType
X = mybir.AxisListType.X
ds = bass.ds

P = 128
EPS = 1e-5
LN_P_SCALE = 6.931471805599453
P_SCALE = 1024.0
RSQRT_MAGIC = 1597463007
NEG = -3.0e38


class Chain:

    def __init__(self, eng, sem, base=0):
        self.eng, self.sem, self.base, self.n = eng, sem, base, 0

    def __call__(self, ins):
        self.n += 1
        ins.then_inc(self.sem, 1)
        self.eng.wait_ge(self.sem, self.base + self.n)


def flamingo_layer(nc, x, ctx, g_xattn, g_ffn, Wq, Wk, Wv, Wo, gq, gk,
                   router_w, gate_up, down, sh_gate, sh_up, sh_down, out):
    B, SQ, DM = x.shape
    KV, DC = ctx.shape[1], ctx.shape[2]
    D = gq.shape[0]
    H = Wq.shape[1] // D
    QT, KT = SQ // P, DM // P
    NT = B * QT
    FT = KV // P
    LAST = KV - FT * P
    NKT = FT + 1
    NG = (NKT + 1) // 2
    INNER = H * D
    E, _, F2 = gate_up.shape
    FF = F2 // 2
    FTT = FF // P
    NE = E + 1
    assert DC == P and D == P and SQ == 256 and H % 2 == 0
    CH = [(0, 401), (401, 400), (801, 400), (1201, 400)]
    assert CH[-1][0] + CH[-1][1] == KV
    SCORE_BANK = [0, 1, 2, 0, 1, 2, 0, 1]
    KROWS = [P] * FT + [LAST]

    top = ExitStack()
    with top:
        def sem(name):
            return top.enter_context(nc.semaphore(name))

        def sb(name, shape, dt, stack=top):
            return stack.enter_context(nc.sbuf_tensor(name, shape, dt))

        x_all = sb("x_all", [P, NT, DM], F32)
        ident = sb("ident", [P, P], F32)
        ident16 = sb("ident16", [P, P], BF16)
        ones = sb("ones", [P, 1], F32)
        gates = sb("gates", [P, 4], F32)
        g1 = sb("g1", [P, 1], F32)
        gcol = sb("gcol", [P, 3], F32)
        ssc = sb("ssc", [P, 3, NKT * H], F32)
        stats = sb("stats", [P, QT, 6], F32)
        mv = sb("mv", [P, QT, 2], F32)
        rstd = sb("rstd", [P, QT], F32)
        att = ExitStack()
        wq_hi = sb("wq_hi", [P, KT, INNER], F16, att)
        wq_lo = sb("wq_lo", [P, KT, INNER], F16, att)
        wk_hi = sb("wk_hi", [P, INNER], F16, att)
        wk_lo = sb("wk_lo", [P, INNER], F16, att)
        wkt_hi = sb("wkt_hi", [P, H, P], F16, att)
        wkt_lo = sb("wkt_lo", [P, H, P], F16, att)
        vo_hi = sb("vo_hi", [P, H, DM], F16, att)
        vo_lo = sb("vo_lo", [P, H, DM], F16, att)
        ctx_f = sb("ctx_f", [P, NKT, P], F32, att)
        ctx_hi = sb("ctx_hi", [P, NKT, P], F16, att)
        ctx_lo = sb("ctx_lo", [P, NKT, P], F16, att)
        ctxt_hi = sb("ctxt_hi", [P, KV], F16, att)
        ctxt_lo = sb("ctxt_lo", [P, KV], F16, att)
        xn = sb("xn", [P, QT, DM], F32, att)
        xnt_hi = sb("xnt_hi", [P, KT, SQ], F16, att)
        xnt_lo = sb("xnt_lo", [P, KT, SQ], F16, att)
        SP = [[sb(f"sp{u}{t}", [P, KV], F32, att) for t in range(QT)] for u in range(2)]
        RK = [sb(f"rk_bcast{u}", [P, KV], F32, att) for u in range(2)]
        pt_hi = sb("pt_hi", [P, NG, 2, SQ], F16, att)
        pt_lo = sb("pt_lo", [P, NG, 2, SQ], F16, att)
        qp_hi = sb("qp_hi", [P, H, SQ], F16, att)
        qp_lo = sb("qp_lo", [P, H, SQ], F16, att)
        q_hi = sb("q_hi", [P, 2, SQ], F16, att)
        q_lo = sb("q_lo", [P, 2, SQ], F16, att)
        q_sq = sb("q_sq", [P, 2, SQ], F32, att)
        k_sq = sb("k_sq", [P, 2, 512], F32, att)
        ssk = sb("ssk", [P, NKT, H], F32, att)
        rk3 = sb("rk3", [P, NKT, 3, H], BF16, att)
        rkt = sb("rkt", [3 * H, KV], BF16, att)
        sel = sb("sel", [3 * H, H, P], BF16, att)
        rq = sb("rq", [P, QT, H], F32, att)
        nrq = sb("nrq", [P, QT, H], F32, att)
        mx4 = sb("mx4", [P, QT, 4], F32, att)
        mx = sb("mx", [P, QT], F32, att)
        nbias = sb("nbias", [P, QT], F32, att)
        psum_p = sb("psum_p", [P, 2, QT], F32, att)
        rden = sb("rden", [P, QT], F32, att)
        ot_hi = sb("ot_hi", [P, SQ], F16, att)
        ot_lo = sb("ot_lo", [P, SQ], F16, att)
        att.close()
        ffn = ExitStack()
        xn2 = sb("xn2", [P, NT, DM], F32, ffn)
        xt_hi = sb("xt_hi", [P, NT, KT, P], F16, ffn)
        xt_lo = sb("xt_lo", [P, NT, KT, P], F16, ffn)
        wstage = sb("wstage", [P, KT * F2 + FTT * DM], F32, ffn)
        w_hi = sb("w_hi", [P, 2, KT * F2 + FTT * DM], F16, ffn)
        w_lo = sb("w_lo", [P, 2, KT * F2 + FTT * DM], F16, ffn)
        silu = sb("silu", [P, 2, FF], F32, ffn)
        hmid = sb("hmid", [P, 2, FF], F32, ffn)
        st2 = sb("st2", [P, NT, 6], F32, ffn)
        mv2 = sb("mv2", [P, NT, 2], F32, ffn)
        rwt_hi = sb("rwt_hi", [P, KT, E], F16, ffn)
        rwt_lo = sb("rwt_lo", [P, KT, E], F16, ffn)
        ht_hi = sb("ht_hi", [P, 2, FTT, P], F16, ffn)
        ht_lo = sb("ht_lo", [P, 2, FTT, P], F16, ffn)
        rw = sb("rw", [E, DM], F32, ffn)
        logit = sb("logit", [P, NT, E], F32, ffn)
        smax = sb("smax", [P, 4, NT], F32, ffn)
        sw = sb("sw", [P, NE, NT], F32, ffn)
        ffn.close()

        bank = [top.enter_context(nc.psum_tensor(f"bank{i}", [P, 512], F32)) for i in range(8)]
        S_BANK, T_BANK, O_BANK, V_BANK, R_BANK = bank[0:3], bank[3:6], bank[6], bank[7], bank[7]
        rkt_ps = [b[:, :].bitcast(BF16) for b in (bank[0], bank[1])]

        ld = {n: sem("ld_" + n) for n in ("x", "small", "wk", "wv", "wo", "wq")}
        c_done = sem("consts_done")
        w_split, wk_t, wk_ts, wv_t, wv_ts, vo_ps, vo_s = map(sem, (
            "wsplit", "wkt_ps", "wkt_split", "wvt_ps", "wvt_copied", "vo_ps", "vo_split"))
        setup_chain = sem("setup_chain")
        ctx_ld, ctx_free, xn_ready = map(sem, ("ctx_ld", "ctx_free", "xn_ready"))
        tp_ps, tp_hi, tp_lo = map(sem, ("tp_ps", "tp_hi", "tp_lo"))
        kn_ps, kn_sq, kn_sum = map(sem, ("kn_ps", "kn_sq", "kn_sum"))
        q_ps, q_hi_s, q_lo_s, qp_ps, qp_hi_s, qp_lo_s, rq_ps = map(sem, (
            "q_ps", "q_hi_s", "q_lo_s", "qp_ps", "qp_hi_s", "qp_lo_s", "rq_ps"))
        rk_ready, rkt_tp, rkt_ready, rq_ready = map(sem, ("rk_ready", "rkt_tp", "rkt_ready", "rq_ready"))
        prep_chain, max_chain, den_chain, ctx_split, mem0 = map(sem, (
            "prep_chain", "max_chain", "den_chain", "ctx_hi_done", "ssk_set"))
        s_rb, s_rbc, s_sc, s_scd, s_nb, s_exp, s_tr, s_hi, s_lo, s_pv, s_oh, s_ol, s_vo, s_acc = map(sem, (
            "rb_ps", "rb_copied", "score_ps", "score_used", "bias_ready", "exp_done", "pt_ps", "pt_hi_done",
            "pt_lo_done", "pv_done", "ot_hi_done", "ot_lo_done", "vo_done", "head_added"))
        f_ld, f_w, f_wfree, f_small = map(sem, ("f_ld", "f_wsplit", "f_wfree", "f_small"))
        f_xn, f_tp, f_thi, f_tlo, f_rt, f_rtc, f_lg, f_lgc, f_sel = map(sem, (
            "f_xn", "f_tp", "f_thi", "f_tlo", "f_rt", "f_rtc", "f_lg", "f_lgc", "f_sel"))
        f_g, f_whi, f_dma = sem("f_g"), sem("f_whi"), sem("f_dma")
        f_gu, f_silu, f_h, f_ht, f_hhi, f_hlo, f_y, f_acc, f_chain = map(sem, (
            "f_gu", "f_silu", "f_h", "f_ht", "f_hhi", "f_hlo", "f_y", "f_acc", "f_chain"))
        st = sem("stored")
        paced_dve, paced_pe = sem("paced_dve"), sem("paced_pe")
        w_hi_s, gate_s, q_sq_s, rkt_c, ctx_lo_s = map(sem, ("w_hi_done", "gate_tanh", "q_squared", "rkt_first", "ctx_lo_done"))
        PREP_STEPS = 4 + 1 + 11 + 2 + 1 + 11 + 3 + 1 + 11 + 1

        block = top.enter_context(nc.Block())

        stage_wk = [SP[0][0][:, 0:1024], SP[0][1][:, 0:1024]]
        stage_wv = [SP[1][0][:, 0:1024], SP[1][1][:, 0:1024]]
        stage_wo = ctx_f[:, :, :].rearrange("p t c -> p (t c)")
        wvt = RK[1][:, :]

        def splits3(pe, ps, lhs, rhs, start=True, stop=True):
            pe.matmul(ps, lhs[0], rhs[0], start=start, stop=False)
            pe.matmul(ps, lhs[0], rhs[1], start=False, stop=False)
            return pe.matmul(ps, lhs[1], rhs[0], start=False, stop=stop)

        def group_parts(g):
            if 2 * g + 1 < FT:
                return [(P, slice(0, 2))]
            return [(KROWS[2 * g + i], slice(i, i + 1)) for i in range(2) if 2 * g + i < NKT]

        def rsqrt(dve, chain, v, y, t):
            chain(dve.tensor_scalar(t.bitcast(I32), v.bitcast(I32), 1, None, ALU.logical_shift_right))
            chain(dve.tensor_scalar(y.bitcast(I32), t.bitcast(I32), -1.0, float(RSQRT_MAGIC), ALU.mult, ALU.add))
            for _ in range(3):
                chain(dve.tensor_tensor(t, y, y, ALU.mult))
                chain(dve.scalar_tensor_tensor(out=t, in0=t, scalar=-0.5, in1=v, op0=ALU.mult, op1=ALU.mult))
                chain(dve.scalar_tensor_tensor(out=y, in0=t, scalar=1.5, in1=y, op0=ALU.add, op1=ALU.mult))

        @block.sync
        def _(sp):
            for k in range(2):
                sp.dma_start(stage_wk[k], Wk[:, k * 1024:(k + 1) * 1024]).then_inc(ld["wk"], 16)
            sp.dma_start(gcol[:, 0:1], gq.rearrange("(d a) -> d a", a=1)).then_inc(ld["small"], 16)
            sp.dma_start(gcol[:, 1:2], gk.rearrange("(d a) -> d a", a=1)).then_inc(ld["small"], 16)
            sp.dma_start(gates[:, 0:1], g_xattn.rearrange("(a b) -> a b", a=1).broadcast_to([P, 1])).then_inc(ld["small"], 16)
            sp.dma_start(gates[:, 1:2], g_ffn.rearrange("(a b) -> a b", a=1).broadcast_to([P, 1])).then_inc(ld["small"], 16)
            for k in range(2):
                sp.dma_start(stage_wv[k], Wv[:, k * 1024:(k + 1) * 1024]).then_inc(ld["wv"], 16)
            sp.dma_start(x_all[:, :, :], x.rearrange("b (t p) m -> p (b t) m", p=P)).then_inc(ld["x"], 16)
            for c in range(4):
                if c:
                    sp.wait_ge(vo_ps, 4 * c)
                sp.dma_start(stage_wo[:, 0:4 * DM].rearrange("p (h m) -> p h m", h=4),
                             Wo[c * 4 * D:(c + 1) * 4 * D, :].rearrange("(h d) m -> d h m", d=D)).then_inc(ld["wo"], 16)
            for k in range(KT):
                for s in range(2):
                    n = 2 * k + s
                    buf = (stage_wk + stage_wv)[n]
                    if n == 0:
                        sp.wait_ge(wk_t, H)
                        sp.wait_ge(w_split, 2)
                        sp.wait_ge(wv_t, H)
                    sp.dma_start(buf, Wq[k * P:(k + 1) * P, s * 1024:(s + 1) * 1024]).then_inc(ld["wq"], 16)
            with sp.Fori(0, B) as b:
                sp.wait_ge(vo_ps, H)
                sp.wait_ge(ctx_free, b + 1)
                sp.dma_start(ctx_f[:, 0:FT, :], ctx[ds(b, 1), 0:FT * P, :].rearrange("a (t p) c -> p (a t) c", p=P)
                             ).then_inc(ctx_ld, 16)
                sp.dma_start(ctx_f[0:LAST, FT, :], ctx[ds(b, 1), FT * P:KV, :].rearrange("a p c -> p (a c)")
                             ).then_inc(ctx_ld, 16)
            gu_v = wstage[:, 0:KT * F2].rearrange("p (k f) -> p k f", k=KT)
            dn_v = wstage[:, KT * F2:].rearrange("p (f m) -> p f m", f=FTT)
            sp.wait_ge(s_acc, B * H + 1)
            sp.dma_start(rw[:, :], router_w).then_inc(f_small, 16)
            with sp.Fori(0, E) as e:
                sp.wait_ge(f_w, e + 1)
                sp.dma_start(gu_v, gate_up[ds(e, 1)].rearrange("a (k p) f -> p (a k) f", p=P)).then_inc(f_ld, 16)
                sp.dma_start(dn_v, down[ds(e, 1)].rearrange("a (f p) m -> p (a f) m", p=P)).then_inc(f_ld, 16)
            sp.wait_ge(f_w, E + 1)
            sp.dma_start(gu_v[:, :, 0:FF], sh_gate.rearrange("(k p) f -> p k f", p=P)).then_inc(f_ld, 16)
            sp.dma_start(gu_v[:, :, FF:F2], sh_up.rearrange("(k p) f -> p k f", p=P)).then_inc(f_ld, 16)
            sp.dma_start(dn_v, sh_down.rearrange("(f p) m -> p f m", p=P)).then_inc(f_ld, 16)
            with sp.Fori(0, NT) as t:
                sp.wait_ge(f_acc, E * NT + 2 + t)
                sp.dma_start(out.rearrange("b (t p) m -> p (b t) m", p=P)[:, ds(t, 1), :], x_all[:, ds(t, 1), :]
                             ).then_inc(st, 16)
            sp.wait_ge(st, 16 * NT)

        @block.gpsimd
        def _(pool):
            pool.memset(ident[:, :], 0.0).then_inc(c_done, 1)
            pool.memset(ident16[:, :], 0.0).then_inc(c_done, 1)
            pool.memset(sel[:, :, :], 0.0).then_inc(c_done, 1)
            pool.memset(ones[:, :], 1.0).then_inc(c_done, 1)
            n = 4
            for buf in (ident, ident16):
                pool.wait_ge(c_done, n)
                pool.affine_select(out=buf[:, :], in_=buf[:, :], compare_op=ALU.not_equal, fill=1.0, base=0,
                                   pattern=[[-1, P]], channel_multiplier=1).then_inc(c_done, 1)
                n += 1
            for r in range(3):
                pool.wait_ge(c_done, n)
                pool.affine_select(out=sel[:, :, :], in_=sel[:, :, :], compare_op=ALU.not_equal, fill=1.0,
                                   base=-H * r, pattern=[[-1, H], [0, P]], channel_multiplier=1).then_inc(c_done, 1)
                n += 1
        CONSTS = 9

        @block.tensor
        def _(pe):
            pe.wait_ge(c_done, CONSTS)
            for h in range(H):
                if h == 0:
                    pe.wait_ge(ld["wk"], 32)
                if h >= 2:
                    pe.wait_ge(wk_ts, h - 1)
                pe.transpose(T_BANK[h % 2][:, 0:P], stage_wk[h // 8][:, (h % 8) * P:(h % 8 + 1) * P], ident[:, :]
                             ).then_inc(wk_t, 1)
            for h in range(H):
                if h == 0:
                    pe.wait_ge(ld["wv"], 32)
                if h >= 2:
                    pe.wait_ge(wv_ts, h - 1)
                pe.transpose(S_BANK[h % 2][:, 0:P], stage_wv[h // 8][:, (h % 8) * P:(h % 8 + 1) * P], ident[:, :]
                             ).then_inc(wv_t, 1)
                if h % 4 == 0:
                    pe.wait_ge(ld["wo"], 4 * h + 16)
                pe.wait_ge(wv_ts, h + 1)
                if h >= 1:
                    pe.wait_ge(vo_s, h)
                pe.matmul(O_BANK[:, 0:DM], wvt[:, (h % 8) * P:(h % 8 + 1) * P],
                          stage_wo[:, (h % 4) * DM:(h % 4 + 1) * DM], start=True, stop=True).then_inc(vo_ps, 1)
            pe.wait_ge(wk_ts, H)
            pe.wait_ge(vo_s, H)
            pe.wait_ge(w_split, 6)

            with pe.Fori(0, B) as b:
                pe.wait_ge(ctx_ld, b * 32 + 32)
                pe.wait_ge(s_acc, b * H + 1)
                for c in range(4):
                    for t in range(4 * c, min(4 * c + 4, NKT)):
                        r = KROWS[t]
                        m = pe.transpose(bank[c][:, (t - 4 * c) * P:(t - 4 * c) * P + r], ctx_f[0:r, t, :],
                                         ident[0:r, 0:r])
                    m.then_inc(tp_ps, 1)
                pe.wait_ge(xn_ready, b + 1)
                for k in range(KT):
                    for t in range(QT):
                        m = pe.transpose(bank[4][:, k * SQ + t * P:k * SQ + (t + 1) * P], xn[:, t, k * P:(k + 1) * P],
                                         ident[:, :])
                m.then_inc(tp_ps, 1)
                pe.wait_ge(tp_lo, b * 5 + 5)
                pe.sem_inc(paced_pe, 1)

                def key_tile(t, r):
                    for g in range(4):
                        pe.wait_ge(kn_sq, (b * NKT + t) * 4 + g + 1)
                        cols = ds(t * P, r)
                        splits3(pe, bank[g][0:r, :], (ctxt_hi[:, cols], ctxt_lo[:, cols]),
                                (wk_hi[:, g * 512:(g + 1) * 512], wk_lo[:, g * 512:(g + 1) * 512])).then_inc(kn_ps, 1)
                with pe.Fori(0, FT) as t:
                    key_tile(t, P)
                key_tile(FT, LAST)

                def q_mm(h, u):
                    pe.wait_ge(q_lo_s, b * H + h + 1)
                    for k in range(KT):
                        m = splits3(pe, bank[4 + u][:, 0:SQ],
                                    (wq_hi[:, k, ds(h * P, P)], wq_lo[:, k, ds(h * P, P)]),
                                    (xnt_hi[:, k, :], xnt_lo[:, k, :]), start=(k == 0), stop=(k == KT - 1))
                    m.then_inc(q_ps, 1)

                def qp_mm(h, u):
                    pe.wait_ge(q_lo_s, b * H + h + 3)
                    pe.wait_ge(qp_lo_s, b * H + h + 1)
                    splits3(pe, bank[6][:, 0:SQ], (wkt_hi[:, ds(h, 1), :], wkt_lo[:, ds(h, 1), :]),
                            (q_hi[:, u, :], q_lo[:, u, :])).then_inc(qp_ps, 1)
                    for t in range(QT):
                        m = pe.matmul(bank[7][:, ds(h + t * H, 1)], q_sq[:, u, t * P:(t + 1) * P], ones[:, :],
                                      start=True, stop=True)
                    m.then_inc(rq_ps, 1)

                q_mm(0, 0)
                with pe.Fori(0, H // 2 - 1) as j:
                    q_mm(2 * j + 1, 1)
                    qp_mm(2 * j, 0)
                    q_mm(2 * j + 2, 0)
                    qp_mm(2 * j + 1, 1)
                q_mm(H - 1, 1)
                qp_mm(H - 2, 0)
                qp_mm(H - 1, 1)

                pe.wait_ge(rk_ready, b + 1)
                pe.wait_ge(kn_sq, (b + 1) * NKT * 4 + 4)
                pe.sem_inc(paced_pe, 1)
                for t in range(NKT):
                    r = KROWS[t]
                    o = (t % 8) * P
                    m = pe.transpose(rkt_ps[t // 8][0:3 * H, o:o + r],
                                     rk3[0:r, t, :, :].rearrange("p a h -> p (a h)"), ident16[0:r, 0:r])
                m.then_inc(rkt_tp, 1)
                pe.wait_ge(rkt_ready, b + 1)
                pe.wait_ge(rq_ready, b + 1)
                pe.wait_ge(qp_lo_s, (b + 1) * H + 1)

                def bcast(h, j, shared=True):
                    if shared:
                        pe.wait_ge(s_acc, b * H + h - 1)
                    pe.wait_ge(s_rbc, (b * H + h) * 4 + j + 1)
                    pe.sem_inc(paced_pe, 1)
                    c0, cn = CH[j]
                    pe.matmul(R_BANK[:, 0:cn], sel[:, ds(h, 1), :], rkt[:, c0:c0 + cn], start=True, stop=True
                              ).then_inc(s_rb, 1)

                def score(h, k):
                    n8 = (b * H + h) * 8
                    t, (c0, cn) = k // 4, CH[k % 4]
                    last = {0: -2, 1: -1, 2: -3}.get(k, k - 3)
                    pe.wait_ge(s_scd, n8 + last + 17)
                    q0 = (qp_hi[:, ds(h, 1), t * P:(t + 1) * P], qp_lo[:, ds(h, 1), t * P:(t + 1) * P])
                    splits3(pe, S_BANK[SCORE_BANK[k]][:, 0:cn], q0,
                            (ctxt_hi[:, c0:c0 + cn], ctxt_lo[:, c0:c0 + cn])).then_inc(s_sc, 1)

                def tr(h, u, g):
                    n = b * H + h
                    if g == 0:
                        pe.wait_ge(s_exp, n * 2 + 4)
                    last = {0: -1, 1: -3, 2: -2}.get(g, g - 3)
                    pe.wait_ge(s_lo, n * 7 + last + 8)
                    for s in range(2):
                        t = 2 * g + s
                        if t < NKT:
                            r = KROWS[t]
                            for q in range(QT):
                                m = pe.transpose(T_BANK[g % 3][0:r, s * SQ + q * P:s * SQ + (q + 1) * P],
                                                 SP[u][q][:, t * P:t * P + r], ident[:, :])
                    m.then_inc(s_tr, 1)

                def pv(h, g):
                    n = b * H + h
                    pe.wait_ge(s_lo, n * 7 + g + 8)
                    if g == 0:
                        pe.wait_ge(s_ol, n + 1)
                    for s in range(2):
                        t = 2 * g + s
                        if t < NKT:
                            r = KROWS[t]
                            m = splits3(pe, O_BANK[:, 0:SQ], (ctx_hi[0:r, t, :], ctx_lo[0:r, t, :]),
                                        (pt_hi[0:r, g, s, :], pt_lo[0:r, g, s, :]), start=(t == 0), stop=(t == NKT - 1))
                    m.then_inc(s_pv, 1)

                def vo(h):
                    n = b * H + h
                    pe.wait_ge(s_ol, n + 2)
                    pe.wait_ge(s_acc, n + 1)
                    pe.wait_ge(s_rbc, (b * H + (min(h + 3, H) if type(h) is int else h + 3)) * 4 + 1)
                    for q in range(QT):
                        m = splits3(pe, V_BANK[:, q * DM:(q + 1) * DM],
                                    (ot_hi[:, q * P:(q + 1) * P], ot_lo[:, q * P:(q + 1) * P]),
                                    (vo_hi[:, ds(h, 1), :], vo_lo[:, ds(h, 1), :]))
                    m.then_inc(s_vo, 1)

                def head(h, u, scores=True, bc=True, v=True):
                    for step in ("C0 S2 V C1 S3 D0 R0 C2 S4 D1 R1 C3 S5 D2 R2 C4 S6 D3 R3 C5 S7 D4 C6 "
                                 "N0 D5 N1 D6").split():
                        kind, i = step[0], int(step[1:] or 0)
                        if kind == "S" and scores:
                            score(h + 1, i)
                        elif kind == "N" and bc:
                            score(h + 2, i)
                        elif kind == "C":
                            tr(h, u, i)
                        elif kind == "D":
                            pv(h, i)
                        elif kind == "R" and bc:
                            bcast(h + 2, i)
                        elif kind == "V" and v:
                            vo(h - 1)

                for h in range(2):
                    for j in range(4):
                        bcast(h, j, shared=False)
                for k in range(8):
                    score(0, k)
                for k in range(2):
                    score(1, k)
                head(0, 0, v=False)
                with pe.Fori(0, H // 2 - 2) as j:
                    head(2 * j + 1, 1)
                    head(2 * j + 2, 0)
                head(H - 3, 1)
                head(H - 2, 0, bc=False)
                head(H - 1, 1, scores=False, bc=False)
                vo(H - 1)

            pe.wait_ge(s_acc, B * H + 1)
            pe.wait_ge(f_small, 16)
            for k in range(KT):
                m = pe.transpose(bank[2][:, k * E:(k + 1) * E], rw[:, k * P:(k + 1) * P], ident[0:E, 0:E])
            m.then_inc(f_rt, 1)
            for t in range(NT):
                pe.wait_ge(f_xn, t + 1)
                pe.wait_ge(f_tlo, t + 1)
                for k in range(KT):
                    m = pe.transpose(bank[t % 2][:, k * P:(k + 1) * P], xn2[:, t, k * P:(k + 1) * P], ident[:, :])
                m.then_inc(f_tp, 1)
            pe.wait_ge(f_rtc, 1)
            pe.wait_ge(f_tlo, NT + 2)
            for t in range(NT):
                for k in range(KT):
                    m = splits3(pe, bank[3][:, t * E:(t + 1) * E], (xt_hi[:, t, k, :], xt_lo[:, t, k, :]),
                                (rwt_hi[:, k, :], rwt_lo[:, k, :]), start=(k == 0), stop=(k == KT - 1))
            m.then_inc(f_lg, 1)

            def gate_or_up(half, e, t, u, w):
                i = e * NT + t
                if half == 0:
                    pe.wait_ge(f_silu, i + 1)
                else:
                    pe.wait_ge(f_h, i + 1)
                for k in range(KT):
                    cols = slice(k * F2 + half * FF, k * F2 + (half + 1) * FF)
                    m = splits3(pe, bank[2 * half + u][:, :], (xt_hi[:, ds(t, 1), k, :], xt_lo[:, ds(t, 1), k, :]),
                                (w_hi[:, w, cols], w_lo[:, w, cols]), start=(k == 0), stop=(k == KT - 1))
                m.then_inc(f_gu if half else f_g, 1)

            def mid_t(e, t, u):
                i = e * NT + t
                pe.wait_ge(f_h, i + 3)
                pe.wait_ge(f_hlo, i + 1)
                for f in range(FTT):
                    m = pe.transpose(bank[4 + u][:, f * P:(f + 1) * P], hmid[:, u, f * P:(f + 1) * P], ident[:, :])
                m.then_inc(f_ht, 1)

            def down_mm(e, t, u, w):
                i = e * NT + t
                pe.wait_ge(f_hlo, i + 3)
                pe.wait_ge(f_acc, i)
                for f in range(FTT):
                    cols = slice(KT * F2 + f * DM, KT * F2 + (f + 1) * DM)
                    m = splits3(pe, bank[6 + u][:, 0:DM], (ht_hi[:, u, f, :], ht_lo[:, u, f, :]),
                                (w_hi[:, w, cols], w_lo[:, w, cols]), start=(f == 0), stop=(f == FTT - 1))
                m.then_inc(f_y, 1)

            def expert(e, w):
                pe.wait_ge(f_w, e + 2)
                for half in range(2):
                    gate_or_up(half, e, 0, 0, w)

                def tile(t, u, more=True):
                    if more:
                        gate_or_up(0, e, t + 1, 1 - u, w)
                    mid_t(e, t, u)
                    if more:
                        gate_or_up(1, e, t + 1, 1 - u, w)
                    down_mm(e, t, u, w)
                with pe.Fori(0, NT // 2 - 1) as j:
                    tile(2 * j, 0)
                    tile(2 * j + 1, 1)
                tile(NT - 2, 0)
                tile(NT - 1, 1, more=False)
            with pe.Fori(0, E // 2 - 1) as j:
                expert(2 * j, 0)
                expert(2 * j + 1, 1)
            expert(E - 2, 0)
            expert(E - 1, 1)
            expert(E, 0)

        @block.scalar
        def _(act):
            for k in range(2):
                if k == 0:
                    act.wait_ge(ld["wk"], 32)
                act.activation(wk_hi[:, k * 1024:(k + 1) * 1024], stage_wk[k], ACT.Copy).then_inc(w_hi_s, 1)
            for h in range(H):
                act.wait_ge(wv_t, h + 1)
                act.activation(wvt[:, (h % 8) * P:(h % 8 + 1) * P], S_BANK[h % 2][:, 0:P], ACT.Copy).then_inc(wv_ts, 1)
            for n in range(4):
                k, s = n // 2, n % 2
                if n == 0:
                    act.wait_ge(ld["wq"], 64)
                act.activation(wq_hi[:, k, s * 1024:(s + 1) * 1024], (stage_wk + stage_wv)[n], ACT.Copy
                               ).then_inc(w_hi_s, 1)
            act.wait_ge(ld["small"], 64)
            act.activation(gates[:, 2:4], gates[:, 0:2], ACT.Tanh).then_inc(gate_s, 1)

            with act.Fori(0, B) as b:
                act.wait_ge(ctx_ld, b * 32 + 32)
                act.wait_ge(s_pv, b * (H * NG) + NG)
                act.activation(ctx_hi[:, 0:FT, :], ctx_f[:, 0:FT, :], ACT.Copy).then_inc(ctx_split, 1)
                act.activation(ctx_hi[0:LAST, FT, :], ctx_f[0:LAST, FT, :], ACT.Copy).then_inc(ctx_split, 1)
                for c in range(4):
                    c1 = min(KV, (c + 1) * 512)
                    act.wait_ge(tp_ps, b * 5 + c + 1)
                    act.activation(ctxt_hi[:, c * 512:c1], bank[c][:, 0:c1 - c * 512], ACT.Copy).then_inc(tp_hi, 1)
                act.wait_ge(tp_ps, b * 5 + 5)
                act.activation(xnt_hi[:, :, :].rearrange("p k q -> p (k q)"), bank[4][:, :], ACT.Copy).then_inc(tp_hi, 1)

                def squares(t, r):
                    for g in range(4):
                        i = (b * NKT + t) * 4 + g
                        act.wait_ge(kn_sum, i + 1)
                        act.wait_ge(kn_ps, i + 1)
                        act.activation(k_sq[0:r, g % 2, :], bank[g][0:r, :], ACT.Square).then_inc(kn_sq, 1)
                with act.Fori(0, FT) as t:
                    squares(t, P)
                squares(FT, LAST)

                def q_evac(h, u):
                    act.wait_ge(rq_ps, b * H + h + 1)
                    act.wait_ge(q_ps, b * H + h + 1)
                    act.activation(q_sq[:, u, :], bank[4 + u][:, 0:SQ], ACT.Square).then_inc(q_sq_s, 1)
                    act.activation(q_hi[:, u, :], bank[4 + u][:, 0:SQ], ACT.Copy).then_inc(q_hi_s, 1)

                def qp_evac(h):
                    act.wait_ge(qp_ps, b * H + h + 1)
                    act.activation(qp_hi[:, ds(h, 1), :], bank[6][:, 0:SQ], ACT.Copy).then_inc(qp_hi_s, 1)

                q_evac(0, 0)
                with act.Fori(0, H // 2 - 1) as j:
                    q_evac(2 * j + 1, 1)
                    qp_evac(2 * j)
                    q_evac(2 * j + 2, 0)
                    qp_evac(2 * j + 1)
                q_evac(H - 1, 1)
                qp_evac(H - 2)
                qp_evac(H - 1)
                act.wait_ge(rkt_tp, b + 1)
                act.activation(rkt[:, 0:8 * P], rkt_ps[0][0:3 * H, :], ACT.Copy).then_inc(rkt_c, 1)
                act.activation(rkt[:, 8 * P:KV], rkt_ps[1][0:3 * H, 0:KV - 8 * P], ACT.Copy).then_inc(rkt_ready, 1)

                def bcast_copy(h, u, j):
                    n = b * H + h
                    c0, cn = CH[j]
                    act.wait_ge(s_scd, 8 * n + j + 5)
                    act.wait_ge(s_rb, 4 * n + j + 1)
                    act.activation(RK[u][:, c0:c0 + cn], R_BANK[:, 0:cn], ACT.Copy).then_inc(s_rbc, 1)

                def exps(h, u, q):
                    act.wait_ge(s_nb, (b * H + h) * 2 + q + 1)
                    act.activation(SP[u][q][:, :], SP[u][q][:, :], ACT.Exp, bias=nbias[:, q:q + 1],
                                   scale=rq[:, q, ds(h, 1)], accum_out=psum_p[:, u, q:q + 1]).then_inc(s_exp, 1)

                def p_hi(h, g):
                    n = b * H + h
                    act.wait_ge(s_pv, n * NG + g + 1)
                    act.wait_ge(s_tr, n * NG + g + 1)
                    for r, w in group_parts(g):
                        m = act.activation(pt_hi[0:r, g, w, :], T_BANK[g % 3][0:r, :].rearrange(
                            "p (s q) -> p s q", s=2)[:, w, :], ACT.Copy)
                    m.then_inc(s_hi, 1)

                def head(h, u, scores=True, bc=True):
                    for step in "H0 H1 R0 H2 X0 R1 H3 R2 H4 R3 H5 H6 X1 O".split():
                        kind, i = step[0], int(step[1:] or 0)
                        if kind == "H":
                            p_hi(h, i)
                        elif kind == "X" and scores:
                            exps(h + 1, 1 - u, i)
                        elif kind == "R" and bc:
                            bcast_copy(h + 2, u, i)
                        elif kind == "O":
                            n = b * H + h
                            act.wait_ge(s_pv, n * NG + 2 * NG)
                            act.wait_ge(s_vo, n + 1)
                            act.activation(ot_hi[:, :], O_BANK[:, 0:SQ], ACT.Copy, scale=1.0 / P_SCALE).then_inc(s_oh, 1)

                for h in range(2):
                    for j in range(4):
                        bcast_copy(h, h, j)
                for q in range(QT):
                    exps(0, 0, q)
                head(0, 0)
                with act.Fori(0, H // 2 - 2) as j:
                    head(2 * j + 1, 1)
                    head(2 * j + 2, 0)
                head(H - 3, 1)
                head(H - 2, 0, bc=False)
                head(H - 1, 1, scores=False, bc=False)
            with act.Fori(0, NT // 2) as j:
                for u in range(2):
                    t = 2 * j + u
                    act.wait_ge(f_tp, t + 1)
                    act.activation(xt_hi[:, ds(t, 1), :, :].rearrange("p a k q -> p (a k q)"), bank[u][:, 0:DM], ACT.Copy
                                   ).then_inc(f_thi, 1)
            act.wait_ge(f_lgc, 1)
            act.activation(smax[:, 1, :], smax[:, 0, :], ACT.Exp, scale=-1.0).then_inc(f_sel, 1)

            def w_split_hi(e, w):
                act.wait_ge(f_ld, 32 * e + (48 if type(e) is int and e == E else 32))
                if not (type(e) is int and e == 0):
                    act.wait_ge(f_y, (e - 1) * NT + 2)
                act.activation(w_hi[:, w, :], wstage[:, :], ACT.Copy).then_inc(f_whi, 1)

            def silu_of(e, t, u):
                i = e * NT + t
                act.wait_ge(f_g, i + 1)
                act.wait_ge(f_h, i + 1)
                act.activation(silu[:, u, :], bank[u][:, :], ACT.Silu, scale=sw[:, e, ds(t, 1)] if type(e) is int
                               else sw[:, ds(e, 1), ds(t, 1)].rearrange("p a b -> p (a b)")).then_inc(f_silu, 1)

            def h_hi(e, t, u):
                i = e * NT + t
                act.wait_ge(f_ht, i + 1)
                act.wait_ge(f_y, i + 1)
                act.activation(ht_hi[:, u, :, :].rearrange("p f q -> p (f q)"), bank[4 + u][:, :], ACT.Copy
                               ).then_inc(f_hhi, 1)

            def expert(e, w, nxt=True):
                silu_of(e, 0, 0)
                if nxt:
                    w_split_hi(e + 1, 1 - w)

                def tile(t, u, more=True):
                    if more:
                        silu_of(e, t + 1, 1 - u)
                    h_hi(e, t, u)
                with act.Fori(0, NT // 2 - 1) as j:
                    tile(2 * j, 0)
                    tile(2 * j + 1, 1)
                tile(NT - 2, 0)
                tile(NT - 1, 1, more=False)
            w_split_hi(0, 0)
            with act.Fori(0, E // 2 - 1) as j:
                expert(2 * j, 0)
                expert(2 * j + 1, 1)
            expert(E - 2, 0)
            expert(E - 1, 1)
            expert(E, 0, nxt=False)

        @block.vector
        def _(dve):
            for s, v in ((s_scd, 16), (s_lo, 7), (s_pv, 7), (s_ol, 1), (s_acc, 1), (s_rbc, 1), (s_vo, 1), (s_exp, 2),
                         (kn_sq, 4), (kn_sum, 2), (q_lo_s, 2), (qp_lo_s, 1), (rq_ps, 2), (ctx_free, 1)):
                dve.sem_inc(s, v)
            setup = Chain(dve, setup_chain)
            setup(dve.memset(ssk[:, :, :], 1.0))
            dve.wait_ge(ld["small"], 64)
            setup(dve.tensor_tensor(gcol[:, 2:3], gcol[:, 0:1], gcol[:, 1:2], ALU.mult))
            for k in range(2):
                cols = slice(k * 1024, (k + 1) * 1024)
                dve.wait_ge(w_hi_s, k + 1)
                dve.tensor_tensor(wk_lo[:, cols], stage_wk[k], wk_hi[:, cols], ALU.subtract).then_inc(w_split, 1)
            for h in range(H):
                tmp = q_sq[:, h % 2, 0:P]
                dve.wait_ge(wk_t, h + 1)
                setup(dve.tensor_scalar(tmp, T_BANK[h % 2][:, 0:P], gcol[:, 2:3], None, ALU.mult))
                setup(dve.tensor_copy(wkt_hi[:, h, :], tmp))
                dve.tensor_tensor(wkt_lo[:, h, :], tmp, wkt_hi[:, h, :], ALU.subtract).then_inc(wk_ts, 1)
            for h in range(H):
                dve.wait_ge(vo_ps, h + 1)
                setup(dve.tensor_copy(vo_hi[:, h, :], O_BANK[:, 0:DM]))
                dve.tensor_tensor(vo_lo[:, h, :], O_BANK[:, 0:DM], vo_hi[:, h, :], ALU.subtract).then_inc(vo_s, 1)
            for n in range(4):
                k, cols = n // 2, slice(n % 2 * 1024, (n % 2 + 1) * 1024)
                dve.wait_ge(w_hi_s, n + 3)
                dve.tensor_tensor(wq_lo[:, k, cols], (stage_wk + stage_wv)[n], wq_hi[:, k, cols], ALU.subtract
                                  ).then_inc(w_split, 1)
            dve.wait_ge(gate_s, 1)
            setup(dve.tensor_scalar(g1[:, :], gates[:, 2:3], P_SCALE, None, ALU.mult))
            dve.wait_ge(ld["x"], 16)

            with dve.Fori(0, B) as b:
                chain = Chain(dve, prep_chain, b * PREP_STEPS)
                for t in range(QT):
                    chain(dve.bn_stats(stats[:, t, :], x_all[:, ds(b * QT + t, 1), :]))
                    dve.sem_inc(paced_dve, 1)
                    chain(dve.bn_aggr(mv[:, t, :], stats[:, t, :]))
                v, y, w = ssc[:, 0, 0:QT], ssc[:, 1, 0:QT], ssc[:, 2, 0:QT]
                chain(dve.tensor_scalar(v, mv[:, :, 1], EPS, None, ALU.add))
                rsqrt(dve, chain, v, y, w)
                for t in range(QT):
                    m = dve.tensor_scalar(xn[:, t, :], x_all[:, ds(b * QT + t, 1), :], mv[:, t, 0:1],
                                          ssc[:, 1, t:t + 1], ALU.subtract, ALU.mult)
                    chain(m)
                dve.sem_inc(xn_ready, 1)
                dve.wait_ge(ctx_split, b * 2 + 2)
                dve.tensor_tensor(ctx_lo[:, 0:FT, :], ctx_f[:, 0:FT, :], ctx_hi[:, 0:FT, :], ALU.subtract
                                  ).then_inc(ctx_lo_s, 1)
                dve.tensor_tensor(ctx_lo[0:LAST, FT, :], ctx_f[0:LAST, FT, :], ctx_hi[0:LAST, FT, :], ALU.subtract
                                  ).then_inc(ctx_lo_s, 1)
                for c in range(4):
                    c1 = min(KV, (c + 1) * 512)
                    dve.wait_ge(tp_hi, b * 5 + c + 1)
                    dve.tensor_tensor(ctxt_lo[:, c * 512:c1], bank[c][:, 0:c1 - c * 512], ctxt_hi[:, c * 512:c1],
                                      ALU.subtract).then_inc(tp_lo, 1)
                dve.wait_ge(ctx_lo_s, b * 2 + 2)
                dve.wait_ge(tp_lo, b * 5 + 4)
                dve.sem_inc(ctx_free, 1)
                dve.wait_ge(tp_hi, b * 5 + 5)
                dve.tensor_tensor(xnt_lo[:, :, :].rearrange("p k q -> p (k q)"), bank[4][:, :],
                                  xnt_hi[:, :, :].rearrange("p k q -> p (k q)"), ALU.subtract).then_inc(tp_lo, 1)

                def key_sums(t, r):
                    for g in range(4):
                        i = (b * NKT + t) * 4 + g
                        dve.wait_ge(kn_sq, i + 5)
                        dve.tensor_reduce(ssk[0:r, ds(t, 1), g * 4:(g + 1) * 4], k_sq[0:r, g % 2, :].rearrange(
                            "p (h d) -> p h d", h=4), X, ALU.add).then_inc(kn_sum, 1)
                with dve.Fori(0, FT) as t:
                    key_sums(t, P)
                key_sums(FT, LAST)
                dve.wait_ge(kn_sum, (b + 1) * NKT * 4 + 2)
                v, y, w = ssc[:, 0, :], ssc[:, 1, :], ssc[:, 2, :]
                grid = lambda a: a.rearrange("p (t h) -> p t h", t=NKT)
                chain(dve.tensor_scalar(v, ssk[:, :, :].rearrange("p t h -> p (t h)"), 1.0 / D, EPS, ALU.mult, ALU.add))
                rsqrt(dve, chain, v, y, w)
                chain(dve.tensor_copy(rk3[:, :, 0, :], grid(y)))
                chain(dve.tensor_tensor(grid(w), grid(y), rk3[:, :, 0, :], ALU.subtract))
                chain(dve.tensor_copy(rk3[:, :, 1, :], grid(w)))
                dve.tensor_tensor(rk3[:, :, 2, :], grid(w), rk3[:, :, 1, :], ALU.subtract).then_inc(rk_ready, 1)

                def q_rest(h, u):
                    dve.wait_ge(q_hi_s, b * H + h + 1)
                    dve.tensor_tensor(q_lo[:, u, :], bank[4 + u][:, 0:SQ], q_hi[:, u, :], ALU.subtract).then_inc(q_lo_s, 1)

                def qp_rest(h):
                    dve.wait_ge(qp_hi_s, b * H + h + 1)
                    dve.tensor_tensor(qp_lo[:, ds(h, 1), :], bank[6][:, 0:SQ], qp_hi[:, ds(h, 1), :], ALU.subtract
                                      ).then_inc(qp_lo_s, 1)
                q_rest(0, 0)
                with dve.Fori(0, H // 2 - 1) as j:
                    q_rest(2 * j + 1, 1)
                    qp_rest(2 * j)
                    q_rest(2 * j + 2, 0)
                    qp_rest(2 * j + 1)
                q_rest(H - 1, 1)
                qp_rest(H - 2)
                qp_rest(H - 1)
                dve.wait_ge(rq_ps, (b + 1) * H + 2)
                dve.wait_ge(rk_ready, b + 1)
                v, y, w = (ssc[:, i, 0:QT * H] for i in range(3))
                chain(dve.tensor_scalar(v, bank[7][:, 0:QT * H], 1.0 / D, EPS, ALU.mult, ALU.add))
                rsqrt(dve, chain, v, y, w)
                chain(dve.tensor_scalar(rq[:, :, :].rearrange("p t h -> p (t h)"), y, float(D) ** -0.5, None, ALU.mult))
                dve.tensor_scalar(nrq[:, :, :].rearrange("p t h -> p (t h)"), y, -float(D) ** -0.5, None, ALU.mult
                                  ).then_inc(rq_ready, 1)
                assert chain.n == PREP_STEPS, chain.n

                def scaled(h, u, k):
                    n, q, (c0, cn) = b * H + h, k // 4, CH[k % 4]
                    if k < 4:
                        dve.wait_ge(s_rbc, 4 * n + k + 2)
                    dve.wait_ge(s_sc, 8 * n + k + 1)
                    dve.sem_inc(paced_dve, 1)
                    dve.tensor_tensor_reduce(SP[u][q][:, c0:c0 + cn], S_BANK[SCORE_BANK[k]][:, 0:cn],
                                             RK[u][:, c0:c0 + cn], 1.0, NEG, ALU.mult, ALU.max,
                                             mx4[:, q, k % 4:k % 4 + 1]).then_inc(s_scd, 1)

                def bias(h, q):
                    n = b * H + h
                    dve.wait_ge(s_scd, 8 * n + 4 * q + 4 + 16)
                    dve.wait_ge(s_exp, 2 * n + q + 1)
                    dve.tensor_reduce(mx[:, q:q + 1], mx4[:, q, :], X, ALU.max).then_inc(max_chain, 1)
                    dve.wait_ge(max_chain, 2 * n + q + 1)
                    dve.tensor_scalar(nbias[:, q:q + 1], mx[:, q:q + 1], nrq[:, q, ds(h, 1)], LN_P_SCALE,
                                      ALU.mult, ALU.add).then_inc(s_nb, 1)

                def p_rest(h, g):
                    n = b * H + h
                    dve.wait_ge(s_hi, n * NG + g + 1)
                    for r, w in group_parts(g):
                        m = dve.tensor_tensor(pt_lo[0:r, g, w, :], T_BANK[g % 3][0:r, :].rearrange(
                            "p (s q) -> p s q", s=2)[:, w, :], pt_hi[0:r, g, w, :], ALU.subtract)
                    m.then_inc(s_lo, 1)

                def ot_rest(h, u):
                    n = b * H + h
                    dve.wait_ge(s_oh, n + 1)
                    dve.scalar_tensor_tensor(out=ot_lo[:, :], in0=O_BANK[:, 0:SQ], scalar=1.0 / P_SCALE,
                                             in1=ot_hi[:, :], op0=ALU.mult, op1=ALU.subtract).then_inc(s_ol, 1)
                    dve.wait_ge(s_acc, n + 1)
                    dve.reciprocal(rden[:, :], psum_p[:, u, :]).then_inc(den_chain, 1)
                    dve.wait_ge(den_chain, 2 * n + 1)
                    dve.tensor_scalar(rden[:, :], rden[:, :], g1[:, 0:1], None, ALU.mult).then_inc(den_chain, 1)

                def add_head(h):
                    n = b * H + h
                    dve.wait_ge(den_chain, 2 * n + 2)
                    dve.wait_ge(s_vo, n + 2)
                    for q in range(QT):
                        xt = x_all[:, ds(b * QT + q, 1), :]
                        m = dve.scalar_tensor_tensor(out=xt, in0=V_BANK[:, q * DM:(q + 1) * DM],
                                                     scalar=rden[:, q:q + 1], in1=xt, op0=ALU.mult, op1=ALU.add)
                    m.then_inc(s_acc, 1)

                def head(h, u, scores=True, more=True, add=True):
                    for step in "L0 T2 A L1 T3 M0 L2 T4 L3 T5 L4 T6 L5 T7 M1 L6 N0 N1 O".split():
                        kind, i = step[0], int(step[1:] or 0)
                        if kind == "T" and scores:
                            scaled(h + 1, 1 - u, i)
                        elif kind == "N" and more:
                            scaled(h + 2, u, i)
                        elif kind == "M" and scores:
                            bias(h + 1, i)
                        elif kind == "L":
                            p_rest(h, i)
                        elif kind == "O":
                            ot_rest(h, u)
                        elif kind == "A" and add:
                            add_head(h - 1)

                for k in range(8):
                    scaled(0, 0, k)
                    if k % 4 == 3:
                        bias(0, k // 4)
                for k in range(2):
                    scaled(1, 1, k)
                head(0, 0, add=False)
                with dve.Fori(0, H // 2 - 2) as j:
                    head(2 * j + 1, 1)
                    head(2 * j + 2, 0)
                head(H - 3, 1)
                head(H - 2, 0, more=False)
                head(H - 1, 1, scores=False, more=False)
                add_head(H - 1)
            for sm, v in ((f_tlo, 2), (f_silu, 2), (f_h, 2), (f_hlo, 2), (f_acc, 1), (f_w, 1), (f_y, 2)):
                dve.sem_inc(sm, v)
            chain = Chain(dve, f_chain)
            dve.wait_ge(s_acc, B * H + 1)
            for t in range(NT):
                chain(dve.bn_stats(st2[:, t, :], x_all[:, t, :]))
                chain(dve.bn_aggr(mv2[:, t, :], st2[:, t, :]))
            v, y, w = (ssc[:, i, 0:NT] for i in range(3))
            chain(dve.tensor_scalar(v, mv2[:, :, 1], EPS, None, ALU.add))
            rsqrt(dve, chain, v, y, w)
            for t in range(NT):
                dve.tensor_scalar(xn2[:, t, :], x_all[:, t, :], mv2[:, t, 0:1], ssc[:, 1, t:t + 1],
                                  ALU.subtract, ALU.mult).then_inc(f_xn, 1)
            dve.wait_ge(f_rt, 1)
            chain(dve.tensor_copy(rwt_hi[:, :, :].rearrange("p k e -> p (k e)"), bank[2][:, 0:KT * E]))
            dve.tensor_tensor(rwt_lo[:, :, :].rearrange("p k e -> p (k e)"), bank[2][:, 0:KT * E],
                              rwt_hi[:, :, :].rearrange("p k e -> p (k e)"), ALU.subtract).then_inc(f_rtc, 1)
            with dve.Fori(0, NT // 2) as j:
                for u in range(2):
                    t = 2 * j + u
                    flat = lambda a: a[:, ds(t, 1), :, :].rearrange("p a k q -> p (a k q)")
                    dve.wait_ge(f_thi, t + 1)
                    dve.tensor_tensor(flat(xt_lo), bank[u][:, 0:DM], flat(xt_hi), ALU.subtract).then_inc(f_tlo, 1)
            dve.wait_ge(f_lg, 1)
            chain(dve.tensor_copy(logit[:, :, :].rearrange("p t e -> p (t e)"), bank[3][:, 0:NT * E]))
            dve.tensor_reduce(smax[:, 0, :], logit[:, :, :], X, ALU.max).then_inc(f_lgc, 1)
            dve.wait_ge(f_sel, 1)
            chain(dve.tensor_scalar(smax[:, 1, :], smax[:, 1, :], 1.0, None, ALU.add))
            chain(dve.reciprocal(smax[:, 1, :], smax[:, 1, :]))
            for e in range(E):
                chain(dve.tensor_tensor(smax[:, 2, :], logit[:, :, e], smax[:, 0, :], ALU.is_equal))
                chain(dve.tensor_tensor(sw[:, e, :], smax[:, 2, :], smax[:, 1, :], ALU.mult))
                chain(dve.tensor_scalar(smax[:, 3, :], smax[:, 2, :], -1.0, 1.0, ALU.mult, ALU.add))
                chain(dve.tensor_tensor(smax[:, 1, :], smax[:, 1, :], smax[:, 3, :], ALU.mult))
            chain(dve.memset(sw[:, E, :], 1.0))

            def w_split_lo(e, w):
                dve.wait_ge(f_whi, e + 1)
                dve.tensor_tensor(w_lo[:, w, :], wstage[:, :], w_hi[:, w, :], ALU.subtract).then_inc(f_w, 1)

            def mid(e, t, u):
                i = e * NT + t
                dve.wait_ge(f_gu, i + 1)
                dve.wait_ge(f_silu, i + 3)
                dve.scalar_tensor_tensor(out=hmid[:, u, :], in0=bank[2 + u][:, :],
                                         scalar=sw[:, e, ds(t, 1)] if type(e) is int
                                         else sw[:, ds(e, 1), ds(t, 1)].rearrange("p a b -> p (a b)"),
                                         in1=silu[:, u, :], op0=ALU.mult, op1=ALU.mult).then_inc(f_h, 1)

            def h_lo(e, t, u):
                dve.wait_ge(f_hhi, e * NT + t + 1)
                dve.tensor_tensor(ht_lo[:, u, :, :].rearrange("p f q -> p (f q)"), bank[4 + u][:, :],
                                  ht_hi[:, u, :, :].rearrange("p f q -> p (f q)"), ALU.subtract).then_inc(f_hlo, 1)

            def add_out(e, t, u):
                i = e * NT + t
                xt = x_all[:, ds(t, 1), :]
                dve.wait_ge(f_y, i + 3)
                dve.scalar_tensor_tensor(out=xt, in0=bank[6 + u][:, 0:DM], scalar=gates[:, 3:4], in1=xt,
                                         op0=ALU.mult, op1=ALU.add).then_inc(f_acc, 1)

            def expert(e, w, nxt=True):
                mid(e, 0, 0)
                if nxt:
                    w_split_lo(e + 1, 1 - w)

                def tile(t, u, more=True):
                    h_lo(e, t, u)
                    if more:
                        mid(e, t + 1, 1 - u)
                    add_out(e, t, u)
                with dve.Fori(0, NT // 2 - 1) as j:
                    tile(2 * j, 0)
                    tile(2 * j + 1, 1)
                tile(NT - 2, 0)
                tile(NT - 1, 1, more=False)
            w_split_lo(0, 0)
            with dve.Fori(0, E // 2 - 1) as j:
                expert(2 * j, 0)
                expert(2 * j + 1, 1)
            expert(E - 2, 0)
            expert(E - 1, 1)
            expert(E, 0, nxt=False)


_INS = ['x', 'ctx_1024', 'g_xattn', 'g_ffn', 'L0_xattn_Wq', 'L0_xattn_Wk', 'L0_xattn_Wv', 'L0_xattn_Wo',
        'L0_xattn_gq', 'L0_xattn_gk', 'L0_ffn_router_w', 'L0_ffn_gate_up_proj', 'L0_ffn_down_proj',
        'L0_ffn_shared_gate_w', 'L0_ffn_shared_up_w', 'L0_ffn_shared_down_w']
_OUTS = [((8, 256, 256), 'float32')]


def kernel(**inputs):
    import numpy as _np
    import concourse.bacc as _bacc
    from concourse import mybir as _mybir
    from concourse.bass_utils import run_bass_kernel_spmd as _run

    nc = _bacc.Bacc("TRN2", target_bir_lowering=False, num_devices=1)
    arrays, args = {}, []
    for name in _INS:
        a = _np.ascontiguousarray(inputs[name])
        arrays[f"in_{name}_dram"] = a
        args.append(nc.dram_tensor(f"in_{name}_dram", a.shape, _mybir.dt.from_np(a.dtype), kind="ExternalInput").ap())
    for i, (shape, dtype) in enumerate(_OUTS):
        dt = _mybir.dt.from_np(_np.dtype(dtype))
        args.append(nc.dram_tensor(f"out_{i}_dram", shape, dt, kind="ExternalOutput").ap())
    flamingo_layer(nc, *args)
    r = _run(nc, [arrays], core_ids=[0])
    return r.results[0]["out_0_dram"]
```

```python
from contextlib import ExitStack

import concourse.bass as bass
from concourse import mybir

F32 = mybir.dt.float32
F16 = mybir.dt.float16
BF16 = mybir.dt.bfloat16
I32 = mybir.dt.int32
ALU = mybir.AluOpType
ACT = mybir.ActivationFunctionType
X = mybir.AxisListType.X
ds = bass.ds

P = 128
EPS = 1e-5
LN_P_SCALE = 6.931471805599453
P_SCALE = 1024.0
RSQRT_MAGIC = 1597463007
NEG = -3.0e38


class Chain:

    def __init__(self, eng, sem, base=0, carrier=None):
        self.eng, self.sem, self.base, self.n, self.carrier = eng, sem, base, 0, carrier

    def __call__(self, ins):
        self.n += 1
        ins.then_inc(self.sem, 1)
        self.eng.wait_ge(self.sem, self.base + self.n)
        if self.carrier is not None:
            self.eng.sem_inc(self.carrier, 1)


def flamingo_layer(nc, x, ctx, g_xattn, g_ffn, Wq, Wk, Wv, Wo, gq, gk,
                   router_w, gate_up, down, sh_gate, sh_up, sh_down, out):
    B, SQ, DM = x.shape
    KV, DC = ctx.shape[1], ctx.shape[2]
    D = gq.shape[0]
    H = Wq.shape[1] // D
    QT, KT = SQ // P, DM // P
    NT = B * QT
    FT = KV // P
    LAST = KV - FT * P
    NKT = FT + 1
    NG = (NKT + 1) // 2
    INNER = H * D
    E, _, F2 = gate_up.shape
    FF = F2 // 2
    FTT = FF // P
    WC = KT * F2 + FTT * DM
    NS = NT + E - 1
    HALF = NT // 2
    assert DC == P and D == P and SQ == 256 and H % 2 == 0
    CH = [(0, 401), (401, 400), (801, 400), (1201, 400)]
    assert CH[-1][0] + CH[-1][1] == KV
    SCORE_BANK = [0, 1, 2, 0, 1, 2, 0, 1]
    KROWS = [P] * FT + [LAST]

    top = ExitStack()
    with top:
        def sem(name):
            return top.enter_context(nc.semaphore(name))

        def sb(name, shape, dt, stack=top):
            return stack.enter_context(nc.sbuf_tensor(name, shape, dt))

        x_all = sb("x_all", [P, NT, DM], F32)
        ident = sb("ident", [P, P], F32)
        zeros = sb("zeros", [P, DM], F32)
        before = sb("before", [P, P], BF16)
        ones_b = sb("ones_b", [P, P], BF16)
        iota_s = sb("iota_s", [P, NS], F32)
        ident16 = sb("ident16", [P, P], BF16)
        ones = sb("ones", [P, 1], F32)
        gates = sb("gates", [P, 4], F32)
        g1 = sb("g1", [P, 1], F32)
        gcol = sb("gcol", [P, 3], F32)
        ssc = sb("ssc", [P, 3, NKT * H], F32)
        stats = sb("stats", [P, NT, 6], F32)
        mv = sb("mv", [P, NT, 2], F32)
        rs3 = sb("rs3", [P, 3, QT * H], F32)
        att = ExitStack()
        wq_hi = sb("wq_hi", [P, KT, INNER], F16, att)
        wq_lo = sb("wq_lo", [P, KT, INNER], F16, att)
        wk_hi = sb("wk_hi", [P, INNER], F16, att)
        wk_lo = sb("wk_lo", [P, INNER], F16, att)
        wkt_hi = sb("wkt_hi", [P, H, P], F16, att)
        wkt_lo = sb("wkt_lo", [P, H, P], F16, att)
        vo_hi = sb("vo_hi", [P, H, DM], F16, att)
        vo_lo = sb("vo_lo", [P, H, DM], F16, att)
        ctx_f = sb("ctx_f", [P, NKT, P], F32, att)
        ctx_hi = sb("ctx_hi", [P, NKT, P], F16, att)
        ctx_lo = sb("ctx_lo", [P, NKT, P], F16, att)
        ctxt_hi = sb("ctxt_hi", [P, KV], F16, att)
        ctxt_lo = sb("ctxt_lo", [P, KV], F16, att)
        xn = sb("xn", [P, 4, DM], F32, att)
        xnt_hi = sb("xnt_hi", [P, B, KT * SQ], F16, att)
        xnt_lo = sb("xnt_lo", [P, B, KT * SQ], F16, att)
        SP = [[sb(f"sp{u}{t}", [P, KV], F32, att) for t in range(QT)] for u in range(2)]
        RK = [sb(f"rk_bcast{u}", [P, KV], F32, att) for u in range(2)]
        pt_hi = sb("pt_hi", [P, NG, 2, SQ], F16, att)
        pt_lo = sb("pt_lo", [P, NG, 2, SQ], F16, att)
        qp_hi = sb("qp_hi", [P, H, SQ], F16, att)
        qp_lo = sb("qp_lo", [P, H, SQ], F16, att)
        q_hi = sb("q_hi", [P, 4, SQ], F16, att)
        q_lo = sb("q_lo", [P, 4, SQ], F16, att)
        q_sq = sb("q_sq", [P, 4, SQ], F32, att)
        k_sq = sb("k_sq", [P, 2, 512], F32, att)
        ssk = sb("ssk", [P, NKT, H], F32, att)
        rk3 = sb("rk3", [P, NKT, 3, H], BF16, att)
        rkt = sb("rkt", [3 * H, KV], BF16, att)
        sel = sb("sel", [3 * H, H, P], BF16, att)
        rq = sb("rq", [P, QT, H], F32, att)
        nrq = sb("nrq", [P, QT, H], F32, att)
        mx4 = sb("mx4", [P, QT, 4], F32, att)
        mx = sb("mx", [P, QT], F32, att)
        nbias = sb("nbias", [P, QT], F32, att)
        psum_p = sb("psum_p", [P, 2, QT], F32, att)
        rden = sb("rden", [P, QT], F32, att)
        ot_hi = sb("ot_hi", [P, SQ], F16, att)
        ot_lo = sb("ot_lo", [P, SQ], F16, att)
        att.close()
        ffn = ExitStack()
        xn2 = sb("xn2", [P, NT, DM], F32, ffn)
        xt_hi = sb("xt_hi", [P, NT, KT, P], F16, ffn)
        xt_lo = sb("xt_lo", [P, NT, KT, P], F16, ffn)
        wstage = sb("wstage", [P, 2, WC], F32, ffn)
        w_hi = sb("w_hi", [P, E + 1, WC], F16, ffn)
        w_lo = sb("w_lo", [P, E + 1, WC], F16, ffn)
        silu = sb("silu", [P, 2, FF], F32, ffn)
        hmid = sb("hmid", [P, 2, FF], F32, ffn)
        ht_hi = sb("ht_hi", [P, 2, FTT, P], F16, ffn)
        ht_lo = sb("ht_lo", [P, 2, FTT, P], F16, ffn)
        xs_in = sb("xs_in", [P, 2, DM], F32, ffn)
        xs_hi = sb("xs_hi", [P, 2, KT, P], F16, ffn)
        xs_lo = sb("xs_lo", [P, 2, KT, P], F16, ffn)
        ys_out = sb("ys_out", [P, 2, DM], F32, ffn)
        ys_in = wstage[:, :, :].rearrange("p a c -> p (a c)")[:, 0:NT * DM].rearrange("p (t m) -> p t m", t=NT)
        rw = ys_out[0:E, 0, :]
        rwt_hi = sb("rwt_hi", [P, KT, E], F16, ffn)
        rwt_lo = sb("rwt_lo", [P, KT, E], F16, ffn)
        logit = sb("logit", [P, NT, E], F32, ffn)
        smax = sb("smax", [P, 4, NT], F32, ffn)
        onehot = sb("onehot", [P, NT, E], F32, ffn)
        onehot_b = sb("onehot_b", [P, NT, E], BF16, ffn)
        count = sb("count", [P, NT, E], F32, ffn)
        slot = sb("slot", [P, NT, E], F32, ffn)
        run = sb("run", [P, NT, E], F32, ffn)
        ecol = sb("ecol", [P, 4, E], F32, ffn)
        etile = sb("etile", [P, E], I32, ffn)
        pos = sb("pos", [P, NT], F32, ffn)
        pos_i = sb("pos_i", [P, NT], I32, ffn)
        owner = sb("owner", [P, NS], F32, ffn)
        owner_i = sb("owner_i", [P, NS], I32, ffn)
        ffn.close()

        xs_dram = nc.dram_tensor("sorted_tokens", [NS * P, DM], F32).ap()
        ys_dram = nc.dram_tensor("sorted_outputs", [NS * P, DM], F32).ap()

        bank = [top.enter_context(nc.psum_tensor(f"bank{i}", [P, 512], F32)) for i in range(8)]
        S_BANK, T_BANK, O_BANK, V_BANK, R_BANK = bank[0:3], bank[3:6], bank[6], bank[7], bank[7]
        rkt_ps = bank[7][:, :].bitcast(BF16)

        ld = {n: sem("ld_" + n) for n in ("x", "small", "wk", "wv", "wo", "wq")}
        c_done = sem("consts_done")
        w_split, wk_t, wk_ts, wv_t, wv_ts, vo_ps, vo_s = map(sem, (
            "wsplit", "wkt_ps", "wkt_split", "wvt_ps", "wvt_copied", "vo_ps", "vo_split"))
        setup_chain = sem("setup_chain")
        ctx_ld, ctx_free, xn_ready = map(sem, ("ctx_ld", "ctx_free", "xn_ready"))
        tp_ps, tp_hi, tp_lo = map(sem, ("tp_ps", "tp_hi", "tp_lo"))
        kn_ps, kn_sq, kn_sum = map(sem, ("kn_ps", "kn_sq", "kn_sum"))
        q_ps, q_hi_s, q_lo_s, qp_ps, qp_hi_s, qp_lo_s, rq_ps = map(sem, (
            "q_ps", "q_hi_s", "q_lo_s", "qp_ps", "qp_hi_s", "qp_lo_s", "rq_ps"))
        rk_ready, rkt_tp, rkt_ready, rq_ready = map(sem, ("rk_ready", "rkt_tp", "rkt_ready", "rq_ready"))
        prep_chain, max_chain, den_chain, ctx_split, mem0 = map(sem, (
            "prep_chain", "max_chain", "den_chain", "ctx_hi_done", "ssk_set"))
        s_rb, s_rbc, s_sc, s_scd, s_nb, s_exp, s_tr, s_hi, s_lo, s_pv, s_oh, s_ol, s_vo, s_acc = map(sem, (
            "rb_ps", "rb_copied", "score_ps", "score_used", "bias_ready", "exp_done", "pt_ps", "pt_hi_done",
            "pt_lo_done", "pv_done", "ot_hi_done", "ot_lo_done", "vo_done", "head_added"))
        f_small, f_w, f_whi, f_ld0, f_ld1, f_xn, f_tp, f_thi, f_tlo, f_rt, f_rtc, f_lg, f_lgc, f_sel = map(sem, (
            "f_small", "f_w", "f_whi", "f_ld0", "f_ld1", "f_xn", "f_tp", "f_thi", "f_tlo", "f_rt", "f_rtc", "f_lg",
            "f_lgc", "f_sel"))
        f_g, f_gu, f_silu, f_h, f_ht, f_hhi, f_hlo, f_y, f_acc, f_chain = map(sem, (
            "f_g", "f_gu", "f_silu", "f_h", "f_ht", "f_hhi", "f_hlo", "f_y", "f_acc", "f_chain"))
        f_xld, f_yst = [sem("f_xs_loaded0"), sem("f_xs_loaded1")], [sem("f_ys_stored0"), sem("f_ys_stored1")]
        f_gat = [sem(f"f_gathered{n}") for n in range(4)]
        f_onehot, f_rank, f_pos, f_owner, f_xr, f_zero, f_scat, f_xsp, f_xsh, f_xsl, f_done = map(
            sem, ("f_onehot", "f_rank", "f_pos", "f_owner", "f_xr", "f_zero", "f_scattered", "f_xs_ps",
                  "f_xs_hi", "f_xs_lo", "f_done"))
        st = sem("stored")
        paced_dve, paced_pe, paced_pool = sem("paced_dve"), sem("paced_pe"), sem("paced_pool")
        w_hi_s, gate_s, q_sq_s, rkt_c, ctx_lo_s = map(sem, ("w_hi_done", "gate_tanh", "q_squared", "rkt_first", "ctx_lo_done"))
        rk_guess, rq_guess, pool_chain, xt_ps, xt_hi_s, xt_lo_s, wk_th = map(sem, (
            "rk_guess", "rq_guess", "pool_chain", "xt_ps", "xt_hi_s", "xt_lo_s", "wkt_hi_done"))
        PREP_STEPS = 2 + 2
        POOL_STEPS = 12 + 3 + 12 + 1
        NEWTON = 3
        gcol_s, vo_h = sem("gcol_ready"), sem("vo_hi_done")

        block = top.enter_context(nc.Block())

        stage_wk = [SP[0][0][:, 0:1024], SP[0][1][:, 0:1024]]
        stage_wv = [SP[1][0][:, 0:1024], SP[1][1][:, 0:1024]]
        stage_wo = ctx_f[:, :, :].rearrange("p t c -> p (t c)")
        wvt = RK[1][:, :]

        def splits3(pe, ps, lhs, rhs, start=True, stop=True):
            pe.matmul(ps, lhs[0], rhs[0], start=start, stop=False)
            pe.matmul(ps, lhs[0], rhs[1], start=False, stop=False)
            return pe.matmul(ps, lhs[1], rhs[0], start=False, stop=stop)

        def group_parts(g):
            if 2 * g + 1 < FT:
                return [(P, slice(0, 2))]
            return [(KROWS[2 * g + i], slice(i, i + 1)) for i in range(2) if 2 * g + i < NKT]

        def rsqrt(dve, chain, v, y, t):
            chain(dve.tensor_scalar(t.bitcast(I32), v.bitcast(I32), 1, None, ALU.logical_shift_right))
            chain(dve.tensor_scalar(y.bitcast(I32), t.bitcast(I32), -1.0, float(RSQRT_MAGIC), ALU.mult, ALU.add))
            for _ in range(NEWTON):
                chain(dve.tensor_tensor(t, y, y, ALU.mult))
                chain(dve.scalar_tensor_tensor(out=t, in0=t, scalar=-0.5, in1=v, op0=ALU.mult, op1=ALU.mult))
                chain(dve.scalar_tensor_tensor(out=y, in0=t, scalar=1.5, in1=y, op0=ALU.add, op1=ALU.mult))

        def guess(dve, chain, v, y, t):
            chain(dve.tensor_scalar(t.bitcast(I32), v.bitcast(I32), 1, None, ALU.logical_shift_right))
            return dve.tensor_scalar(y.bitcast(I32), t.bitcast(I32), -1.0, float(RSQRT_MAGIC), ALU.mult, ALU.add)

        def newton(pool, chain, v, y, t):
            for _ in range(NEWTON):
                chain(pool.tensor_tensor(t, y, y, ALU.mult))
                chain(pool.tensor_tensor(t, t, v, ALU.mult))
                chain(pool.tensor_scalar(t, t, -0.5, 1.5, ALU.mult, ALU.add))
                chain(pool.tensor_tensor(y, y, t, ALU.mult))

        CONSTS = 14
        @block.sync
        def _(sp):
            for k in range(2):
                sp.dma_start(stage_wk[k], Wk[:, k * 1024:(k + 1) * 1024]).then_inc(ld["wk"], 16)
            sp.dma_start(gcol[:, 0:1], gq.rearrange("(d a) -> d a", a=1)).then_inc(ld["small"], 16)
            sp.dma_start(gcol[:, 1:2], gk.rearrange("(d a) -> d a", a=1)).then_inc(ld["small"], 16)
            sp.dma_start(gates[:, 0:1], g_xattn.rearrange("(a b) -> a b", a=1).broadcast_to([P, 1])).then_inc(ld["small"], 16)
            sp.dma_start(gates[:, 1:2], g_ffn.rearrange("(a b) -> a b", a=1).broadcast_to([P, 1])).then_inc(ld["small"], 16)
            sp.dma_start(x_all[:, :, :], x.rearrange("b (t p) m -> p (b t) m", p=P)).then_inc(ld["x"], 16)
            for k in range(2):
                sp.dma_start(stage_wv[k], Wv[:, k * 1024:(k + 1) * 1024]).then_inc(ld["wv"], 16)
            for c in range(4):
                if c:
                    sp.wait_ge(vo_ps, 4 * c)
                sp.dma_start(stage_wo[:, 0:4 * DM].rearrange("p (h m) -> p h m", h=4),
                             Wo[c * 4 * D:(c + 1) * 4 * D, :].rearrange("(h d) m -> d h m", d=D)).then_inc(ld["wo"], 16)
            for k in range(KT):
                for s in range(2):
                    n = 2 * k + s
                    buf = (stage_wk + stage_wv)[n]
                    if n == 0:
                        sp.wait_ge(wk_t, H)
                        sp.wait_ge(w_split, 2)
                        sp.wait_ge(wv_t, H)
                    sp.dma_start(buf, Wq[k * P:(k + 1) * P, s * 1024:(s + 1) * 1024]).then_inc(ld["wq"], 16)
            sp.wait_ge(c_done, CONSTS)
            with sp.Fori(0, NS) as j:
                sp.dma_start(xs_dram[ds(j * P, P), :], zeros[:, :]).then_inc(f_zero, 16)
            with sp.Fori(0, B) as b:
                sp.wait_ge(vo_ps, H)
                sp.wait_ge(ctx_free, b + 1)
                sp.dma_start(ctx_f[:, 0:FT, :], ctx[ds(b, 1), 0:FT * P, :].rearrange("a (t p) c -> p (a t) c", p=P)
                             ).then_inc(ctx_ld, 16)
                sp.dma_start(ctx_f[0:LAST, FT, :], ctx[ds(b, 1), FT * P:KV, :].rearrange("a p c -> p (a c)")
                             ).then_inc(ctx_ld, 16)
            gu_v = [wstage[:, n, 0:KT * F2].rearrange("p (k f) -> p k f", k=KT) for n in range(2)]
            dn_v = [wstage[:, n, KT * F2:].rearrange("p (f m) -> p f m", f=FTT) for n in range(2)]
            sp.wait_ge(s_acc, B * H + 1)
            sp.dma_start(rw, router_w).then_inc(f_small, 16)
            sp.dma_start(gu_v[0][:, :, 0:FF], sh_gate.rearrange("(k p) f -> p k f", p=P)).then_inc(f_ld0, 16)
            sp.dma_start(gu_v[0][:, :, FF:F2], sh_up.rearrange("(k p) f -> p k f", p=P)).then_inc(f_ld0, 16)
            sp.dma_start(dn_v[0], sh_down.rearrange("(f p) m -> p f m", p=P)).then_inc(f_ld0, 16)
            with sp.Fori(0, E // 2) as j:
                for n, buf, loaded in ((0, 1, f_ld1), (1, 0, f_ld0)):
                    e = 2 * j + n
                    sp.wait_ge(f_w, e + 1)
                    sp.dma_start(gu_v[buf], gate_up[ds(e, 1)].rearrange("a (k p) f -> p (a k) f", p=P)).then_inc(loaded, 16)
                    sp.dma_start(dn_v[buf], down[ds(e, 1)].rearrange("a (f p) m -> p (a f) m", p=P)).then_inc(loaded, 16)
            sp.wait_ge(f_scat, 16 * NT)
            for j in range(2):
                sp.dma_start(xs_in[:, j, :], xs_dram[j * P:(j + 1) * P, :]).then_inc(f_xld[j], 16)

            def tile_io(j, u, more=True):
                if more:
                    sp.wait_ge(f_xsp, j + 1)
                    sp.dma_start(xs_in[:, u, :], xs_dram[ds((j + 2) * P, P), :]).then_inc(f_xld[u], 16)
                sp.wait_ge(f_acc, HALF + j + 2)
                sp.dma_start(ys_dram[ds(j * P, P), :], ys_out[:, u, :]).then_inc(f_yst[u], 16)
            with sp.Fori(0, (NS - 2) // 2) as j:
                tile_io(2 * j, 0)
                tile_io(2 * j + 1, 1)
            tile_io(NS - 3, 0)
            tile_io(NS - 2, 1, more=False)
            tile_io(NS - 1, 0, more=False)
            with sp.Fori(0, NT) as t:
                sp.wait_ge(f_done, t + 1)
                sp.dma_start(out.rearrange("b (t p) m -> p (b t) m", p=P)[:, ds(t, 1), :], x_all[:, ds(t, 1), :]
                             ).then_inc(st, 16)
            sp.wait_ge(st, 16 * NT)

        @block.gpsimd
        def _(pool):
            pool.memset(ident[:, :], 0.0).then_inc(c_done, 1)
            pool.memset(ident16[:, :], 0.0).then_inc(c_done, 1)
            pool.memset(sel[:, :, :], 0.0).then_inc(c_done, 1)
            pool.memset(ones[:, :], 1.0).then_inc(c_done, 1)
            pool.memset(zeros[:, :], 0.0).then_inc(c_done, 1)
            pool.memset(ones_b[:, :], 1.0).then_inc(c_done, 1)
            pool.memset(before[:, :], 1.0).then_inc(c_done, 1)
            pool.iota(iota_s[:, :], pattern=[[1, NS]], base=0, channel_multiplier=0,
                      allow_small_or_imprecise_dtypes=True).then_inc(c_done, 1)
            n = 8
            for buf in (ident, ident16):
                pool.wait_ge(c_done, n)
                pool.affine_select(out=buf[:, :], in_=buf[:, :], compare_op=ALU.not_equal, fill=1.0, base=0,
                                   pattern=[[-1, P]], channel_multiplier=1).then_inc(c_done, 1)
                n += 1
            pool.wait_ge(c_done, n)
            pool.affine_select(out=before[:, :], in_=before[:, :], compare_op=ALU.is_gt, fill=0.0, base=0,
                               pattern=[[1, P]], channel_multiplier=-1).then_inc(c_done, 1)
            n += 1
            for r in range(3):
                pool.wait_ge(c_done, n)
                pool.affine_select(out=sel[:, :, :], in_=sel[:, :, :], compare_op=ALU.not_equal, fill=1.0,
                                   base=-H * r, pattern=[[-1, H], [0, P]], channel_multiplier=1).then_inc(c_done, 1)
                n += 1

            grid = lambda a: a.rearrange("p (t h) -> p t h", t=NKT)
            with pool.Fori(0, B) as b:
                chain = Chain(pool, pool_chain, b * POOL_STEPS, carrier=paced_pool)
                v, y, w = ssc[:, 0, :], ssc[:, 1, :], ssc[:, 2, :]
                pool.wait_ge(rk_guess, b + 1)
                pool.sem_inc(paced_pool, 1)
                newton(pool, chain, v, y, w)
                chain(pool.tensor_copy(rk3[:, :, 0, :], grid(y)))
                chain(pool.tensor_tensor(grid(w), grid(y), rk3[:, :, 0, :], ALU.subtract))
                chain(pool.tensor_copy(rk3[:, :, 1, :], grid(w)))
                pool.tensor_tensor(rk3[:, :, 2, :], grid(w), rk3[:, :, 1, :], ALU.subtract).then_inc(rk_ready, 1)
                v, y, w = rs3[:, 0, :], rs3[:, 1, :], rs3[:, 2, :]
                pool.wait_ge(rq_guess, b + 1)
                pool.sem_inc(paced_pool, 1)
                newton(pool, chain, v, y, w)
                chain(pool.tensor_scalar(rq[:, :, :].rearrange("p t h -> p (t h)"), y, float(D) ** -0.5, None, ALU.mult))
                pool.tensor_scalar(nrq[:, :, :].rearrange("p t h -> p (t h)"), y, -float(D) ** -0.5, None, ALU.mult
                                   ).then_inc(rq_ready, 1)
                assert chain.n == POOL_STEPS, chain.n
            pool.wait_ge(f_zero, 16 * NS)
            pool.wait_ge(f_pos, 1)
            for t in range(NT):
                pool.wait_ge(f_xr, t + 1)
                pool.indirect_dma_start(xs_dram, bass.IndirectOffsetOnAxis(pos_i[:, t:t + 1], 0), xn2[:, t, :], None
                                        ).then_inc(f_scat, 16)
            pool.wait_ge(f_yst[0], 16 * ((NS + 1) // 2))
            pool.wait_ge(f_yst[1], 16 * (NS // 2))
            for t in range(NT):
                pool.indirect_dma_start(ys_in[:, t, :], None, ys_dram, bass.IndirectOffsetOnAxis(pos_i[:, t:t + 1], 0)
                                        ).then_inc(f_gat[t // 4], 16)

        @block.tensor
        def _(pe):
            pe.wait_ge(c_done, CONSTS)
            for h in range(H):
                if h == 0:
                    pe.wait_ge(ld["wk"], 32)
                if h >= 2:
                    pe.wait_ge(wk_ts, h - 1)
                pe.transpose(T_BANK[h % 2][:, 0:P], stage_wk[h // 8][:, (h % 8) * P:(h % 8 + 1) * P], ident[:, :]
                             ).then_inc(wk_t, 1)
            for b in range(B):
                if b >= 2:
                    pe.wait_ge(xt_lo_s, b - 1)
                for k in range(KT):
                    for t in range(QT):
                        pe.wait_ge(xn_ready, b * QT + QT) if k == t == 0 else None
                        m = pe.transpose(bank[5 + 2 * (b % 2)][:, k * SQ + t * P:k * SQ + (t + 1) * P],
                                         xn[:, (b * QT + t) % 4, k * P:(k + 1) * P], ident[:, :])
                m.then_inc(xt_ps, 1)
            for h in range(H):
                if h == 0:
                    pe.wait_ge(ld["wv"], 32)
                if h >= 2:
                    pe.wait_ge(wv_ts, h - 1)
                pe.transpose(S_BANK[h % 2][:, 0:P], stage_wv[h // 8][:, (h % 8) * P:(h % 8 + 1) * P], ident[:, :]
                             ).then_inc(wv_t, 1)
                if h % 4 == 0:
                    pe.wait_ge(ld["wo"], 4 * h + 16)
                pe.wait_ge(wv_ts, h + 1)
                if h >= 1:
                    pe.wait_ge(vo_s, h)
                pe.matmul(O_BANK[:, 0:DM], wvt[:, (h % 8) * P:(h % 8 + 1) * P],
                          stage_wo[:, (h % 4) * DM:(h % 4 + 1) * DM], start=True, stop=True).then_inc(vo_ps, 1)
            pe.wait_ge(wk_ts, H)
            pe.wait_ge(vo_s, H)
            pe.wait_ge(xt_lo_s, B)
            pe.wait_ge(w_split, 6)

            with pe.Fori(0, B) as b:
                pe.wait_ge(ctx_ld, b * 32 + 32)
                pe.wait_ge(s_acc, b * H + 1)
                for c in range(4):
                    for t in range(4 * c, min(4 * c + 4, NKT)):
                        r = KROWS[t]
                        m = pe.transpose(bank[c][:, (t - 4 * c) * P:(t - 4 * c) * P + r], ctx_f[0:r, t, :],
                                         ident[0:r, 0:r])
                    m.then_inc(tp_ps, 1)
                pe.wait_ge(tp_lo, b * 4 + 4)
                pe.sem_inc(paced_pe, 1)

                def key_tile(t, r):
                    for g in range(4):
                        pe.wait_ge(kn_sq, (b * NKT + t) * 4 + g + 1)
                        cols = ds(t * P, r)
                        splits3(pe, bank[g][0:r, :], (ctxt_hi[:, cols], ctxt_lo[:, cols]),
                                (wk_hi[:, g * 512:(g + 1) * 512], wk_lo[:, g * 512:(g + 1) * 512])).then_inc(kn_ps, 1)
                with pe.Fori(0, FT) as t:
                    key_tile(t, P)
                key_tile(FT, LAST)

                def q_mm(h, u):
                    pe.wait_ge(q_lo_s, b * H + h + 1)
                    for k in range(KT):
                        cols = slice(k * SQ, (k + 1) * SQ)
                        m = splits3(pe, bank[u][:, 0:SQ],
                                    (wq_hi[:, k, ds(h * P, P)], wq_lo[:, k, ds(h * P, P)]),
                                    (xnt_hi[:, ds(b, 1), cols], xnt_lo[:, ds(b, 1), cols]),
                                    start=(k == 0), stop=(k == KT - 1))
                    m.then_inc(q_ps, 1)

                def qp_mm(h, u):
                    pe.wait_ge(q_lo_s, b * H + h + 5)
                    pe.wait_ge(qp_lo_s, b * H + h + 1)
                    splits3(pe, bank[4 + u % 2][:, 0:SQ], (wkt_hi[:, ds(h, 1), :], wkt_lo[:, ds(h, 1), :]),
                            (q_hi[:, u, :], q_lo[:, u, :])).then_inc(qp_ps, 1)
                    for t in range(QT):
                        m = pe.matmul(bank[6][:, ds(h + t * H, 1)], q_sq[:, u, t * P:(t + 1) * P], ones[:, :],
                                      start=True, stop=True)
                    m.then_inc(rq_ps, 1)

                def rk_rows(first, n):
                    pe.wait_ge(rk_ready, b + 1)
                    if first:
                        pe.wait_ge(rkt_c, b + 1)
                    pe.sem_inc(paced_pe, 1)
                    for t in range(first, first + n):
                        r, o = KROWS[t], (t - first) * P
                        m = pe.transpose(rkt_ps[0:3 * H, o:o + r],
                                         rk3[0:r, t, :, :].rearrange("p a h -> p (a h)"), ident16[0:r, 0:r])
                    m.then_inc(rkt_tp, 1)

                pe.wait_ge(kn_sq, (b + 1) * NKT * 4 + 4)
                q_mm(0, 0)
                q_mm(1, 1)
                with pe.Fori(0, 2) as j:
                    for u in range(4):
                        q_mm(4 * j + u + 2, (u + 2) % 4)
                        qp_mm(4 * j + u, u)

                def bcast(h, j, shared=True):
                    if shared:
                        pe.wait_ge(s_acc, b * H + h - 1)
                    pe.wait_ge(s_rbc, (b * H + h) * 4 + j + 1)
                    pe.sem_inc(paced_pe, 1)
                    c0, cn = CH[j]
                    pe.matmul(R_BANK[:, 0:cn], sel[:, ds(h, 1), :], rkt[:, c0:c0 + cn], start=True, stop=True
                              ).then_inc(s_rb, 1)

                for h in range(8, H):
                    if h + 2 < H:
                        q_mm(h + 2, (h + 2) % 4)
                    qp_mm(h, h % 4)
                    if h == 8:
                        rk_rows(0, 8)
                    elif h == 10:
                        rk_rows(8, NKT - 8)
                    elif h >= 12:
                        if h == 12:
                            pe.wait_ge(rkt_ready, b + 1)
                        for j in range(2 * (h - 12), 2 * (h - 12) + 2):
                            bcast(j // 4, j % 4, shared=False)
                pe.wait_ge(qp_lo_s, (b + 1) * H + 2)

                def score(h, k):
                    n8 = (b * H + h) * 8
                    t, (c0, cn) = k // 4, CH[k % 4]
                    last = {0: -2, 1: -1, 2: -3}.get(k, k - 3)
                    pe.wait_ge(s_scd, n8 + last + 17)
                    q0 = (qp_hi[:, ds(h, 1), t * P:(t + 1) * P], qp_lo[:, ds(h, 1), t * P:(t + 1) * P])
                    splits3(pe, S_BANK[SCORE_BANK[k]][:, 0:cn], q0,
                            (ctxt_hi[:, c0:c0 + cn], ctxt_lo[:, c0:c0 + cn])).then_inc(s_sc, 1)

                def tr(h, u, g):
                    n = b * H + h
                    if g == 0:
                        pe.wait_ge(s_exp, n * 2 + 4)
                    last = {0: -1, 1: -3, 2: -2}.get(g, g - 3)
                    pe.wait_ge(s_lo, n * 7 + last + 8)
                    for s in range(2):
                        t = 2 * g + s
                        if t < NKT:
                            r = KROWS[t]
                            for q in range(QT):
                                m = pe.transpose(T_BANK[g % 3][0:r, s * SQ + q * P:s * SQ + (q + 1) * P],
                                                 SP[u][q][:, t * P:t * P + r], ident[:, :])
                    m.then_inc(s_tr, 1)

                def pv(h, g):
                    n = b * H + h
                    pe.wait_ge(s_lo, n * 7 + g + 8)
                    if g == 0:
                        pe.wait_ge(s_ol, n + 1)
                        pe.wait_ge(rq_ready, b + 1)
                    for s in range(2):
                        t = 2 * g + s
                        if t < NKT:
                            r = KROWS[t]
                            m = splits3(pe, O_BANK[:, 0:SQ], (ctx_hi[0:r, t, :], ctx_lo[0:r, t, :]),
                                        (pt_hi[0:r, g, s, :], pt_lo[0:r, g, s, :]), start=(t == 0), stop=(t == NKT - 1))
                    m.then_inc(s_pv, 1)

                def vo(h):
                    n = b * H + h
                    pe.wait_ge(s_ol, n + 2)
                    pe.wait_ge(s_acc, n + 1)
                    pe.wait_ge(s_rbc, (b * H + (min(h + 3, H) if type(h) is int else h + 3)) * 4 + 1)
                    for q in range(QT):
                        m = splits3(pe, V_BANK[:, q * DM:(q + 1) * DM],
                                    (ot_hi[:, q * P:(q + 1) * P], ot_lo[:, q * P:(q + 1) * P]),
                                    (vo_hi[:, ds(h, 1), :], vo_lo[:, ds(h, 1), :]))
                    m.then_inc(s_vo, 1)

                def head(h, u, scores=True, bc=True, v=True):
                    for step in ("C0 S2 V C1 S3 D0 R0 C2 S4 D1 R1 C3 S5 D2 R2 C4 S6 D3 R3 C5 S7 D4 C6 "
                                 "N0 D5 N1 D6").split():
                        kind, i = step[0], int(step[1:] or 0)
                        if kind == "S" and scores:
                            score(h + 1, i)
                        elif kind == "N" and bc:
                            score(h + 2, i)
                        elif kind == "C":
                            tr(h, u, i)
                        elif kind == "D":
                            pv(h, i)
                        elif kind == "R" and bc:
                            bcast(h + 2, i)
                        elif kind == "V" and v:
                            vo(h - 1)

                for k in range(8):
                    score(0, k)
                for k in range(2):
                    score(1, k)
                head(0, 0, v=False)
                with pe.Fori(0, H // 2 - 2) as j:
                    head(2 * j + 1, 1)
                    head(2 * j + 2, 0)
                head(H - 3, 1)
                head(H - 2, 0, bc=False)
                head(H - 1, 1, scores=False, bc=False)
                vo(H - 1)

            pe.wait_ge(s_acc, B * H + 1)
            pe.wait_ge(f_small, 16)
            for k in range(KT):
                m = pe.transpose(bank[2][:, k * E:(k + 1) * E], rw[:, k * P:(k + 1) * P], ident[0:E, 0:E])
            m.then_inc(f_rt, 1)
            for t in range(NT):
                pe.wait_ge(f_xn, t + 1)
                pe.wait_ge(f_tlo, t + 1)
                for k in range(KT):
                    m = pe.transpose(bank[t % 2][:, k * P:(k + 1) * P], xn2[:, t, k * P:(k + 1) * P], ident[:, :])
                m.then_inc(f_tp, 1)
            pe.wait_ge(f_rtc, 1)
            pe.wait_ge(f_tlo, NT + 2)
            for t in range(NT):
                for k in range(KT):
                    m = splits3(pe, bank[3][:, t * E:(t + 1) * E], (xt_hi[:, t, k, :], xt_lo[:, t, k, :]),
                                (rwt_hi[:, k, :], rwt_lo[:, k, :]), start=(k == 0), stop=(k == KT - 1))
            m.then_inc(f_lg, 1)

            pe.wait_ge(f_onehot, 1)
            flat = onehot_b[:, :, :].rearrange("p t e -> p (t e)")
            pe.matmul(bank[3][:, 0:NT * E], before[:, :], flat, start=True, stop=True)
            pe.matmul(bank[3][:, NT * E:2 * NT * E], ones_b[:, :], flat, start=True, stop=True).then_inc(f_rank, 1)
            pe.wait_ge(f_pos, 1)

            def weights(kind, t, cols):
                if kind == "shared":
                    return w_hi[:, E, cols], w_lo[:, E, cols]
                return w_hi[:, ds(t, 1), cols], w_lo[:, ds(t, 1), cols]

            def owner_of(kind, t):
                if kind == "shared":
                    return None
                return pe.value_load(owner_i[0:1, ds(t, 1)], min_val=0, max_val=E - 1)

            def gate_or_up(kind, half, e, i, t, u):
                if half == 0:
                    pe.wait_ge(f_silu, i + 1)
                    if kind == "routed":
                        pe.wait_ge(f_xsl, t + 2)
                else:
                    pe.wait_ge(f_h, i + 1)
                for k in range(KT):
                    lhs = ((xt_hi[:, ds(t, 1), k, :], xt_lo[:, ds(t, 1), k, :]) if kind == "shared" else
                           (xs_hi[:, u, k, :], xs_lo[:, u, k, :]))
                    m = splits3(pe, bank[2 * half + u][:, :], lhs,
                                weights(kind, e, slice(k * F2 + half * FF, k * F2 + (half + 1) * FF)),
                                start=(k == 0), stop=(k == KT - 1))
                m.then_inc(f_gu if half else f_g, 1)

            def mid_t(i, u):
                pe.wait_ge(f_h, i + 3)
                pe.wait_ge(f_hlo, i + 1)
                for f in range(FTT):
                    m = pe.transpose(bank[4 + u][:, f * P:(f + 1) * P], hmid[:, u, f * P:(f + 1) * P], ident[:, :])
                m.then_inc(f_ht, 1)

            def down_mm(kind, e, i, u):
                pe.wait_ge(f_hlo, i + 3)
                pe.wait_ge(f_acc, i + 1)
                for f in range(FTT):
                    m = splits3(pe, bank[6][:, 0:DM], (ht_hi[:, u, f, :], ht_lo[:, u, f, :]),
                                weights(kind, e, slice(KT * F2 + f * DM, KT * F2 + (f + 1) * DM)),
                                start=(f == 0), stop=(f == FTT - 1))
                m.then_inc(f_y, 1)

            def sorted_t(t, n, u):
                pe.wait_ge(f_xld[u], 16 * n + 16)
                pe.wait_ge(f_xsl, t + 1)
                for k in range(KT):
                    m = pe.transpose(bank[7][:, k * P:(k + 1) * P], xs_in[:, u, k * P:(k + 1) * P], ident[:, :])
                m.then_inc(f_xsp, 1)

            def tile(kind, i, t, n, u, more, more2):
                if more:
                    e1 = owner_of(kind, t + 1)
                    gate_or_up(kind, 0, e1, i + 1, t + 1, 1 - u)
                mid_t(i, u)
                if more:
                    gate_or_up(kind, 1, e1, i + 1, t + 1, 1 - u)
                if more2 and kind == "routed":
                    sorted_t(t + 2, n + 1, u)
                down_mm(kind, owner_of(kind, t), i, u)

            def experts(kind, count, first, i0, p0):
                if kind == "routed":
                    sorted_t(0, 0, 0)
                    sorted_t(1, 0, 1)
                e0 = owner_of(kind, first)
                for half in range(2):
                    gate_or_up(kind, half, e0, i0, first, p0)
                full = (count - 2) // 2
                with pe.Fori(0, full) as j:
                    for n in range(2):
                        tile(kind, 2 * j + n + i0, 2 * j + n + first, j, (n + p0) % 2, True, True)
                for t in range(2 * full, count):
                    tile(kind, i0 + t, first + t, t // 2, (t + p0) % 2, t + 1 < count, t + 2 < count)

            pe.wait_ge(f_w, 2)
            experts("shared", HALF, 0, 0, 0)
            pe.wait_ge(f_w, E + 2)
            pe.wait_ge(f_owner, 1)
            experts("routed", NS, 0, HALF, HALF % 2)
            experts("shared", NT - HALF, HALF, HALF + NS, (HALF + NS) % 2)

        @block.scalar
        def _(act):
            for k in range(2):
                if k == 0:
                    act.wait_ge(ld["wk"], 32)
                act.activation(wk_hi[:, k * 1024:(k + 1) * 1024], stage_wk[k], ACT.Copy).then_inc(w_hi_s, 1)
            act.wait_ge(gcol_s, 1)
            for h in range(H):
                act.wait_ge(wk_t, h + 1)
                act.activation(wkt_hi[:, h, :], T_BANK[h % 2][:, 0:P], ACT.Copy, scale=gcol[:, 2:3]).then_inc(wk_th, 1)
            for b in range(B):
                act.wait_ge(xt_ps, b + 1)
                act.activation(xnt_hi[:, b, :], bank[5 + 2 * (b % 2)][:, :], ACT.Copy).then_inc(xt_hi_s, 1)
            for h in range(H):
                act.wait_ge(wv_t, h + 1)
                act.activation(wvt[:, (h % 8) * P:(h % 8 + 1) * P], S_BANK[h % 2][:, 0:P], ACT.Copy).then_inc(wv_ts, 1)
                act.wait_ge(vo_ps, h + 1)
                act.activation(vo_hi[:, h, :], O_BANK[:, 0:DM], ACT.Copy).then_inc(vo_h, 1)
            for n in range(4):
                k, s = n // 2, n % 2
                if n == 0:
                    act.wait_ge(ld["wq"], 64)
                act.activation(wq_hi[:, k, s * 1024:(s + 1) * 1024], (stage_wk + stage_wv)[n], ACT.Copy
                               ).then_inc(w_hi_s, 1)
            act.wait_ge(ld["small"], 64)
            act.activation(gates[:, 2:4], gates[:, 0:2], ACT.Tanh).then_inc(gate_s, 1)

            with act.Fori(0, B) as b:
                act.wait_ge(ctx_ld, b * 32 + 32)
                act.wait_ge(s_pv, b * (H * NG) + NG)
                act.activation(ctx_hi[:, 0:FT, :], ctx_f[:, 0:FT, :], ACT.Copy).then_inc(ctx_split, 1)
                act.activation(ctx_hi[0:LAST, FT, :], ctx_f[0:LAST, FT, :], ACT.Copy).then_inc(ctx_split, 1)
                for c in range(4):
                    c1 = min(KV, (c + 1) * 512)
                    act.wait_ge(tp_ps, b * 4 + c + 1)
                    act.activation(ctxt_hi[:, c * 512:c1], bank[c][:, 0:c1 - c * 512], ACT.Copy).then_inc(tp_hi, 1)

                def squares(t, r):
                    for g in range(4):
                        i = (b * NKT + t) * 4 + g
                        act.wait_ge(kn_sum, i + 1)
                        act.wait_ge(kn_ps, i + 1)
                        act.activation(k_sq[0:r, g % 2, :], bank[g][0:r, :], ACT.Square).then_inc(kn_sq, 1)
                with act.Fori(0, FT) as t:
                    squares(t, P)
                squares(FT, LAST)

                def q_evac(h, u):
                    act.wait_ge(rq_ps, b * H + h + 1)
                    act.wait_ge(q_ps, b * H + h + 1)
                    act.activation(q_sq[:, u, :], bank[u][:, 0:SQ], ACT.Square).then_inc(q_sq_s, 1)
                    act.activation(q_hi[:, u, :], bank[u][:, 0:SQ], ACT.Copy).then_inc(q_hi_s, 1)

                def qp_evac(h, u):
                    act.wait_ge(qp_ps, b * H + h + 1)
                    act.activation(qp_hi[:, ds(h, 1), :], bank[4 + u % 2][:, 0:SQ], ACT.Copy).then_inc(qp_hi_s, 1)

                def bcast_copy(h, u, j):
                    n = b * H + h
                    c0, cn = CH[j]
                    act.wait_ge(s_scd, 8 * n + j + 5)
                    act.wait_ge(s_rb, 4 * n + j + 1)
                    act.activation(RK[u][:, c0:c0 + cn], R_BANK[:, 0:cn], ACT.Copy).then_inc(s_rbc, 1)

                q_evac(0, 0)
                q_evac(1, 1)
                with act.Fori(0, 2) as j:
                    for u in range(4):
                        q_evac(4 * j + u + 2, (u + 2) % 4)
                        qp_evac(4 * j + u, u)
                for h in range(8, H):
                    if h + 2 < H:
                        q_evac(h + 2, (h + 2) % 4)
                    qp_evac(h, h % 4)
                    if h == 8:
                        act.wait_ge(rkt_tp, 2 * b + 1)
                        act.activation(rkt[:, 0:8 * P], rkt_ps[0:3 * H, :], ACT.Copy).then_inc(rkt_c, 1)
                    elif h == 10:
                        act.wait_ge(rkt_tp, 2 * b + 2)
                        act.activation(rkt[:, 8 * P:KV], rkt_ps[0:3 * H, 0:KV - 8 * P], ACT.Copy).then_inc(rkt_ready, 1)
                    elif h >= 12:
                        for j in range(2 * (h - 12), 2 * (h - 12) + 2):
                            bcast_copy(j // 4, j // 4, j % 4)

                def exps(h, u, q):
                    act.wait_ge(rq_ready, b + 1)
                    act.wait_ge(s_nb, (b * H + h) * 2 + q + 1)
                    act.activation(SP[u][q][:, :], SP[u][q][:, :], ACT.Exp, bias=nbias[:, q:q + 1],
                                   scale=rq[:, q, ds(h, 1)], accum_out=psum_p[:, u, q:q + 1]).then_inc(s_exp, 1)

                def p_hi(h, g):
                    n = b * H + h
                    act.wait_ge(s_pv, n * NG + g + 1)
                    act.wait_ge(s_tr, n * NG + g + 1)
                    for r, w in group_parts(g):
                        m = act.activation(pt_hi[0:r, g, w, :], T_BANK[g % 3][0:r, :].rearrange(
                            "p (s q) -> p s q", s=2)[:, w, :], ACT.Copy)
                    m.then_inc(s_hi, 1)

                def head(h, u, scores=True, bc=True):
                    for step in "H0 H1 R0 H2 X0 R1 H3 R2 H4 R3 H5 H6 X1 O".split():
                        kind, i = step[0], int(step[1:] or 0)
                        if kind == "H":
                            p_hi(h, i)
                        elif kind == "X" and scores:
                            exps(h + 1, 1 - u, i)
                        elif kind == "R" and bc:
                            bcast_copy(h + 2, u, i)
                        elif kind == "O":
                            n = b * H + h
                            act.wait_ge(s_pv, n * NG + 2 * NG)
                            act.wait_ge(s_vo, n + 1)
                            act.activation(ot_hi[:, :], O_BANK[:, 0:SQ], ACT.Copy, scale=1.0 / P_SCALE).then_inc(s_oh, 1)

                for q in range(QT):
                    exps(0, 0, q)
                head(0, 0)
                with act.Fori(0, H // 2 - 2) as j:
                    head(2 * j + 1, 1)
                    head(2 * j + 2, 0)
                head(H - 3, 1)
                head(H - 2, 0, bc=False)
                head(H - 1, 1, scores=False, bc=False)
            with act.Fori(0, NT // 2) as j:
                for u in range(2):
                    t = 2 * j + u
                    act.wait_ge(f_tp, t + 1)
                    act.activation(xt_hi[:, ds(t, 1), :, :].rearrange("p a k q -> p (a k q)"), bank[u][:, 0:DM], ACT.Copy
                                   ).then_inc(f_thi, 1)
            act.wait_ge(f_lgc, 1)
            act.activation(smax[:, 1, :], smax[:, 0, :], ACT.Exp, scale=-1.0).then_inc(f_sel, 1)

            def w_split_hi(n):
                act.wait_ge(f_ld1 if n % 2 else f_ld0, 32 * ((n + 1) // 2) if n % 2 else 48 + 16 * n)
                act.activation(w_hi[:, (n - 1) % (E + 1), :], wstage[:, n % 2, :], ACT.Copy).then_inc(f_whi, 1)

            def silu_of(i, u):
                act.wait_ge(f_g, i + 1)
                act.wait_ge(f_h, i + 1)
                act.activation(silu[:, u, :], bank[u][:, :], ACT.Silu).then_inc(f_silu, 1)

            def h_hi(i, u):
                act.wait_ge(f_ht, i + 1)
                act.wait_ge(f_y, i + 1)
                act.activation(ht_hi[:, u, :, :].rearrange("p f q -> p (f q)"), bank[4 + u][:, :], ACT.Copy
                               ).then_inc(f_hhi, 1)

            def sorted_hi(t, u):
                act.wait_ge(f_xsp, t + 1)
                act.wait_ge(f_gu, HALF + t - 1) if not (type(t) is int and t < 2) else None
                act.activation(xs_hi[:, u, :, :].rearrange("p k q -> p (k q)"), bank[7][:, 0:DM], ACT.Copy
                               ).then_inc(f_xsh, 1)

            def y_out(i, t, n, u):
                act.wait_ge(f_y, i + 3)
                act.wait_ge(f_yst[u], 16 * n) if not (type(n) is int and n == 0) else None
                act.activation(ys_out[:, u, :], bank[6][:, 0:DM], ACT.Copy).then_inc(f_acc, 1)

            def tile(kind, i, t, n, u, more, more2):
                if more:
                    silu_of(i + 1, 1 - u)
                h_hi(i, u)
                if kind == "routed":
                    if more2:
                        sorted_hi(t + 2, u)
                    y_out(i, t, n, u)

            def experts(kind, count, first, i0, p0):
                if kind == "routed":
                    sorted_hi(0, 0)
                    sorted_hi(1, 1)
                silu_of(i0, p0)
                peeled = 2 if kind == "routed" else count
                for t in range(0, peeled):
                    tile(kind, i0 + t, first + t, t // 2, (t + p0) % 2, t + 1 < count, t + 2 < count)
                    if kind == "shared" and first == 0:
                        w_split_hi(t + 1)
                if kind == "routed":
                    full = (count - 2) // 2
                    with act.Fori(1, full) as j:
                        for n in range(2):
                            tile(kind, 2 * j + n + i0, 2 * j + n + first, j, (n + p0) % 2, True, True)
                    for t in range(2 * full, count):
                        tile(kind, i0 + t, first + t, t // 2, (t + p0) % 2, t + 1 < count, t + 2 < count)
            w_split_hi(0)
            experts("shared", HALF, 0, 0, 0)
            experts("routed", NS, 0, HALF, HALF % 2)
            experts("shared", NT - HALF, HALF, HALF + NS, (HALF + NS) % 2)

        @block.vector
        def _(dve):
            for s, v in ((s_scd, 16), (s_lo, 7), (s_pv, 7), (s_ol, 1), (s_acc, 1), (s_rbc, 1), (s_vo, 1), (s_exp, 2),
                         (kn_sq, 4), (kn_sum, 2), (q_lo_s, 4), (qp_lo_s, 2), (rq_ps, 4), (ctx_free, 1)):
                dve.sem_inc(s, v)
            setup = Chain(dve, setup_chain)
            setup(dve.memset(ssk[:, :, :], 1.0))
            dve.wait_ge(ld["small"], 64)
            dve.tensor_tensor(gcol[:, 2:3], gcol[:, 0:1], gcol[:, 1:2], ALU.mult).then_inc(gcol_s, 1)
            for k in range(2):
                cols = slice(k * 1024, (k + 1) * 1024)
                dve.wait_ge(w_hi_s, k + 1)
                dve.tensor_tensor(wk_lo[:, cols], stage_wk[k], wk_hi[:, cols], ALU.subtract).then_inc(w_split, 1)
            dve.wait_ge(gcol_s, 1)
            for h in range(H):
                dve.wait_ge(wk_th, h + 1)
                dve.scalar_tensor_tensor(out=wkt_lo[:, h, :], in0=T_BANK[h % 2][:, 0:P], scalar=gcol[:, 2:3],
                                         in1=wkt_hi[:, h, :], op0=ALU.mult, op1=ALU.subtract).then_inc(wk_ts, 1)
            dve.wait_ge(ld["x"], 16)
            for t in range(NT):
                setup(dve.bn_stats(stats[:, t, :], x_all[:, t, :]))
                setup(dve.bn_aggr(mv[:, t, :], stats[:, t, :]))
            v, y, w = (ssc[:, i, 0:NT] for i in range(3))
            setup(dve.tensor_scalar(v, mv[:, :, 1], EPS, None, ALU.add))
            rsqrt(dve, setup, v, y, w)
            for b in range(B + 1):
                if b < B:
                    if b >= 2:
                        dve.wait_ge(xt_ps, b - 1)
                    for t in range(b * QT, b * QT + QT):
                        dve.tensor_scalar(xn[:, t % 4, :], x_all[:, t, :], mv[:, t, 0:1], ssc[:, 1, t:t + 1],
                                          ALU.subtract, ALU.mult).then_inc(xn_ready, 1)
                if b >= 1:
                    dve.wait_ge(xt_hi_s, b)
                    dve.tensor_tensor(xnt_lo[:, b - 1, :], bank[5 + 2 * ((b - 1) % 2)][:, :], xnt_hi[:, b - 1, :],
                                      ALU.subtract).then_inc(xt_lo_s, 1)
            for h in range(H):
                dve.wait_ge(vo_h, h + 1)
                dve.tensor_tensor(vo_lo[:, h, :], O_BANK[:, 0:DM], vo_hi[:, h, :], ALU.subtract).then_inc(vo_s, 1)
            for n in range(4):
                k, cols = n // 2, slice(n % 2 * 1024, (n % 2 + 1) * 1024)
                dve.wait_ge(w_hi_s, n + 3)
                dve.tensor_tensor(wq_lo[:, k, cols], (stage_wk + stage_wv)[n], wq_hi[:, k, cols], ALU.subtract
                                  ).then_inc(w_split, 1)
            dve.wait_ge(gate_s, 1)
            setup(dve.tensor_scalar(g1[:, :], gates[:, 2:3], P_SCALE, None, ALU.mult))

            with dve.Fori(0, B) as b:
                chain = Chain(dve, prep_chain, b * PREP_STEPS)
                dve.wait_ge(ctx_split, b * 2 + 2)
                dve.tensor_tensor(ctx_lo[:, 0:FT, :], ctx_f[:, 0:FT, :], ctx_hi[:, 0:FT, :], ALU.subtract
                                  ).then_inc(ctx_lo_s, 1)
                dve.tensor_tensor(ctx_lo[0:LAST, FT, :], ctx_f[0:LAST, FT, :], ctx_hi[0:LAST, FT, :], ALU.subtract
                                  ).then_inc(ctx_lo_s, 1)
                for c in range(4):
                    c1 = min(KV, (c + 1) * 512)
                    dve.wait_ge(tp_hi, b * 4 + c + 1)
                    dve.tensor_tensor(ctxt_lo[:, c * 512:c1], bank[c][:, 0:c1 - c * 512], ctxt_hi[:, c * 512:c1],
                                      ALU.subtract).then_inc(tp_lo, 1)
                dve.wait_ge(ctx_lo_s, b * 2 + 2)
                dve.wait_ge(tp_lo, b * 4 + 4)
                dve.sem_inc(ctx_free, 1)

                def key_sums(t, r):
                    for g in range(4):
                        i = (b * NKT + t) * 4 + g
                        dve.wait_ge(kn_sq, i + 5)
                        dve.tensor_reduce(ssk[0:r, ds(t, 1), g * 4:(g + 1) * 4], k_sq[0:r, g % 2, :].rearrange(
                            "p (h d) -> p h d", h=4), X, ALU.add).then_inc(kn_sum, 1)
                with dve.Fori(0, FT) as t:
                    key_sums(t, P)
                key_sums(FT, LAST)
                dve.wait_ge(kn_sum, (b + 1) * NKT * 4 + 2)
                v, y, w = ssc[:, 0, :], ssc[:, 1, :], ssc[:, 2, :]
                chain(dve.tensor_scalar(v, ssk[:, :, :].rearrange("p t h -> p (t h)"), 1.0 / D, EPS, ALU.mult, ALU.add))
                guess(dve, chain, v, y, w).then_inc(rk_guess, 1)

                def q_rest(h, u):
                    dve.wait_ge(q_hi_s, b * H + h + 1)
                    dve.tensor_tensor(q_lo[:, u, :], bank[u][:, 0:SQ], q_hi[:, u, :], ALU.subtract).then_inc(q_lo_s, 1)

                def qp_rest(h, u):
                    dve.wait_ge(qp_hi_s, b * H + h + 1)
                    dve.tensor_tensor(qp_lo[:, ds(h, 1), :], bank[4 + u % 2][:, 0:SQ], qp_hi[:, ds(h, 1), :], ALU.subtract
                                      ).then_inc(qp_lo_s, 1)
                q_rest(0, 0)
                q_rest(1, 1)
                with dve.Fori(0, 2) as j:
                    for u in range(4):
                        q_rest(4 * j + u + 2, (u + 2) % 4)
                        qp_rest(4 * j + u, u)
                for h in range(8, H):
                    if h + 2 < H:
                        q_rest(h + 2, (h + 2) % 4)
                    qp_rest(h, h % 4)
                dve.wait_ge(rq_ps, (b + 1) * H + 4)
                v, y, w = rs3[:, 0, :], rs3[:, 1, :], rs3[:, 2, :]
                chain(dve.tensor_scalar(v, bank[6][:, 0:QT * H], 1.0 / D, EPS, ALU.mult, ALU.add))
                guess(dve, chain, v, y, w).then_inc(rq_guess, 1)
                assert chain.n == PREP_STEPS, chain.n

                def scaled(h, u, k):
                    n, q, (c0, cn) = b * H + h, k // 4, CH[k % 4]
                    if k < 4:
                        dve.wait_ge(s_rbc, 4 * n + k + 2)
                    dve.wait_ge(s_sc, 8 * n + k + 1)
                    dve.sem_inc(paced_dve, 1)
                    dve.tensor_tensor_reduce(SP[u][q][:, c0:c0 + cn], S_BANK[SCORE_BANK[k]][:, 0:cn],
                                             RK[u][:, c0:c0 + cn], 1.0, NEG, ALU.mult, ALU.max,
                                             mx4[:, q, k % 4:k % 4 + 1]).then_inc(s_scd, 1)

                def bias(h, q):
                    n = b * H + h
                    dve.wait_ge(s_scd, 8 * n + 4 * q + 4 + 16)
                    dve.wait_ge(s_exp, 2 * n + q + 1)
                    dve.tensor_reduce(mx[:, q:q + 1], mx4[:, q, :], X, ALU.max).then_inc(max_chain, 1)
                    dve.wait_ge(rq_ready, b + 1)
                    dve.wait_ge(max_chain, 2 * n + q + 1)
                    dve.tensor_scalar(nbias[:, q:q + 1], mx[:, q:q + 1], nrq[:, q, ds(h, 1)], LN_P_SCALE,
                                      ALU.mult, ALU.add).then_inc(s_nb, 1)

                def p_rest(h, g):
                    n = b * H + h
                    dve.wait_ge(s_hi, n * NG + g + 1)
                    for r, w in group_parts(g):
                        m = dve.tensor_tensor(pt_lo[0:r, g, w, :], T_BANK[g % 3][0:r, :].rearrange(
                            "p (s q) -> p s q", s=2)[:, w, :], pt_hi[0:r, g, w, :], ALU.subtract)
                    m.then_inc(s_lo, 1)

                def ot_rest(h, u):
                    n = b * H + h
                    dve.wait_ge(s_oh, n + 1)
                    dve.scalar_tensor_tensor(out=ot_lo[:, :], in0=O_BANK[:, 0:SQ], scalar=1.0 / P_SCALE,
                                             in1=ot_hi[:, :], op0=ALU.mult, op1=ALU.subtract).then_inc(s_ol, 1)
                    dve.wait_ge(s_acc, n + 1)
                    dve.reciprocal(rden[:, :], psum_p[:, u, :]).then_inc(den_chain, 1)
                    dve.wait_ge(den_chain, 2 * n + 1)
                    dve.tensor_scalar(rden[:, :], rden[:, :], g1[:, 0:1], None, ALU.mult).then_inc(den_chain, 1)

                def add_head(h):
                    n = b * H + h
                    dve.wait_ge(den_chain, 2 * n + 2)
                    dve.wait_ge(s_vo, n + 2)
                    for q in range(QT):
                        xt = x_all[:, ds(b * QT + q, 1), :]
                        m = dve.scalar_tensor_tensor(out=xt, in0=V_BANK[:, q * DM:(q + 1) * DM],
                                                     scalar=rden[:, q:q + 1], in1=xt, op0=ALU.mult, op1=ALU.add)
                    m.then_inc(s_acc, 1)

                def head(h, u, scores=True, more=True, add=True):
                    for step in "L0 T2 A L1 T3 M0 L2 T4 L3 T5 L4 T6 L5 T7 M1 L6 N0 N1 O".split():
                        kind, i = step[0], int(step[1:] or 0)
                        if kind == "T" and scores:
                            scaled(h + 1, 1 - u, i)
                        elif kind == "N" and more:
                            scaled(h + 2, u, i)
                        elif kind == "M" and scores:
                            bias(h + 1, i)
                        elif kind == "L":
                            p_rest(h, i)
                        elif kind == "O":
                            ot_rest(h, u)
                        elif kind == "A" and add:
                            add_head(h - 1)

                for k in range(8):
                    scaled(0, 0, k)
                    if k % 4 == 3:
                        bias(0, k // 4)
                for k in range(2):
                    scaled(1, 1, k)
                head(0, 0, add=False)
                with dve.Fori(0, H // 2 - 2) as j:
                    head(2 * j + 1, 1)
                    head(2 * j + 2, 0)
                head(H - 3, 1)
                head(H - 2, 0, more=False)
                head(H - 1, 1, scores=False, more=False)
                add_head(H - 1)
            for sm, v in ((f_tlo, 2), (f_silu, 2), (f_h, 2), (f_hlo, 2), (f_acc, 1), (f_w, 1), (f_y, 2), (f_xsl, 1)):
                dve.sem_inc(sm, v)
            chain = Chain(dve, f_chain)
            dve.wait_ge(s_acc, B * H + 1)
            for t in range(NT):
                chain(dve.bn_stats(stats[:, t, :], x_all[:, t, :]))
                chain(dve.bn_aggr(mv[:, t, :], stats[:, t, :]))
            v, y, w = (ssc[:, i, 0:NT] for i in range(3))
            chain(dve.tensor_scalar(v, mv[:, :, 1], EPS, None, ALU.add))
            rsqrt(dve, chain, v, y, w)
            for t in range(NT):
                dve.tensor_scalar(xn2[:, t, :], x_all[:, t, :], mv[:, t, 0:1], ssc[:, 1, t:t + 1],
                                  ALU.subtract, ALU.mult).then_inc(f_xn, 1)
            dve.wait_ge(f_rt, 1)
            chain(dve.tensor_copy(rwt_hi[:, :, :].rearrange("p k e -> p (k e)"), bank[2][:, 0:KT * E]))
            dve.tensor_tensor(rwt_lo[:, :, :].rearrange("p k e -> p (k e)"), bank[2][:, 0:KT * E],
                              rwt_hi[:, :, :].rearrange("p k e -> p (k e)"), ALU.subtract).then_inc(f_rtc, 1)
            with dve.Fori(0, NT // 2) as j:
                for u in range(2):
                    t = 2 * j + u
                    flat = lambda a: a[:, ds(t, 1), :, :].rearrange("p a k q -> p (a k q)")
                    dve.wait_ge(f_thi, t + 1)
                    dve.tensor_tensor(flat(xt_lo), bank[u][:, 0:DM], flat(xt_hi), ALU.subtract).then_inc(f_tlo, 1)
            dve.wait_ge(f_lg, 1)
            chain(dve.tensor_copy(logit[:, :, :].rearrange("p t e -> p (t e)"), bank[3][:, 0:NT * E]))
            dve.tensor_reduce(smax[:, 0, :], logit[:, :, :], X, ALU.max).then_inc(f_lgc, 1)
            dve.wait_ge(f_sel, 1)
            chain(dve.tensor_scalar(smax[:, 1, :], smax[:, 1, :], 1.0, None, ALU.add))
            chain(dve.reciprocal(smax[:, 1, :], smax[:, 1, :]))
            chain(dve.memset(smax[:, 3, :], 1.0))
            for e in range(E):
                chain(dve.tensor_tensor(smax[:, 2, :], logit[:, :, e], smax[:, 0, :], ALU.is_equal))
                chain(dve.tensor_tensor(onehot[:, :, e], smax[:, 2, :], smax[:, 3, :], ALU.mult))
                chain(dve.tensor_tensor(smax[:, 3, :], smax[:, 3, :], onehot[:, :, e], ALU.subtract))
            dve.tensor_copy(onehot_b[:, :, :], onehot[:, :, :]).then_inc(f_onehot, 1)
            for t in range(NT):
                dve.tensor_scalar(xn2[:, t, :], xn2[:, t, :], smax[:, 1, t:t + 1], None, ALU.mult).then_inc(f_xr, 1)
            dve.wait_ge(f_rank, 1)
            chain(dve.tensor_copy(slot[:, :, :].rearrange("p t e -> p (t e)"), bank[3][:, 0:NT * E]))
            chain(dve.tensor_copy(count[:, :, :].rearrange("p t e -> p (t e)"), bank[3][:, NT * E:2 * NT * E]))
            chain(dve.tensor_reduce(ecol[:, 0, :], count[:, :, :].rearrange("p t e -> p e t"), X, ALU.add))
            chain(dve.tensor_scalar(etile[:, :], ecol[:, 0, :], 1.0 / P, (P - 1) / (2.0 * P), ALU.mult, ALU.add))
            chain(dve.tensor_copy(ecol[:, 1, :], etile[:, :]))
            chain(dve.tensor_copy(ecol[:, 2, 0:1], ecol[:, 1, 0:1]))
            for e in range(1, E):
                chain(dve.tensor_tensor(ecol[:, 2, e:e + 1], ecol[:, 2, e - 1:e], ecol[:, 1, e:e + 1], ALU.add))
            chain(dve.tensor_tensor(ecol[:, 3, :], ecol[:, 2, :], ecol[:, 1, :], ALU.subtract))
            chain(dve.tensor_scalar(run[:, 0, :], ecol[:, 3, :], float(P), None, ALU.mult))
            for t in range(1, NT):
                chain(dve.tensor_tensor(run[:, t, :], run[:, t - 1, :], count[:, t - 1, :], ALU.add))
            chain(dve.tensor_tensor(slot[:, :, :], slot[:, :, :], run[:, :, :], ALU.add))
            chain(dve.tensor_tensor(slot[:, :, :], slot[:, :, :], onehot[:, :, :], ALU.mult))
            chain(dve.tensor_reduce(pos[:, :], slot[:, :, :], X, ALU.add))
            dve.tensor_copy(pos_i[:, :], pos[:, :]).then_inc(f_pos, 1)
            chain(dve.tensor_scalar(owner[:, :], iota_s[:, :], ecol[:, 2, 0:1], None, ALU.is_ge))
            for e in range(1, E - 1):
                chain(dve.scalar_tensor_tensor(out=owner[:, :], in0=iota_s[:, :], scalar=ecol[:, 2, e:e + 1],
                                               in1=owner[:, :], op0=ALU.is_ge, op1=ALU.add))
            dve.tensor_copy(owner_i[:, :], owner[:, :]).then_inc(f_owner, 1)

            def w_split_lo(n):
                dve.wait_ge(f_whi, n + 1)
                dve.tensor_tensor(w_lo[:, (n - 1) % (E + 1), :], wstage[:, n % 2, :], w_hi[:, (n - 1) % (E + 1), :],
                                  ALU.subtract).then_inc(f_w, 1)

            def mid(i, u):
                dve.wait_ge(f_gu, i + 1)
                dve.wait_ge(f_silu, i + 3)
                dve.tensor_tensor(hmid[:, u, :], bank[2 + u][:, :], silu[:, u, :], ALU.mult).then_inc(f_h, 1)

            def h_lo(i, u):
                dve.wait_ge(f_hhi, i + 1)
                dve.tensor_tensor(ht_lo[:, u, :, :].rearrange("p f q -> p (f q)"), bank[4 + u][:, :],
                                  ht_hi[:, u, :, :].rearrange("p f q -> p (f q)"), ALU.subtract).then_inc(f_hlo, 1)

            def add_shared(i, t):
                xt = x_all[:, ds(t, 1), :]
                dve.wait_ge(f_y, i + 3)
                dve.scalar_tensor_tensor(out=xt, in0=bank[6][:, 0:DM], scalar=gates[:, 3:4], in1=xt,
                                         op0=ALU.mult, op1=ALU.add).then_inc(f_acc, 1)

            def sorted_lo(t, u):
                dve.wait_ge(f_xsh, t + 1)
                dve.tensor_tensor(xs_lo[:, u, :, :].rearrange("p k q -> p (k q)"), bank[7][:, 0:DM],
                                  xs_hi[:, u, :, :].rearrange("p k q -> p (k q)"), ALU.subtract).then_inc(f_xsl, 1)

            def tile(kind, i, t, u, more, more2):
                h_lo(i, u)
                if more:
                    mid(i + 1, 1 - u)
                if kind == "routed" and more2:
                    sorted_lo(t + 2, u)
                if kind == "shared":
                    add_shared(i, t)

            def experts(kind, count, first, i0, p0):
                if kind == "routed":
                    sorted_lo(0, 0)
                    sorted_lo(1, 1)
                mid(i0, p0)
                if kind == "shared":
                    for t in range(count):
                        tile(kind, i0 + t, first + t, (t + p0) % 2, t + 1 < count, t + 2 < count)
                        if first == 0:
                            w_split_lo(t + 1)
                else:
                    full = (count - 2) // 2
                    with dve.Fori(0, full) as j:
                        for n in range(2):
                            tile(kind, 2 * j + n + i0, 2 * j + n + first, (n + p0) % 2, True, True)
                    for t in range(2 * full, count):
                        tile(kind, i0 + t, first + t, (t + p0) % 2, t + 1 < count, t + 2 < count)
            w_split_lo(0)
            experts("shared", HALF, 0, 0, 0)
            experts("routed", NS, 0, HALF, HALF % 2)
            experts("shared", NT - HALF, HALF, HALF + NS, (HALF + NS) % 2)
            for t in range(NT):
                dve.wait_ge(f_gat[t // 4], 4 * 16)
                dve.wait_ge(f_acc, NT + NS + 1)
                dve.scalar_tensor_tensor(out=x_all[:, t, :], in0=ys_in[:, t, :], scalar=gates[:, 3:4],
                                         in1=x_all[:, t, :], op0=ALU.mult, op1=ALU.add).then_inc(f_done, 1)


_INS = ['x', 'ctx_1024', 'g_xattn', 'g_ffn', 'L0_xattn_Wq', 'L0_xattn_Wk', 'L0_xattn_Wv', 'L0_xattn_Wo',
        'L0_xattn_gq', 'L0_xattn_gk', 'L0_ffn_router_w', 'L0_ffn_gate_up_proj', 'L0_ffn_down_proj',
        'L0_ffn_shared_gate_w', 'L0_ffn_shared_up_w', 'L0_ffn_shared_down_w']
_OUTS = [((8, 256, 256), 'float32')]


def kernel(**inputs):
    import numpy as _np
    import concourse.bacc as _bacc
    from concourse import mybir as _mybir
    from concourse.bass_utils import run_bass_kernel_spmd as _run

    nc = _bacc.Bacc("TRN2", target_bir_lowering=False, num_devices=1)
    arrays, args = {}, []
    for name in _INS:
        a = _np.ascontiguousarray(inputs[name])
        arrays[f"in_{name}_dram"] = a
        args.append(nc.dram_tensor(f"in_{name}_dram", a.shape, _mybir.dt.from_np(a.dtype), kind="ExternalInput").ap())
    for i, (shape, dtype) in enumerate(_OUTS):
        dt = _mybir.dt.from_np(_np.dtype(dtype))
        args.append(nc.dram_tensor(f"out_{i}_dram", shape, dt, kind="ExternalOutput").ap())
    flamingo_layer(nc, *args)
    r = _run(nc, [arrays], core_ids=[0])
    return r.results[0]["out_0_dram"]
```

```python
from contextlib import ExitStack

import concourse.bass as bass
from concourse import mybir

F32 = mybir.dt.float32
F16 = mybir.dt.float16
BF16 = mybir.dt.bfloat16
I32 = mybir.dt.int32
ALU = mybir.AluOpType
ACT = mybir.ActivationFunctionType
X = mybir.AxisListType.X
ds = bass.ds

P = 128
EPS = 1e-5
LN_P_SCALE = 6.931471805599453
P_SCALE = 1024.0
RSQRT_MAGIC = 1597463007
NEG = -3.0e38


class Chain:

    def __init__(self, eng, sem, base=0, carrier=None):
        self.eng, self.sem, self.base, self.n, self.carrier = eng, sem, base, 0, carrier

    def __call__(self, ins):
        self.n += 1
        ins.then_inc(self.sem, 1)
        self.eng.wait_ge(self.sem, self.base + self.n)
        if self.carrier is not None:
            self.eng.sem_inc(self.carrier, 1)


def among_first(t, n):
    return type(t) is int and t < n


def flamingo_layer(nc, x, ctx, g_xattn, g_ffn, Wq, Wk, Wv, Wo, gq, gk,
                   router_w, gate_up, down, sh_gate, sh_up, sh_down, out):
    B, SQ, DM = x.shape
    KV, DC = ctx.shape[1], ctx.shape[2]
    D = gq.shape[0]
    H = Wq.shape[1] // D
    QT, KT = SQ // P, DM // P
    NT = B * QT
    FT = KV // P
    LAST = KV - FT * P
    NKT = FT + 1
    NG = (NKT + 1) // 2
    INNER = H * D
    E, _, F2 = gate_up.shape
    FF = F2 // 2
    FTT = FF // P
    WC = KT * F2 + FTT * DM
    HG = H // 2
    NS = NT + E - 1
    RANKS_AFTER = 2
    FIRST = 10
    assert DC == P and D == P and SQ == 256 and H % 2 == 0
    CH = [(0, 401), (401, 400), (801, 400), (1201, 400)]
    assert CH[-1][0] + CH[-1][1] == KV
    SCORE_BANK = [0, 1, 2, 0, 1, 2, 0, 1]
    CTX_SPLIT = {9: (P, slice(0, FT // 2)), 11: (P, slice(FT // 2, FT)), 13: (LAST, slice(FT, FT + 1))}
    AHEAD = 4
    RK_ROWS = {6: 0, 7: 1, 8: 2, 9: 3}
    PE_STEPS = "C0 S4 V C1 D0 C2 S5 S6 D1 C3 D2 C4 S7 D3 C5 D4 N0 N1 C6 D5 N2 D6 N3"
    ACT_STEPS = "H0 H1 H2 X0 H3 H4 H5 H6 X1 O"
    DVE_STEPS = "L0 M0 A L1 T4 L2 T5 T6 L3 L4 T7 M1 L5 N0 L6 N1 N2 N3 O"
    PE_LAST = "C0 V C1 D0 P0 C2 D1 P1 C3 D2 P2 C4 D3 C5 D4 P3 C6 D5 D6"
    ACT_LAST = "H0 H1 P0 H2 P1 H3 P2 H4 H5 P3 H6 O"
    DVE_LAST = "L0 A L1 P0 L2 P1 L3 P2 L4 L5 P3 L6 O"
    KROWS = [P] * FT + [LAST]

    top = ExitStack()
    with top:
        def sem(name):
            return top.enter_context(nc.semaphore(name))

        def sb(name, shape, dt, stack=top):
            return stack.enter_context(nc.sbuf_tensor(name, shape, dt))

        x_all = sb("x_all", [P, NT, DM], F32)
        ident = sb("ident", [P, P], F32)
        zeros = sb("zeros", [P, DM], F32)
        before = sb("before", [P, P], BF16)
        ones_b = sb("ones_b", [P, P], BF16)
        NO = NS + 3 - NS % 2
        iota_s = sb("iota_s", [P, NO], F32)
        one_col = sb("one_col", [P, 2 * HG - 1], F32)
        gates = sb("gates", [P, 4], F32)
        g1 = sb("g1", [P, 1], F32)
        gcol = sb("gcol", [P, 3], F32)
        ssc = sb("ssc", [P, 3, NKT * H], F32)
        stats = sb("stats", [P, NT, 6], F32)
        mv = sb("mv", [P, NT, 2], F32)
        rs3 = sb("rs3", [P, 3, QT * HG], F32)
        rs_rows = sb("rs_rows", [HG, SQ], F32)
        att = ExitStack()
        wq_hi = sb("wq_hi", [P, KT, INNER], F16, att)
        wq_lo = sb("wq_lo", [P, KT, INNER], F16, att)
        wk_hi = sb("wk_hi", [P, INNER], F16, att)
        wk_lo = sb("wk_lo", [P, INNER], F16, att)
        wkt_hi = sb("wkt_hi", [P, H, P], F16, att)
        wkt_lo = sb("wkt_lo", [P, H, P], F16, att)
        vo_hi = sb("vo_hi", [P, H, DM], F16, att)
        vo_lo = sb("vo_lo", [P, H, DM], F16, att)
        ctx_f = sb("ctx_f", [P, NKT, P], F32, att)
        ctx_hi = sb("ctx_hi", [P, NKT, P], F16, att)
        ctx_lo = sb("ctx_lo", [P, NKT, P], F16, att)
        ctxt_hi = sb("ctxt_hi", [P, KV], F16, att)
        ctxt_lo = sb("ctxt_lo", [P, KV], F16, att)
        xn = sb("xn", [P, 4, DM], F32, att)
        xnt_hi = sb("xnt_hi", [P, B, KT * SQ], F16, att)
        xnt_lo = sb("xnt_lo", [P, B, KT * SQ], F16, att)
        SP = [[sb(f"sp{u}{t}", [P, KV], F32, att) for t in range(QT)] for u in range(2)]
        RK = [sb(f"rk_bcast{u}", [P, KV], F32, att) for u in range(2)]
        pt_hi = sb("pt_hi", [P, NG, 2, SQ], F16, att)
        pt_lo = sb("pt_lo", [P, NG, 2, SQ], F16, att)
        qp_hi = sb("qp_hi", [P, H, SQ], F16, att)
        qp_lo = sb("qp_lo", [P, H, SQ], F16, att)
        q_hi = sb("q_hi", [P, 4, SQ], F16, att)
        q_lo = sb("q_lo", [P, 4, SQ], F16, att)
        q_sq = sb("q_sq", [P, 4, SQ], F32, att)
        k_sq = sb("k_sq", [P, 4, 512], F32, att)
        ssk = sb("ssk", [P, NKT, H], F32, att)
        rkt = sb("rkt", [H, KV], F32, att)
        rq = sb("rq", [P, QT, H], F32, att)
        nrq = sb("nrq", [P, QT, H], F32, att)
        mx4 = sb("mx4", [P, QT, 4], F32, att)
        mx = sb("mx", [P, QT], F32, att)
        nbias = sb("nbias", [P, QT], F32, att)
        psum_p = sb("psum_p", [P, 2, QT], F32, att)
        rden = sb("rden", [P, QT], F32, att)
        ot_hi = sb("ot_hi", [P, SQ], F16, att)
        ot_lo = sb("ot_lo", [P, SQ], F16, att)
        att.close()
        ffn = ExitStack()
        xn2 = sb("xn2", [P, NT, DM], F32, ffn)
        xt_hi = sb("xt_hi", [P, NT, KT, P], F16, ffn)
        xt_lo = sb("xt_lo", [P, NT, KT, P], F16, ffn)
        w16 = sb("w16", [P, E + 1, 2, WC], F16, ffn)
        w_hi, w_lo = w16[:, :, 0, :], w16[:, :, 1, :]
        silu = sb("silu", [P, 2, FF], F32, ffn)
        hmid = sb("hmid", [P, 2, FF], F32, ffn)
        ht_hi = sb("ht_hi", [P, 2, FTT, P], F16, ffn)
        ht_lo = sb("ht_lo", [P, 2, FTT, P], F16, ffn)
        xs_in = sb("xs_in", [P, 2, DM], F32, ffn)
        xs_hi = sb("xs_hi", [P, 2, KT, P], F16, ffn)
        xs_lo = sb("xs_lo", [P, 2, KT, P], F16, ffn)
        ys_out = sb("ys_out", [P, 2, DM], F32, ffn)
        ys_in = sb("ys_in", [P, NT, DM], F32, ffn)
        rw = ys_out[0:E, 0, :]
        rwt_hi = sb("rwt_hi", [P, KT, E], F16, ffn)
        rwt_lo = sb("rwt_lo", [P, KT, E], F16, ffn)
        logit = sb("logit", [P, NT, E], F32, ffn)
        smax = sb("smax", [P, 4, NT], F32, ffn)
        onehot = sb("onehot", [P, NT, E], F32, ffn)
        onehot_b = sb("onehot_b", [P, NT, E], BF16, ffn)
        count = sb("count", [P, NT, E], F32, ffn)
        slot = sb("slot", [P, NT, E], F32, ffn)
        run = sb("run", [P, NT, E], F32, ffn)
        ecol = sb("ecol", [P, 4, E], F32, ffn)
        etile = sb("etile", [P, E], I32, ffn)
        pos = sb("pos", [P, NT], F32, ffn)
        pos_i = sb("pos_i", [P, NT], I32, ffn)
        owner = sb("owner", [P, NO], F32, ffn)
        owners3 = sb("owners3", [P, NO // 2], F32, ffn)
        owners3_i = sb("owners3_i", [P, NO // 2], I32, ffn)
        ffn.close()

        rk_dram = nc.dram_tensor("keys_inverse_norms", [H, KV], F32).ap()
        w16_dram = nc.dram_tensor("split_weights", [(E + 1) * P, 2 * WC], F16).ap()
        CHUNK = FF
        CHUNKS = WC // CHUNK
        EB = (E - 1).bit_length()
        xs_dram = nc.dram_tensor("sorted_tokens", [NS * P, DM], F32).ap()
        ys_dram = nc.dram_tensor("sorted_outputs", [NS * P, DM], F32).ap()

        bank = [top.enter_context(nc.psum_tensor(f"bank{i}", [P, 512], F32)) for i in range(8)]
        S_BANK, T_BANK, O_BANK, V_BANK = bank[0:3], bank[3:6], bank[6], bank[7]
        X_BANK = bank[7]
        logit_ps = X_BANK[:, KT * E:(KT + NT) * E]
        rank_ps = X_BANK[:, (KT + NT) * E:(KT + 3 * NT) * E]

        ld = {n: sem("ld_" + n) for n in ("x", "small", "wk", "wv", "wo", "wq")}
        c_done = sem("consts_done")
        w_split, wk_t, wk_ts, wv_t, wv_ts, vo_ps, vo_s = map(sem, (
            "wsplit", "wkt_ps", "wkt_split", "wvt_ps", "wvt_copied", "vo_ps", "vo_split"))
        setup_chain, ln_stats, ln_aggr = map(sem, ("setup_chain", "ln_stats", "ln_aggr"))
        ctx_ld, ctx_free, xn_ready = map(sem, ("ctx_ld", "ctx_free", "xn_ready"))
        tp_ps, tp_hi, tp_lo = map(sem, ("tp_ps", "tp_hi", "tp_lo"))
        kn_ps, kn_sq, kn_sum = map(sem, ("kn_ps", "kn_sq", "kn_sum"))
        q_ps, q_hi_s, q_lo_s, qp_ps, qp_hi_s, qp_lo_s, rq_ps = map(sem, (
            "q_ps", "q_hi_s", "q_lo_s", "qp_ps", "qp_hi_s", "qp_lo_s", "rq_ps"))
        rk_ready, rkt_tp, rk_stored, rq_ready = map(sem, ("rk_ready", "rkt_tp", "rk_stored", "rq_ready"))
        rk_ld = [sem("rk_loaded0"), sem("rk_loaded1")]
        prep_chain, max_chain, den_chain, ctx_split = map(sem, (
            "prep_chain", "max_chain", "den_chain", "ctx_hi_done"))
        s_sc, s_scd, s_nb, s_exp, s_tr, s_hi, s_lo, s_pv, s_oh, s_ol, s_vo, s_acc = map(sem, (
            "score_ps", "score_used", "bias_ready", "exp_done", "pt_ps", "pt_hi_done",
            "pt_lo_done", "pv_done", "ot_hi_done", "ot_lo_done", "vo_done", "head_added"))
        f_small, f_w0, f_w1, f_xn, f_tp, f_thi, f_tlo, f_rt, f_rtc, f_lg, f_lgc, f_sel = map(sem, (
            "f_small", "f_w0", "f_w1", "f_xn", "f_tp", "f_thi", "f_tlo", "f_rt", "f_rtc", "f_lg",
            "f_lgc", "f_sel"))
        f_g, f_gu, f_silu, f_h, f_ht, f_hhi, f_hlo, f_y, f_acc, f_chain = map(sem, (
            "f_g", "f_gu", "f_silu", "f_h", "f_ht", "f_hhi", "f_hlo", "f_y", "f_acc", "f_chain"))
        f_xld, f_yst = [sem("f_xs_loaded0"), sem("f_xs_loaded1")], [sem("f_ys_stored0"), sem("f_ys_stored1")]
        f_gat = [sem(f"f_gathered{n}") for n in range(4)]
        f_onehot, f_rank, f_pos, f_owner, f_xr, f_zero, f_scat, f_xsp, f_xsh, f_xsl, f_done = map(
            sem, ("f_onehot", "f_rank", "f_pos", "f_owner", "f_xr", "f_zero", "f_scattered", "f_xs_ps",
                  "f_xs_hi", "f_xs_lo", "f_done"))
        st = sem("stored")
        w_loaded, w_chain, w_stored = map(sem, ("w_loaded", "w_chain", "w_stored"))
        paced_dve, paced_pe, paced_pool = sem("paced_dve"), sem("paced_pe"), sem("paced_pool")
        w_hi_s, gate_s, q_sq_s, rkt_c, ctx_lo_s = map(sem, ("w_hi_done", "gate_tanh", "q_squared", "rkt_copied", "ctx_lo_done"))
        rk_guess, rq_guess, rq_sum, rq_t, pool_chain, xt_ps, xt_hi_s, xt_lo_s, wk_th = map(sem, (
            "rk_guess", "rq_guess", "rq_sum", "rq_transposed", "pool_chain", "xt_ps", "xt_hi_s", "xt_lo_s", "wkt_hi_done"))
        PREP_STEPS = 2 + 2 * 2
        POOL_STEPS = 12 + 2 * (12 + 1)
        NEWTON = 3
        gcol_s, vo_h = sem("gcol_ready"), sem("vo_hi_done")

        block = top.enter_context(nc.Block())

        stage_wk = [SP[0][0][:, 0:1024], SP[0][1][:, 0:1024]]
        stage_wv = [SP[1][0][:, 0:1024], SP[1][1][:, 0:1024]]
        stage_wo = [a[:, :, :].rearrange("p h q -> p (h q)").bitcast(F32) for a in (qp_hi, qp_lo)]
        wvt = RK
        four = lambda h: slice((h % 8) * P, (h % 8 + 4) * P)

        def splits3(pe, ps, lhs, rhs, start=True, stop=True):
            pe.matmul(ps, lhs[0], rhs[0], start=start, stop=False)
            pe.matmul(ps, lhs[0], rhs[1], start=False, stop=False)
            return pe.matmul(ps, lhs[1], rhs[0], start=False, stop=stop)

        def group_parts(g):
            if 2 * g + 1 < FT:
                return [(P, slice(0, 2))]
            return [(KROWS[2 * g + i], slice(i, i + 1)) for i in range(2) if 2 * g + i < NKT]

        def rsqrt(dve, chain, v, y, t):
            chain(dve.tensor_scalar(t.bitcast(I32), v.bitcast(I32), 1, None, ALU.logical_shift_right))
            chain(dve.tensor_scalar(y.bitcast(I32), t.bitcast(I32), -1.0, float(RSQRT_MAGIC), ALU.mult, ALU.add))
            for _ in range(NEWTON):
                chain(dve.tensor_tensor(t, y, y, ALU.mult))
                chain(dve.scalar_tensor_tensor(out=t, in0=t, scalar=-0.5, in1=v, op0=ALU.mult, op1=ALU.mult))
                chain(dve.scalar_tensor_tensor(out=y, in0=t, scalar=1.5, in1=y, op0=ALU.add, op1=ALU.mult))

        def guess(dve, chain, v, y, t):
            chain(dve.tensor_scalar(t.bitcast(I32), v.bitcast(I32), 1, None, ALU.logical_shift_right))
            return dve.tensor_scalar(y.bitcast(I32), t.bitcast(I32), -1.0, float(RSQRT_MAGIC), ALU.mult, ALU.add)

        def newton(pool, chain, v, y, t):
            for _ in range(NEWTON):
                chain(pool.tensor_tensor(t, y, y, ALU.mult))
                chain(pool.tensor_tensor(t, t, v, ALU.mult))
                chain(pool.tensor_scalar(t, t, -0.5, 1.5, ALU.mult, ALU.add))
                chain(pool.tensor_tensor(y, y, t, ALU.mult))

        CONSTS = 9
        @block.sync
        def _(sp):
            def load_ctx(b):
                sp.dma_start(ctx_f[:, 0:FT, :], ctx[ds(b, 1), 0:FT * P, :].rearrange("a (t p) c -> p (a t) c", p=P)
                             ).then_inc(ctx_ld, 16)
                sp.dma_start(ctx_f[0:LAST, FT, :], ctx[ds(b, 1), FT * P:KV, :].rearrange("a p c -> p (a c)")
                             ).then_inc(ctx_ld, 16)

            for k in range(2):
                sp.dma_start(stage_wk[k], Wk[:, k * 1024:(k + 1) * 1024]).then_inc(ld["wk"], 16)
            sp.dma_start(gcol[:, 0:1], gq.rearrange("(d a) -> d a", a=1)).then_inc(ld["small"], 16)
            sp.dma_start(gcol[:, 1:2], gk.rearrange("(d a) -> d a", a=1)).then_inc(ld["small"], 16)
            sp.dma_start(gates[:, 0:1], g_xattn.rearrange("(a b) -> a b", a=1).broadcast_to([P, 1])).then_inc(ld["small"], 16)
            sp.dma_start(gates[:, 1:2], g_ffn.rearrange("(a b) -> a b", a=1).broadcast_to([P, 1])).then_inc(ld["small"], 16)
            sp.dma_start(x_all[:, :, :], x.rearrange("b (t p) m -> p (b t) m", p=P)).then_inc(ld["x"], 16)
            for k in range(2):
                sp.dma_start(stage_wv[k], Wv[:, k * 1024:(k + 1) * 1024]).then_inc(ld["wv"], 16)
            for k in range(2):
                sp.dma_start(stage_wo[k].rearrange("p (h m) -> p h m", h=8),
                             Wo[k * 8 * D:(k + 1) * 8 * D, :].rearrange("(h d) m -> d h m", d=D)).then_inc(ld["wo"], 16)
            load_ctx(0)
            for k in range(KT):
                for s in range(2):
                    n = 2 * k + s
                    buf = (stage_wk + stage_wv)[n]
                    if n == 0:
                        sp.wait_ge(wk_t, 4)
                        sp.wait_ge(w_split, 2)
                        sp.wait_ge(wv_t, 4)
                    sp.dma_start(buf, Wq[k * P:(k + 1) * P, s * 1024:(s + 1) * 1024]).then_inc(ld["wq"], 16)
            sp.wait_ge(c_done, CONSTS)
            with sp.Fori(0, NS) as j:
                sp.dma_start(xs_dram[ds(j * P, P), :], zeros[:, :]).then_inc(f_zero, 16)

            def load_rk(b, h, u):
                sp.wait_ge(s_scd, (b * H if among_first(h, 2) else b * H + h - 1) * 8 + 16)
                sp.dma_start(RK[u][:, :], rk_dram[ds(h, 1), :].broadcast_to([P, KV])).then_inc(rk_ld[u], 16)

            def batch_loads(b, last=False):
                sp.wait_ge(rkt_c, 4 * b + 5)
                sp.dma_start(rk_dram, rkt[:, :]).then_inc(rk_stored, 16)
                sp.wait_ge(rk_stored, 16 * b + 16)
                for h in range(2):
                    load_rk(b, h, h)
                if not last:
                    sp.wait_ge(ctx_free, b + 1)
                    load_ctx(b + 1)
                with sp.Fori(1, H // 2) as j:
                    for u in range(2):
                        load_rk(b, 2 * j + u, u)
            with sp.Fori(0, B - 1) as b:
                batch_loads(b)
            batch_loads(B - 1, last=True)
            w16_rows = w16_dram.rearrange("(e p) c -> p e c", p=P)
            sp.wait_ge(s_acc, B * H + 1)
            sp.dma_start(rw, router_w).then_inc(f_small, 16)
            sp.wait_ge(w_stored, 16 * (E + 1) * CHUNKS)
            sp.dma_start(w16[:, E, :, :].rearrange("p s c -> p (s c)"), w16_rows[:, E, :]).then_inc(f_w0, 16)
            with sp.Fori(0, E) as e:
                sp.dma_start(w16[:, ds(e, 1), :, :].rearrange("p e s c -> p e (s c)"), w16_rows[:, ds(e, 1), :]
                             ).then_inc(f_w1, 16)
            sp.wait_ge(f_scat, 16 * NT)
            for j in range(2):
                sp.dma_start(xs_in[:, j, :], xs_dram[j * P:(j + 1) * P, :]).then_inc(f_xld[j], 16)

            def tile_io(j, u, more=True):
                if more:
                    sp.wait_ge(f_xsp, j + 1)
                    sp.dma_start(xs_in[:, u, :], xs_dram[ds((j + 2) * P, P), :]).then_inc(f_xld[u], 16)
                sp.wait_ge(f_acc, FIRST + j + 2)
                sp.dma_start(ys_dram[ds(j * P, P), :], ys_out[:, u, :]).then_inc(f_yst[u], 16)
            with sp.Fori(0, (NS - 2) // 2) as j:
                tile_io(2 * j, 0)
                tile_io(2 * j + 1, 1)
            tile_io(NS - 3, 0)
            tile_io(NS - 2, 1, more=False)
            tile_io(NS - 1, 0, more=False)
            with sp.Fori(0, NT) as t:
                sp.wait_ge(f_done, t + 1)
                sp.dma_start(out.rearrange("b (t p) m -> p (b t) m", p=P)[:, ds(t, 1), :], x_all[:, ds(t, 1), :]
                             ).then_inc(st, 16)
            sp.wait_ge(st, 16 * NT)

        @block.gpsimd
        def _(pool):
            pool.memset(ident[:, :], 0.0).then_inc(c_done, 1)
            pool.wait_ge(c_done, 1)
            pool.affine_select(out=ident[:, :], in_=ident[:, :], compare_op=ALU.not_equal, fill=1.0, base=0,
                               pattern=[[-1, P]], channel_multiplier=1).then_inc(c_done, 1)
            n = 2
            pool.memset(one_col[:, :], 0.0).then_inc(c_done, 1)
            pool.wait_ge(c_done, n + 1)
            pool.memset(one_col[:, HG - 1:HG], 1.0).then_inc(c_done, 1)
            for k in range(2):
                cols = slice(k * 1024, (k + 1) * 1024)
                pool.wait_ge(w_hi_s, k + 1)
                pool.tensor_tensor(wk_lo[:, cols], stage_wk[k], wk_hi[:, cols], ALU.subtract).then_inc(w_split, 1)
            pool.memset(zeros[:, :], 0.0).then_inc(c_done, 1)
            pool.memset(ones_b[:, :], 1.0).then_inc(c_done, 1)
            pool.memset(before[:, :], 1.0).then_inc(c_done, 1)
            pool.iota(iota_s[:, :], pattern=[[1, NO]], base=0, channel_multiplier=0,
                      allow_small_or_imprecise_dtypes=True).then_inc(c_done, 1)
            n = 8
            pool.wait_ge(c_done, n)
            pool.affine_select(out=before[:, :], in_=before[:, :], compare_op=ALU.is_gt, fill=0.0, base=0,
                               pattern=[[1, P]], channel_multiplier=-1).then_inc(c_done, 1)
            for i in range(4):
                k, cols = i // 2, slice(i % 2 * 1024, (i % 2 + 1) * 1024)
                pool.wait_ge(w_hi_s, i + 3)
                pool.tensor_tensor(wq_lo[:, k, cols], (stage_wk + stage_wv)[i], wq_hi[:, k, cols], ALU.subtract
                                   ).then_inc(w_split, 1)

            flat = xn[:, :, :].rearrange("p t m -> p (t m)")
            w_f = flat[:, 0:CHUNK]
            w_16 = flat[:, CHUNK:2 * CHUNK].bitcast(F16).rearrange("p (s c) -> p s c", s=2)
            assert E % B == 0 and KT * F2 % CHUNK == 0 and CHUNK % DM == 0

            def split_weights(e, gate, up, down_w, n):
                for c in range(CHUNKS):
                    k, half = c // 2, c % 2
                    if c < 2 * KT:
                        src = (up if half else gate)[..., k * P:(k + 1) * P, :]
                        dst = w_f
                        if len(src.shape) == 3:
                            src = src.rearrange("a p f -> p (a f)")
                    else:
                        f = (c - 2 * KT) * (CHUNK // DM)
                        rows = down_w[..., f * P:f * P + CHUNK // DM * P, :]
                        dst = w_f.rearrange("p (f m) -> p f m", m=DM)
                        src = (rows.rearrange("a (f p) m -> p (a f) m", p=P) if len(rows.shape) == 3 else
                               rows.rearrange("(f p) m -> p f m", p=P))
                    pool.dma_start(dst, src).then_inc(w_loaded, 16)
                    pool.wait_ge(w_loaded, (n + c + 1) * 16)
                    pool.sem_inc(paced_pool, 1)
                    pool.tensor_copy(w_16[:, 0, :], w_f).then_inc(w_chain, 1)
                    pool.wait_ge(w_chain, (n + c) * 2 + 1)
                    pool.tensor_tensor(w_16[:, 1, :], w_f, w_16[:, 0, :], ALU.subtract).then_inc(w_chain, 1)
                    pool.wait_ge(w_chain, (n + c) * 2 + 2)
                    pool.dma_start(w16_dram[ds(e * P, P), :].rearrange("p (s c) -> p s c", s=2)[
                        :, :, c * CHUNK:(c + 1) * CHUNK], w_16).then_inc(w_stored, 16)
                    pool.wait_ge(w_stored, (n + c + 1) * 16)

            with pool.Fori(0, B) as b:
                chain = Chain(pool, pool_chain, b * POOL_STEPS, carrier=paced_pool)
                v, y, w = ssc[:, 0, :], ssc[:, 1, :], ssc[:, 2, :]
                pool.wait_ge(rk_guess, b + 1)
                pool.sem_inc(paced_pool, 1)
                newton(pool, chain, v, y, w)
                pool.sem_inc(rk_ready, 1)
                v, y, w = rs3[:, 0, :], rs3[:, 1, :], rs3[:, 2, :]
                for g in range(2):
                    heads = slice(g * HG, (g + 1) * HG)
                    pool.wait_ge(rq_guess, 2 * b + g + 1)
                    pool.sem_inc(paced_pool, 1)
                    newton(pool, chain, v, y, w)
                    y2 = y.rearrange("p (t h) -> p t h", t=QT)
                    chain(pool.tensor_scalar(rq[:, :, heads], y2, float(D) ** -0.5, None, ALU.mult))
                    pool.tensor_scalar(nrq[:, :, heads], y2, -float(D) ** -0.5, None, ALU.mult).then_inc(rq_ready, 1)
                assert chain.n == POOL_STEPS, chain.n
                for i in range(E // B):
                    e = b * (E // B) + i
                    w = gate_up[ds(e, 1)]
                    split_weights(e, w[:, :, 0:FF], w[:, :, FF:F2], down[ds(e, 1)], e * CHUNKS)
            split_weights(E, sh_gate, sh_up, sh_down, B * (E // B) * CHUNKS)
            pool.wait_ge(f_zero, 16 * NS)
            pool.wait_ge(f_pos, 1)
            for t in range(NT):
                pool.wait_ge(f_xr, t + 1)
                pool.indirect_dma_start(xs_dram, bass.IndirectOffsetOnAxis(pos_i[:, t:t + 1], 0), xn2[:, t, :], None
                                        ).then_inc(f_scat, 16)
            pool.wait_ge(f_yst[0], 16 * ((NS + 1) // 2))
            pool.wait_ge(f_yst[1], 16 * (NS // 2))
            for t in range(NT):
                pool.indirect_dma_start(ys_in[:, t, :], None, ys_dram, bass.IndirectOffsetOnAxis(pos_i[:, t:t + 1], 0)
                                        ).then_inc(f_gat[t // 4], 16)

        @block.tensor
        def _(pe):
            pe.wait_ge(c_done, 2)
            pe.wait_ge(ld["wk"], 32)
            for h in range(0, H, 4):
                for i in range(4):
                    m = pe.transpose(bank[h // 4][:, i * P:(i + 1) * P],
                                     stage_wk[h // 8][:, (h % 8 + i) * P:(h % 8 + i + 1) * P], ident[:, :])
                m.then_inc(wk_t, 1)
            pe.wait_ge(ld["wv"], 32)
            for h in range(0, H, 4):
                pe.wait_ge(wk_ts, h // 4 + 1)
                for i in range(4):
                    m = pe.transpose(bank[h // 4][:, i * P:(i + 1) * P],
                                     stage_wv[h // 8][:, (h % 8 + i) * P:(h % 8 + i + 1) * P], ident[:, :])
                m.then_inc(wv_t, 1)
            pe.wait_ge(ld["wo"], 32)
            for h in range(0, H, 2):
                if h % 4 == 0:
                    pe.wait_ge(wv_ts, h // 4 + 1)
                if h >= 4:
                    pe.wait_ge(vo_s, h // 2 - 1)
                for i in range(2):
                    n = h % 8 + i
                    m = pe.matmul(bank[4 + h % 4][:, i * DM:(i + 1) * DM], wvt[h // 8][:, n * P:(n + 1) * P],
                                  stage_wo[h // 8][:, n * DM:(n + 1) * DM], start=True, stop=True)
                m.then_inc(vo_ps, 1)
            for b in range(B):
                if b >= 2:
                    pe.wait_ge(xt_lo_s, b - 1)
                pe.wait_ge(xn_ready, b * QT + QT)
                for k in range(KT):
                    for t in range(QT):
                        m = pe.transpose(bank[5 + 2 * (b % 2)][:, k * SQ + t * P:k * SQ + (t + 1) * P],
                                         xn[:, (b * QT + t) % 4, k * P:(k + 1) * P], ident[:, :])
                m.then_inc(xt_ps, 1)
            pe.wait_ge(c_done, CONSTS)
            pe.wait_ge(vo_s, H // 2)
            pe.wait_ge(xt_lo_s, B)
            pe.wait_ge(w_split, 6)

            def ctx_t(b, c):
                if c == 0:
                    pe.wait_ge(ctx_ld, b * 32 + 32)
                    pe.wait_ge(s_scd, b * H * 8 + 16)
                elif c == 3:
                    pe.wait_ge(tp_lo, b * 4 + 1)
                for t in range(4 * c, min(4 * c + 4, NKT)):
                    r = KROWS[t]
                    m = pe.transpose(bank[c % 3][:, (t - 4 * c) * P:(t - 4 * c) * P + r], ctx_f[0:r, t, :],
                                     ident[0:r, 0:r])
                m.then_inc(tp_ps, 1)

            def key_tile(b, t, r):
                for g in range(4):
                    pe.wait_ge(kn_sq, (b * NKT + t) * 4 + g + 1)
                    cols = ds(t * P, r)
                    splits3(pe, bank[g][0:r, :], (ctxt_hi[:, cols], ctxt_lo[:, cols]),
                            (wk_hi[:, g * 512:(g + 1) * 512], wk_lo[:, g * 512:(g + 1) * 512])).then_inc(kn_ps, 1)

            def keys(b, last_head=None):
                pe.wait_ge(tp_lo, b * 4 + 4)
                pe.sem_inc(paced_pe, 1)
                key_tile(b, 0, P)
                if last_head is not None:
                    last_head()
                with pe.Fori(1, FT) as t:
                    key_tile(b, t, P)
                key_tile(b, FT, LAST)

            for c in range(4):
                ctx_t(0, c)
            keys(0)

            def batch(b, last=False):
                def q_mm(h, u):
                    pe.wait_ge(q_lo_s, b * H + h + 1)
                    for k in range(KT):
                        cols = slice(k * SQ, (k + 1) * SQ)
                        m = splits3(pe, bank[u][:, 0:SQ],
                                    (wq_hi[:, k, ds(h * P, P)], wq_lo[:, k, ds(h * P, P)]),
                                    (xnt_hi[:, ds(b, 1), cols], xnt_lo[:, ds(b, 1), cols]),
                                    start=(k == 0), stop=(k == KT - 1))
                    m.then_inc(q_ps, 1)

                def q_sums(h):
                    pe.wait_ge(q_sq_s, b * H + h + 1)
                    pe.sem_inc(paced_pe, 1)
                    if h == HG:
                        pe.wait_ge(rq_sum, 2 * b + 1)
                    pe.matmul(bank[6][0:HG, 0:SQ], one_col[:, HG - 1 - h % HG:2 * HG - 1 - h % HG], q_sq[:, h % 4, :],
                              start=(h % HG == 0), stop=(h % HG == HG - 1)).then_inc(rq_ps, 1)

                def q_sums_t(g, ps):
                    pe.wait_ge(rq_sum, 2 * b + g + 1)
                    pe.sem_inc(paced_pe, 1)
                    for t in range(QT):
                        m = pe.transpose(ps[:, t * HG:(t + 1) * HG], rs_rows[:, t * P:(t + 1) * P], ident[0:HG, 0:HG])
                    m.then_inc(rq_t, 1)

                def qp_mm(h, u):
                    pe.wait_ge(q_lo_s, b * H + h + 5)
                    pe.wait_ge(qp_lo_s, b * H + h + 1)
                    if h == HG + 1:
                        q_sums_t(0, bank[5][:, SQ:])
                    splits3(pe, bank[4 + u % 2][:, 0:SQ], (wkt_hi[:, ds(h, 1), :], wkt_lo[:, ds(h, 1), :]),
                            (q_hi[:, u, :], q_lo[:, u, :])).then_inc(qp_ps, 1)

                def rk_rows(c):
                    if c == 0:
                        pe.wait_ge(s_acc, b * H + 1)
                    pe.wait_ge(rk_ready, b + 1)
                    pe.wait_ge(rkt_c, 4 * b + c + 1)
                    pe.sem_inc(paced_pe, 1)
                    for t in range(4 * c, min(4 * c + 4, NKT)):
                        r, o = KROWS[t], (t - 4 * c) * P
                        m = pe.transpose(bank[7][0:H, o:o + r], ssc[0:r, 1, t * H:(t + 1) * H], ident[0:r, 0:r])
                    m.then_inc(rkt_tp, 1)

                for u in range(2):
                    pe.wait_ge(kn_sq, (b + 1) * NKT * 4 + u + 1)
                    q_mm(u, u)
                pe.wait_ge(kn_sq, (b + 1) * NKT * 4 + 4)
                pe.wait_ge(s_ol, b * H + 1)
                pe.sem_inc(paced_pe, 1)
                for h in range(8):
                    q_mm(h + 2, (h + 2) % 4)
                    qp_mm(h, h % 4)
                    q_sums(h)
                    if h in RK_ROWS:
                        rk_rows(RK_ROWS[h])

                for h in range(8, H):
                    if h + 2 < H:
                        q_mm(h + 2, (h + 2) % 4)
                    qp_mm(h, h % 4)
                    q_sums(h)
                    if h in RK_ROWS:
                        rk_rows(RK_ROWS[h])
                pe.wait_ge(qp_lo_s, (b + 1) * H + 2)

                def score(h, k):
                    n8 = (b * H + h) * 8
                    t, (c0, cn) = k // 4, CH[k % 4]
                    last = {0: -2, 1: -1, 2: -3}.get(k, k - 3)
                    pe.wait_ge(s_scd, n8 + last + 17)
                    q0 = (qp_hi[:, ds(h, 1), t * P:(t + 1) * P], qp_lo[:, ds(h, 1), t * P:(t + 1) * P])
                    splits3(pe, S_BANK[SCORE_BANK[k]][:, 0:cn], q0,
                            (ctxt_hi[:, c0:c0 + cn], ctxt_lo[:, c0:c0 + cn])).then_inc(s_sc, 1)

                def tr(h, u, g):
                    n = b * H + h
                    if g == 0:
                        pe.wait_ge(s_exp, n * 2 + 4)
                    last = {0: -1, 1: -3, 2: -2}.get(g, g - 3)
                    pe.wait_ge(s_lo, n * 7 + last + 8)
                    for s in range(2):
                        t = 2 * g + s
                        if t < NKT:
                            r = KROWS[t]
                            for q in range(QT):
                                m = pe.transpose(T_BANK[g % 3][0:r, s * SQ + q * P:s * SQ + (q + 1) * P],
                                                 SP[u][q][:, t * P:t * P + r], ident[:, :])
                    m.then_inc(s_tr, 1)

                def pv(h, g):
                    n = b * H + h
                    pe.wait_ge(s_lo, n * 7 + g + 8)
                    if g == 0:
                        pe.wait_ge(s_ol, n + 1)
                        pe.wait_ge(rq_guess, 2 * b + 2)
                    for s in range(2):
                        t = 2 * g + s
                        if t < NKT:
                            r = KROWS[t]
                            m = splits3(pe, O_BANK[:, 0:SQ], (ctx_hi[0:r, t, :], ctx_lo[0:r, t, :]),
                                        (pt_hi[0:r, g, s, :], pt_lo[0:r, g, s, :]), start=(t == 0), stop=(t == NKT - 1))
                    m.then_inc(s_pv, 1)

                def vo(h):
                    n = b * H + h
                    pe.wait_ge(s_ol, n + 2)
                    pe.wait_ge(s_acc, n + 1)
                    for q in range(QT):
                        m = splits3(pe, V_BANK[:, q * DM:(q + 1) * DM],
                                    (ot_hi[:, q * P:(q + 1) * P], ot_lo[:, q * P:(q + 1) * P]),
                                    (vo_hi[:, ds(h, 1), :], vo_lo[:, ds(h, 1), :]))
                    m.then_inc(s_vo, 1)

                def head(h, u, more=True, v=True, steps=PE_STEPS):
                    for step in steps.split():
                        kind, i = step[0], int(step[1:] or 0)
                        if kind == "S":
                            score(h + 1, i)
                        elif kind == "N" and more:
                            score(h + 2, i)
                        elif kind == "C":
                            tr(h, u, i)
                        elif kind == "D":
                            pv(h, i)
                        elif kind == "V" and v:
                            vo(h - 1)
                        elif kind == "P" and not last:
                            ctx_t(b + 1, i)

                for k in range(8):
                    score(0, k)
                    if k == 1:
                        q_sums_t(1, bank[6])
                for k in range(AHEAD):
                    score(1, k)
                head(0, 0, v=False)
                with pe.Fori(0, H // 2 - 2) as j:
                    head(2 * j + 1, 1)
                    head(2 * j + 2, 0)
                head(H - 3, 1)
                head(H - 2, 0, more=False)
                head(H - 1, 1, steps=PE_LAST)
                if last:
                    vo(H - 1)
                else:
                    keys(b + 1, lambda: vo(H - 1))

            with pe.Fori(0, B - 1) as b:
                batch(b)
            batch(B - 1, last=True)

            pe.wait_ge(s_acc, B * H + 1)
            pe.wait_ge(f_small, 16)
            for k in range(KT):
                m = pe.transpose(X_BANK[:, k * E:(k + 1) * E], rw[:, k * P:(k + 1) * P], ident[0:E, 0:E])
            m.then_inc(f_rt, 1)
            for g in range(NT // 2):
                pe.wait_ge(f_xn, 2 * g + 2)
                pe.wait_ge(f_tlo, g + 1)
                for i in range(2):
                    for k in range(KT):
                        m = pe.transpose(bank[g % 4][:, (i * KT + k) * P:(i * KT + k + 1) * P],
                                         xn2[:, 2 * g + i, k * P:(k + 1) * P], ident[:, :])
                m.then_inc(f_tp, 1)
            pe.wait_ge(f_rtc, 1)
            pe.wait_ge(f_tlo, NT // 2 + 4)
            for t in range(NT):
                for k in range(KT):
                    m = splits3(pe, logit_ps[:, t * E:(t + 1) * E], (xt_hi[:, t, k, :], xt_lo[:, t, k, :]),
                                (rwt_hi[:, k, :], rwt_lo[:, k, :]), start=(k == 0), stop=(k == KT - 1))
            m.then_inc(f_lg, 1)

            def ranks():
                pe.wait_ge(f_onehot, 1)
                flat = onehot_b[:, :, :].rearrange("p t e -> p (t e)")
                pe.matmul(rank_ps[:, 0:NT * E], before[:, :], flat, start=True, stop=True)
                pe.matmul(rank_ps[:, NT * E:2 * NT * E], ones_b[:, :], flat, start=True, stop=True).then_inc(f_rank, 1)

            def weights(kind, t, cols):
                if kind == "shared":
                    return w_hi[:, E, cols], w_lo[:, E, cols]
                return w_hi[:, ds(t, 1), cols], w_lo[:, ds(t, 1), cols]

            def owners_of(j):
                v = pe.value_load(owners3_i[0:1, ds(j, 1)], min_val=0, max_val=(1 << 3 * EB) - 1)
                return [((v >> EB * i) & (E - 1)) for i in range(3)]

            def gate_or_up(kind, half, e, i, t, u):
                if half == 0:
                    pe.wait_ge(f_silu, i + 1)
                    if kind == "routed":
                        pe.wait_ge(f_xsl, t + 2)
                else:
                    pe.wait_ge(f_h, i + 1)
                for k in range(KT):
                    lhs = ((xt_hi[:, ds(t, 1), k, :], xt_lo[:, ds(t, 1), k, :]) if kind == "shared" else
                           (xs_hi[:, u, k, :], xs_lo[:, u, k, :]))
                    m = splits3(pe, bank[2 * half + u][:, :], lhs,
                                weights(kind, e, slice(k * F2 + half * FF, k * F2 + (half + 1) * FF)),
                                start=(k == 0), stop=(k == KT - 1))
                m.then_inc(f_gu if half else f_g, 1)

            def mid_t(i, u):
                pe.wait_ge(f_h, i + 3)
                pe.wait_ge(f_hlo, i + 1)
                for f in range(FTT):
                    m = pe.transpose(bank[4 + u][:, f * P:(f + 1) * P], hmid[:, u, f * P:(f + 1) * P], ident[:, :])
                m.then_inc(f_ht, 1)

            def down_mm(kind, e, i, u):
                pe.wait_ge(f_hlo, i + 3)
                pe.wait_ge(f_acc, i + 1)
                for f in range(FTT):
                    m = splits3(pe, bank[6][:, 0:DM], (ht_hi[:, u, f, :], ht_lo[:, u, f, :]),
                                weights(kind, e, slice(KT * F2 + f * DM, KT * F2 + (f + 1) * DM)),
                                start=(f == 0), stop=(f == FTT - 1))
                m.then_inc(f_y, 1)

            def sorted_t(t, n, u):
                pe.wait_ge(f_xld[u], 16 * n + 16)
                pe.wait_ge(f_xsl, t + 1)
                for k in range(KT):
                    m = pe.transpose(bank[7][:, k * P:(k + 1) * P], xs_in[:, u, k * P:(k + 1) * P], ident[:, :])
                m.then_inc(f_xsp, 1)

            def tile(kind, i, t, n, u, e, e1, more2):
                more = e1 is not None
                if more:
                    gate_or_up(kind, 0, e1, i + 1, t + 1, 1 - u)
                mid_t(i, u)
                if more:
                    gate_or_up(kind, 1, e1, i + 1, t + 1, 1 - u)
                if more2 and kind == "routed":
                    sorted_t(t + 2, n + 1, u)
                down_mm(kind, e, i, u)

            def routed():
                kind = "routed"
                sorted_t(0, 0, 0)
                sorted_t(1, 0, 1)
                e = owners_of(0)[0]
                for half in range(2):
                    gate_or_up(kind, half, e, FIRST, 0, FIRST % 2)
                full = (NS - 2) // 2
                with pe.Fori(0, full) as j:
                    e0, e1, e2 = owners_of(j)
                    tile(kind, 2 * j + FIRST, 2 * j, j, FIRST % 2, e0, e1, True)
                    tile(kind, 2 * j + 1 + FIRST, 2 * j + 1, j, (FIRST + 1) % 2, e1, e2, True)
                e = owners_of(full)[0:NS - 2 * full] + [None]
                for t in range(2 * full, NS):
                    tile(kind, FIRST + t, t, t // 2, (t + FIRST) % 2, e[t - 2 * full], e[t - 2 * full + 1], t + 2 < NS)

            def shared(count, first, i0, p0):
                kind = "shared"
                for half in range(2):
                    gate_or_up(kind, half, E, i0, first, p0)
                pre = 4 if first == 0 else 0
                for t in range(pre):
                    tile(kind, t, t, t // 2, t % 2, E, E, True)
                    if t == RANKS_AFTER:
                        ranks()
                full = (count - 2) // 2
                if full > pre // 2:
                    with pe.Fori(pre // 2, full) as j:
                        for n in range(2):
                            tile(kind, 2 * j + n + i0, 2 * j + n + first, j, (n + p0) % 2, E, E, True)
                for t in range(2 * full, count):
                    tile(kind, i0 + t, first + t, t // 2, (t + p0) % 2, E, E if t + 1 < count else None, t + 2 < count)

            pe.wait_ge(f_w0, 16)
            shared(FIRST, 0, 0, 0)
            pe.wait_ge(f_w1, 16 * E)
            pe.wait_ge(f_owner, 1)
            routed()
            shared(NT - FIRST, FIRST, FIRST + NS, (FIRST + NS) % 2)

        @block.scalar
        def _(act):
            for k in range(2):
                if k == 0:
                    act.wait_ge(ld["wk"], 32)
                act.activation(wk_hi[:, k * 1024:(k + 1) * 1024], stage_wk[k], ACT.Copy).then_inc(w_hi_s, 1)
            act.wait_ge(gcol_s, 1)
            for h in range(0, H, 4):
                act.wait_ge(wk_t, h // 4 + 1)
                act.activation(wkt_hi[:, h:h + 4, :].rearrange("p h c -> p (h c)"), bank[h // 4][:, :], ACT.Copy,
                               scale=gcol[:, 2:3]).then_inc(wk_th, 1)
            for h in range(0, H, 4):
                act.wait_ge(wv_t, h // 4 + 1)
                act.activation(wvt[h // 8][:, four(h)], bank[h // 4][:, :], ACT.Copy).then_inc(wv_ts, 1)
            for h in range(0, H, 2):
                act.wait_ge(vo_ps, h // 2 + 1)
                act.activation(vo_hi[:, h:h + 2, :].rearrange("p h m -> p (h m)"), bank[4 + h % 4][:, :], ACT.Copy
                               ).then_inc(vo_h, 1)
            for n in range(4):
                k, s = n // 2, n % 2
                if n == 0:
                    act.wait_ge(ld["wq"], 64)
                act.activation(wq_hi[:, k, s * 1024:(s + 1) * 1024], (stage_wk + stage_wv)[n], ACT.Copy
                               ).then_inc(w_hi_s, 1)
            for b in range(B):
                act.wait_ge(xt_ps, b + 1)
                act.activation(xnt_hi[:, b, :], bank[5 + 2 * (b % 2)][:, :], ACT.Copy).then_inc(xt_hi_s, 1)
            act.wait_ge(ld["small"], 64)
            act.activation(gates[:, 2:4], gates[:, 0:2], ACT.Tanh).then_inc(gate_s, 1)

            def ctx_t_hi(b, c):
                c1 = min(KV, (c + 1) * 512)
                act.wait_ge(tp_ps, b * 4 + c + 1)
                act.activation(ctxt_hi[:, c * 512:c1], bank[c % 3][:, 0:c1 - c * 512], ACT.Copy).then_inc(tp_hi, 1)

            def keys(b):
                def squares(t, r):
                    for g in range(4):
                        i = (b * NKT + t) * 4 + g
                        act.wait_ge(kn_sum, i + 1)
                        act.wait_ge(kn_ps, i + 1)
                        act.activation(k_sq[0:r, g, :], bank[g][0:r, :], ACT.Square).then_inc(kn_sq, 1)
                with act.Fori(0, FT) as t:
                    squares(t, P)
                squares(FT, LAST)

            for c in range(4):
                ctx_t_hi(0, c)
            keys(0)

            def batch(b, last=False):
                def q_evac(h, u):
                    act.wait_ge(rq_ps, b * H + h + 1)
                    act.wait_ge(q_ps, b * H + h + 1)
                    act.activation(q_sq[:, u, :], bank[u][:, 0:SQ], ACT.Square).then_inc(q_sq_s, 1)
                    act.activation(q_hi[:, u, :], bank[u][:, 0:SQ], ACT.Copy).then_inc(q_hi_s, 1)

                def qp_evac(h, u):
                    act.wait_ge(qp_ps, b * H + h + 1)
                    act.activation(qp_hi[:, ds(h, 1), :], bank[4 + u % 2][:, 0:SQ], ACT.Copy).then_inc(qp_hi_s, 1)

                def rk_copy(c):
                    c1 = min(KV, (c + 1) * 512)
                    act.wait_ge(rkt_tp, 4 * b + c + 1)
                    act.activation(rkt[:, c * 512:c1], bank[7][0:H, 0:c1 - c * 512], ACT.Copy).then_inc(rkt_c, 1)

                q_evac(0, 0)
                q_evac(1, 1)
                for h in range(H):
                    if h + 2 < H:
                        q_evac(h + 2, (h + 2) % 4)
                    qp_evac(h, h % 4)
                    if h in RK_ROWS:
                        rk_copy(RK_ROWS[h])
                    if h in CTX_SPLIT:
                        r, w = CTX_SPLIT[h]
                        act.wait_ge(ctx_ld, b * 32 + 32)
                        act.wait_ge(s_pv, b * (H * NG) + NG)
                        act.activation(ctx_hi[0:r, w, :], ctx_f[0:r, w, :], ACT.Copy).then_inc(ctx_split, 1)

                def exps(h, u, q):
                    act.wait_ge(rq_ready, 2 * b + (1 if among_first(h, 1) else 2))
                    act.wait_ge(s_nb, (b * H + h) * 2 + q + 1)
                    act.activation(SP[u][q][:, :], SP[u][q][:, :], ACT.Exp, bias=nbias[:, q:q + 1],
                                   scale=rq[:, q, ds(h, 1)], accum_out=psum_p[:, u, q:q + 1]).then_inc(s_exp, 1)

                def p_hi(h, g):
                    n = b * H + h
                    act.wait_ge(s_pv, n * NG + g + 1)
                    act.wait_ge(s_tr, n * NG + g + 1)
                    for r, w in group_parts(g):
                        m = act.activation(pt_hi[0:r, g, w, :], T_BANK[g % 3][0:r, :].rearrange(
                            "p (s q) -> p s q", s=2)[:, w, :], ACT.Copy)
                    m.then_inc(s_hi, 1)

                def head(h, u, steps=ACT_STEPS):
                    for step in steps.split():
                        kind, i = step[0], int(step[1:] or 0)
                        if kind == "H":
                            p_hi(h, i)
                        elif kind == "X":
                            exps(h + 1, 1 - u, i)
                        elif kind == "P" and not last:
                            ctx_t_hi(b + 1, i)
                        elif kind == "O":
                            n = b * H + h
                            act.wait_ge(s_pv, n * NG + 2 * NG)
                            act.wait_ge(s_vo, n + 1)
                            act.activation(ot_hi[:, :], O_BANK[:, 0:SQ], ACT.Copy, scale=1.0 / P_SCALE).then_inc(s_oh, 1)

                for q in range(QT):
                    exps(0, 0, q)
                head(0, 0)
                with act.Fori(0, H // 2 - 2) as j:
                    head(2 * j + 1, 1)
                    head(2 * j + 2, 0)
                head(H - 3, 1)
                head(H - 2, 0)
                head(H - 1, 1, steps=ACT_LAST)
                if not last:
                    keys(b + 1)

            with act.Fori(0, B - 1) as b:
                batch(b)
            batch(B - 1, last=True)

            for g in range(NT // 2):
                act.wait_ge(f_tp, g + 1)
                act.activation(xt_hi[:, 2 * g:2 * g + 2, :, :].rearrange("p a k q -> p (a k q)"), bank[g % 4][:, :],
                               ACT.Copy).then_inc(f_thi, 1)
            act.wait_ge(f_lgc, 1)
            act.activation(smax[:, 1, :], smax[:, 0, :], ACT.Exp, scale=-1.0).then_inc(f_sel, 1)

            def silu_of(i, u):
                act.wait_ge(f_g, i + 1)
                act.wait_ge(f_h, i + 1)
                act.activation(silu[:, u, :], bank[u][:, :], ACT.Silu).then_inc(f_silu, 1)

            def h_hi(i, u):
                act.wait_ge(f_ht, i + 1)
                act.wait_ge(f_y, i + 1)
                act.activation(ht_hi[:, u, :, :].rearrange("p f q -> p (f q)"), bank[4 + u][:, :], ACT.Copy
                               ).then_inc(f_hhi, 1)

            def sorted_hi(t, u):
                act.wait_ge(f_xsp, t + 1)
                if not among_first(t, 2):
                    act.wait_ge(f_gu, FIRST + t - 1)
                act.activation(xs_hi[:, u, :, :].rearrange("p k q -> p (k q)"), bank[7][:, 0:DM], ACT.Copy
                               ).then_inc(f_xsh, 1)

            def y_out(i, t, n, u):
                act.wait_ge(f_y, i + 3)
                if not among_first(n, 1):
                    act.wait_ge(f_yst[u], 16 * n)
                act.activation(ys_out[:, u, :], bank[6][:, 0:DM], ACT.Copy).then_inc(f_acc, 1)

            def tile(kind, i, t, n, u, more, more2):
                if more:
                    silu_of(i + 1, 1 - u)
                h_hi(i, u)
                if kind == "routed":
                    if more2:
                        sorted_hi(t + 2, u)
                    y_out(i, t, n, u)

            def experts(kind, count, first, i0, p0):
                if kind == "routed":
                    sorted_hi(0, 0)
                    sorted_hi(1, 1)
                silu_of(i0, p0)
                peeled = 2 if kind == "routed" else 0
                for t in range(peeled):
                    tile(kind, i0 + t, first + t, t // 2, (t + p0) % 2, True, True)
                full = (count - 2) // 2
                with act.Fori(peeled // 2, full) as j:
                    for n in range(2):
                        tile(kind, 2 * j + n + i0, 2 * j + n + first, j, (n + p0) % 2, True, True)
                for t in range(2 * full, count):
                    tile(kind, i0 + t, first + t, t // 2, (t + p0) % 2, t + 1 < count, t + 2 < count)
            experts("shared", FIRST, 0, 0, 0)
            experts("routed", NS, 0, FIRST, FIRST % 2)
            experts("shared", NT - FIRST, FIRST, FIRST + NS, (FIRST + NS) % 2)

        @block.vector
        def _(dve):
            for s, v in ((s_scd, 16), (s_lo, 7), (s_pv, 7), (s_ol, 1), (s_acc, 1), (rkt_c, 1), (s_vo, 1), (s_exp, 2),
                         (kn_sq, 4), (kn_sum, 4), (q_lo_s, 4), (qp_lo_s, 2), (rq_ps, 4)):
                dve.sem_inc(s, v)
            setup = Chain(dve, setup_chain)
            setup(dve.memset(ssk[:, :, :], 1.0))
            dve.wait_ge(ld["small"], 64)
            dve.tensor_tensor(gcol[:, 2:3], gcol[:, 0:1], gcol[:, 1:2], ALU.mult).then_inc(gcol_s, 1)
            dve.wait_ge(gcol_s, 1)
            for h in range(0, H, 4):
                dve.wait_ge(wk_th, h // 4 + 1)
                flat = lambda a: a[:, h:h + 4, :].rearrange("p h c -> p (h c)")
                dve.scalar_tensor_tensor(out=flat(wkt_lo), in0=bank[h // 4][:, :], scalar=gcol[:, 2:3],
                                         in1=flat(wkt_hi), op0=ALU.mult, op1=ALU.subtract).then_inc(wk_ts, 1)
            dve.wait_ge(ld["x"], 16)
            for t in range(NT):
                dve.bn_stats(stats[:, t, :], x_all[:, t, :]).then_inc(ln_stats, 1)
            for t in range(NT):
                dve.wait_ge(ln_stats, t + 1)
                dve.bn_aggr(mv[:, t, :], stats[:, t, :]).then_inc(ln_aggr, 1)
            dve.wait_ge(ln_aggr, NT)
            v, y, w = (ssc[:, i, 0:NT] for i in range(3))
            setup(dve.tensor_scalar(v, mv[:, :, 1], EPS, None, ALU.add))
            rsqrt(dve, setup, v, y, w)
            for h in range(0, H, 2):
                flat = lambda a: a[:, h:h + 2, :].rearrange("p h m -> p (h m)")
                dve.wait_ge(vo_h, h // 2 + 1)
                dve.tensor_tensor(flat(vo_lo), bank[4 + h % 4][:, :], flat(vo_hi), ALU.subtract).then_inc(vo_s, 1)
            for b in range(B + 1):
                if b < B:
                    if b >= 2:
                        dve.wait_ge(xt_ps, b - 1)
                    for t in range(b * QT, b * QT + QT):
                        dve.tensor_scalar(xn[:, t % 4, :], x_all[:, t, :], mv[:, t, 0:1], ssc[:, 1, t:t + 1],
                                          ALU.subtract, ALU.mult).then_inc(xn_ready, 1)
                if b >= 1:
                    dve.wait_ge(xt_hi_s, b)
                    dve.tensor_tensor(xnt_lo[:, b - 1, :], bank[5 + 2 * ((b - 1) % 2)][:, :], xnt_hi[:, b - 1, :],
                                      ALU.subtract).then_inc(xt_lo_s, 1)
            dve.wait_ge(gate_s, 1)
            setup(dve.tensor_scalar(g1[:, :], gates[:, 2:3], P_SCALE, None, ALU.mult))

            def ctx_t_lo(b, c):
                c1 = min(KV, (c + 1) * 512)
                dve.wait_ge(tp_hi, b * 4 + c + 1)
                dve.tensor_tensor(ctxt_lo[:, c * 512:c1], bank[c % 3][:, 0:c1 - c * 512], ctxt_hi[:, c * 512:c1],
                                  ALU.subtract).then_inc(tp_lo, 1)

            def keys(b, last_head=None):
                def key_sums(t, r):
                    for g in range(4):
                        i = (b * NKT + t) * 4 + g
                        dve.wait_ge(kn_sq, i + 5)
                        dve.tensor_reduce(ssk[0:r, ds(t, 1), g * 4:(g + 1) * 4], k_sq[0:r, g, :].rearrange(
                            "p (h d) -> p h d", h=4), X, ALU.add).then_inc(kn_sum, 1)
                key_sums(0, P)
                if last_head is not None:
                    last_head()
                with dve.Fori(1, FT) as t:
                    key_sums(t, P)
                key_sums(FT, LAST)
                chain = Chain(dve, prep_chain, b * PREP_STEPS)
                dve.wait_ge(kn_sum, (b + 1) * NKT * 4 + 4)
                v, y, w = ssc[:, 0, :], ssc[:, 1, :], ssc[:, 2, :]
                chain(dve.tensor_scalar(v, ssk[:, :, :].rearrange("p t h -> p (t h)"), 1.0 / D, EPS, ALU.mult, ALU.add))
                guess(dve, chain, v, y, w).then_inc(rk_guess, 1)

            def ln_stat(tiles):
                for t in tiles:
                    dve.bn_stats(stats[:, t, :], x_all[:, t, :]).then_inc(ln_stats, 1)

            def ln_aggregate(tiles):
                for t in tiles:
                    dve.wait_ge(ln_stats, NT + t + 1)
                    dve.bn_aggr(mv[:, t, :], stats[:, t, :]).then_inc(ln_aggr, 1)

            for c in range(4):
                ctx_t_lo(0, c)
            keys(0)

            def batch(b, last=False):
                chain = Chain(dve, prep_chain, b * PREP_STEPS + 2)
                def q_sums_rows(g):
                    dve.wait_ge(rq_ps, b * H + (g + 1) * HG + 4)
                    dve.tensor_scalar(rs_rows[:, :], bank[6][0:HG, 0:SQ], 1.0 / D, EPS, ALU.mult, ALU.add
                                      ).then_inc(rq_sum, 1)

                def q_sums_guess(g, ps):
                    dve.wait_ge(rq_t, 2 * b + g + 1)
                    if g:
                        dve.wait_ge(rq_ready, 2 * b + g)
                    dve.sem_inc(paced_dve, 1)
                    v, y, w = rs3[:, 0, :], rs3[:, 1, :], rs3[:, 2, :]
                    chain(dve.tensor_copy(v, ps[:, 0:QT * HG]))
                    guess(dve, chain, v, y, w).then_inc(rq_guess, 1)

                def q_rest(h, u):
                    dve.wait_ge(q_hi_s, b * H + h + 1)
                    dve.tensor_tensor(q_lo[:, u, :], bank[u][:, 0:SQ], q_hi[:, u, :], ALU.subtract).then_inc(q_lo_s, 1)

                def qp_rest(h, u):
                    dve.wait_ge(qp_hi_s, b * H + h + 1)
                    dve.tensor_tensor(qp_lo[:, ds(h, 1), :], bank[4 + u % 2][:, 0:SQ], qp_hi[:, ds(h, 1), :], ALU.subtract
                                      ).then_inc(qp_lo_s, 1)
                q_rest(0, 0)
                q_rest(1, 1)
                with dve.Fori(0, 2) as j:
                    for u in range(4):
                        q_rest(4 * j + u + 2, (u + 2) % 4)
                        qp_rest(4 * j + u, u)
                for h in range(8, H):
                    if h == HG:
                        q_sums_rows(0)
                    if h + 2 < H:
                        q_rest(h + 2, (h + 2) % 4)
                    if h == HG + 1:
                        dve.wait_ge(qp_hi_s, b * H + h + 1)
                        q_sums_guess(0, bank[5][:, SQ:])
                    qp_rest(h, h % 4)
                    if h in CTX_SPLIT:
                        r, w = CTX_SPLIT[h]
                        dve.wait_ge(ctx_split, b * 3 + list(CTX_SPLIT).index(h) + 1)
                        dve.tensor_tensor(ctx_lo[0:r, w, :], ctx_f[0:r, w, :], ctx_hi[0:r, w, :], ALU.subtract
                                          ).then_inc(ctx_lo_s, 1)
                    if last:
                        ln_stat(range(2 * (h - 8), min(2 * (h - 7), NT - QT)))
                if last:
                    ln_aggregate(range(NT - QT))
                dve.wait_ge(ctx_lo_s, b * 3 + 3)
                dve.sem_inc(ctx_free, 1)
                def scaled(h, u, k):
                    n, q, (c0, cn) = b * H + h, k // 4, CH[k % 4]
                    if k == 0:
                        dve.wait_ge(rk_ld[u], 8 * (n - u) + 16)
                    dve.wait_ge(s_sc, 8 * n + k + 1)
                    dve.sem_inc(paced_dve, 1)
                    dve.tensor_tensor_reduce(SP[u][q][:, c0:c0 + cn], S_BANK[SCORE_BANK[k]][:, 0:cn],
                                             RK[u][:, c0:c0 + cn], 1.0, NEG, ALU.mult, ALU.max,
                                             mx4[:, q, k % 4:k % 4 + 1]).then_inc(s_scd, 1)

                q_sums_rows(1)
                scaled(0, 0, 0)
                scaled(0, 0, 1)
                q_sums_guess(1, bank[6])
                assert chain.n + 2 == PREP_STEPS, chain.n

                def bias(h, q):
                    n = b * H + h
                    dve.wait_ge(s_scd, 8 * n + 4 * q + 4 + 16)
                    dve.wait_ge(s_exp, 2 * n + q + 1)
                    dve.tensor_reduce(mx[:, q:q + 1], mx4[:, q, :], X, ALU.max).then_inc(max_chain, 1)
                    dve.wait_ge(rq_ready, 2 * b + (1 if among_first(h, 1) else 2))
                    dve.wait_ge(max_chain, 2 * n + q + 1)
                    dve.tensor_scalar(nbias[:, q:q + 1], mx[:, q:q + 1], nrq[:, q, ds(h, 1)], LN_P_SCALE,
                                      ALU.mult, ALU.add).then_inc(s_nb, 1)

                def p_rest(h, g):
                    n = b * H + h
                    dve.wait_ge(s_hi, n * NG + g + 1)
                    for r, w in group_parts(g):
                        m = dve.tensor_tensor(pt_lo[0:r, g, w, :], T_BANK[g % 3][0:r, :].rearrange(
                            "p (s q) -> p s q", s=2)[:, w, :], pt_hi[0:r, g, w, :], ALU.subtract)
                    m.then_inc(s_lo, 1)

                def ot_rest(h, u):
                    n = b * H + h
                    dve.wait_ge(s_oh, n + 1)
                    dve.scalar_tensor_tensor(out=ot_lo[:, :], in0=O_BANK[:, 0:SQ], scalar=1.0 / P_SCALE,
                                             in1=ot_hi[:, :], op0=ALU.mult, op1=ALU.subtract).then_inc(s_ol, 1)
                    dve.wait_ge(s_acc, n + 1)
                    dve.reciprocal(rden[:, :], psum_p[:, u, :]).then_inc(den_chain, 1)
                    dve.wait_ge(den_chain, 2 * n + 1)
                    dve.tensor_scalar(rden[:, :], rden[:, :], g1[:, 0:1], None, ALU.mult).then_inc(den_chain, 1)

                def add_head(h):
                    n = b * H + h
                    dve.wait_ge(den_chain, 2 * n + 2)
                    dve.wait_ge(s_vo, n + 2)
                    for q in range(QT):
                        xt = x_all[:, ds(b * QT + q, 1), :]
                        m = dve.scalar_tensor_tensor(out=xt, in0=V_BANK[:, q * DM:(q + 1) * DM],
                                                     scalar=rden[:, q:q + 1], in1=xt, op0=ALU.mult, op1=ALU.add)
                    m.then_inc(s_acc, 1)

                def head(h, u, more=True, add=True, steps=DVE_STEPS):
                    for step in steps.split():
                        kind, i = step[0], int(step[1:] or 0)
                        if kind == "T":
                            scaled(h + 1, 1 - u, i)
                        elif kind == "N" and more:
                            scaled(h + 2, u, i)
                        elif kind == "M":
                            bias(h + 1, i)
                        elif kind == "L":
                            p_rest(h, i)
                        elif kind == "O":
                            ot_rest(h, u)
                        elif kind == "A" and add:
                            add_head(h - 1)
                        elif kind == "P" and not last:
                            ctx_t_lo(b + 1, i)

                for k in range(2, 8):
                    scaled(0, 0, k)
                    if k % 4 == 3:
                        bias(0, k // 4)
                for k in range(AHEAD):
                    scaled(1, 1, k)
                head(0, 0, add=False)
                with dve.Fori(0, H // 2 - 2) as j:
                    head(2 * j + 1, 1)
                    head(2 * j + 2, 0)
                head(H - 3, 1)
                head(H - 2, 0, more=False)
                head(H - 1, 1, steps=DVE_LAST)
                if last:
                    add_head(H - 1)
                else:
                    keys(b + 1, lambda: add_head(H - 1))

            with dve.Fori(0, B - 1) as b:
                batch(b)
            batch(B - 1, last=True)

            for sm, v in ((f_tlo, 4), (f_silu, 2), (f_h, 2), (f_hlo, 2), (f_acc, 1), (f_y, 2), (f_xsl, 1)):
                dve.sem_inc(sm, v)
            chain = Chain(dve, f_chain)
            dve.wait_ge(s_acc, B * H + 1)
            ln_stat(range(NT - QT, NT))
            ln_aggregate(range(NT - QT, NT))
            dve.wait_ge(ln_aggr, 2 * NT)
            v, y, w = (ssc[:, i, 0:NT] for i in range(3))
            chain(dve.tensor_scalar(v, mv[:, :, 1], EPS, None, ALU.add))
            rsqrt(dve, chain, v, y, w)
            for t in range(NT):
                dve.tensor_scalar(xn2[:, t, :], x_all[:, t, :], mv[:, t, 0:1], ssc[:, 1, t:t + 1],
                                  ALU.subtract, ALU.mult).then_inc(f_xn, 1)
            dve.wait_ge(f_rt, 1)
            chain(dve.tensor_copy(rwt_hi[:, :, :].rearrange("p k e -> p (k e)"), X_BANK[:, 0:KT * E]))
            dve.tensor_tensor(rwt_lo[:, :, :].rearrange("p k e -> p (k e)"), X_BANK[:, 0:KT * E],
                              rwt_hi[:, :, :].rearrange("p k e -> p (k e)"), ALU.subtract).then_inc(f_rtc, 1)
            for g in range(NT // 2):
                flat = lambda a: a[:, 2 * g:2 * g + 2, :, :].rearrange("p a k q -> p (a k q)")
                dve.wait_ge(f_thi, g + 1)
                dve.tensor_tensor(flat(xt_lo), bank[g % 4][:, :], flat(xt_hi), ALU.subtract).then_inc(f_tlo, 1)

            dve.wait_ge(f_lg, 1)
            chain(dve.tensor_copy(logit[:, :, :].rearrange("p t e -> p (t e)"), logit_ps))
            dve.tensor_reduce(smax[:, 0, :], logit[:, :, :], X, ALU.max).then_inc(f_lgc, 1)
            chain(dve.memset(smax[:, 3, :], 1.0))

            def choose(first, last):
                dve.wait_ge(f_lgc, 1)
                for e in range(first, last):
                    chain(dve.tensor_tensor(smax[:, 2, :], logit[:, :, e], smax[:, 0, :], ALU.is_equal))
                    chain(dve.tensor_tensor(onehot[:, :, e], smax[:, 2, :], smax[:, 3, :], ALU.mult))
                    chain(dve.tensor_tensor(smax[:, 3, :], smax[:, 3, :], onehot[:, :, e], ALU.subtract))
                if last == E:
                    dve.tensor_copy(onehot_b[:, :, :], onehot[:, :, :]).then_inc(f_onehot, 1)

            def scale_tokens(first, last):
                if first == 0:
                    dve.wait_ge(f_sel, 1)
                    chain(dve.tensor_scalar(smax[:, 1, :], smax[:, 1, :], 1.0, None, ALU.add))
                    chain(dve.reciprocal(smax[:, 1, :], smax[:, 1, :]))
                for t in range(first, last):
                    dve.tensor_scalar(xn2[:, t, :], xn2[:, t, :], smax[:, 1, t:t + 1], None, ALU.mult).then_inc(f_xr, 1)

            def expert_tiles():
                dve.wait_ge(f_rank, 1)
                chain(dve.tensor_copy(slot[:, :, :].rearrange("p t e -> p (t e)"), rank_ps[:, 0:NT * E]))
                chain(dve.tensor_copy(count[:, :, :].rearrange("p t e -> p (t e)"), rank_ps[:, NT * E:2 * NT * E]))
                chain(dve.tensor_reduce(ecol[:, 0, :], count[:, :, :].rearrange("p t e -> p e t"), X, ALU.add))
                chain(dve.tensor_scalar(etile[:, :], ecol[:, 0, :], float(P - 1), None, ALU.add))
                chain(dve.tensor_scalar(etile[:, :], etile[:, :], P.bit_length() - 1, None, ALU.logical_shift_right))
                chain(dve.tensor_copy(ecol[:, 1, :], etile[:, :]))
                chain(dve.tensor_copy(ecol[:, 2, 0:1], ecol[:, 1, 0:1]))
                for e in range(1, E):
                    chain(dve.tensor_tensor(ecol[:, 2, e:e + 1], ecol[:, 2, e - 1:e], ecol[:, 1, e:e + 1], ALU.add))
                chain(dve.tensor_tensor(ecol[:, 3, :], ecol[:, 2, :], ecol[:, 1, :], ALU.subtract))
                chain(dve.tensor_scalar(run[:, 0, :], ecol[:, 3, :], float(P), None, ALU.mult))

            def first_slots(first, last):
                for t in range(first, last):
                    chain(dve.tensor_tensor(run[:, t, :], run[:, t - 1, :], count[:, t - 1, :], ALU.add))

            def token_slots():
                chain(dve.tensor_tensor(slot[:, :, :], slot[:, :, :], run[:, :, :], ALU.add))
                chain(dve.tensor_tensor(slot[:, :, :], slot[:, :, :], onehot[:, :, :], ALU.mult))
                chain(dve.tensor_reduce(pos[:, :], slot[:, :, :], X, ALU.add))
                dve.tensor_copy(pos_i[:, :], pos[:, :]).then_inc(f_pos, 1)

            def tile_owners():
                chain(dve.tensor_scalar(owner[:, :], iota_s[:, :], ecol[:, 2, 0:1], None, ALU.is_ge))
                for e in range(1, E - 1):
                    chain(dve.scalar_tensor_tensor(out=owner[:, :], in0=iota_s[:, :], scalar=ecol[:, 2, e:e + 1],
                                                   in1=owner[:, :], op0=ALU.is_ge, op1=ALU.add))
                o = [owner[:, i:i + 2 * (NO // 2) - 1:2] for i in range(3)]
                chain(dve.scalar_tensor_tensor(out=owners3[:, :], in0=o[1], scalar=float(1 << EB), in1=o[0],
                                               op0=ALU.mult, op1=ALU.add))
                chain(dve.scalar_tensor_tensor(out=owners3[:, :], in0=o[2], scalar=float(1 << 2 * EB),
                                               in1=owners3[:, :], op0=ALU.mult, op1=ALU.add))
                dve.tensor_copy(owners3_i[:, :], owners3[:, :]).then_inc(f_owner, 1)

            def routing(t):
                if t == 0:
                    choose(0, E // 2)
                elif t == 1:
                    choose(E // 2, E)
                elif t == 3:
                    expert_tiles()
                elif t == 4:
                    first_slots(1, NT)
                    token_slots()
                elif t == 5:
                    scale_tokens(0, NT)
                elif t == 6:
                    tile_owners()

            def add_routed(t):
                if t % 4 == 0:
                    dve.wait_ge(f_gat[t // 4], 4 * 16)
                if t < FIRST:
                    dve.wait_ge(f_acc, t + 2)
                else:
                    dve.wait_ge(f_acc, t + NS + 2)
                dve.scalar_tensor_tensor(out=x_all[:, t, :], in0=ys_in[:, t, :], scalar=gates[:, 3:4],
                                         in1=x_all[:, t, :], op0=ALU.mult, op1=ALU.add).then_inc(f_done, 1)

            def mid(i, u):
                dve.wait_ge(f_gu, i + 1)
                dve.wait_ge(f_silu, i + 3)
                dve.tensor_tensor(hmid[:, u, :], bank[2 + u][:, :], silu[:, u, :], ALU.mult).then_inc(f_h, 1)

            def h_lo(i, u):
                dve.wait_ge(f_hhi, i + 1)
                dve.tensor_tensor(ht_lo[:, u, :, :].rearrange("p f q -> p (f q)"), bank[4 + u][:, :],
                                  ht_hi[:, u, :, :].rearrange("p f q -> p (f q)"), ALU.subtract).then_inc(f_hlo, 1)

            def add_shared(i, t):
                xt = x_all[:, ds(t, 1), :]
                dve.wait_ge(f_y, i + 3)
                dve.scalar_tensor_tensor(out=xt, in0=bank[6][:, 0:DM], scalar=gates[:, 3:4], in1=xt,
                                         op0=ALU.mult, op1=ALU.add).then_inc(f_acc, 1)

            def sorted_lo(t, u):
                dve.wait_ge(f_xsh, t + 1)
                dve.tensor_tensor(xs_lo[:, u, :, :].rearrange("p k q -> p (k q)"), bank[7][:, 0:DM],
                                  xs_hi[:, u, :, :].rearrange("p k q -> p (k q)"), ALU.subtract).then_inc(f_xsl, 1)

            def tile(kind, i, t, u, more, more2):
                h_lo(i, u)
                if more:
                    mid(i + 1, 1 - u)
                if kind == "routed" and more2:
                    sorted_lo(t + 2, u)
                if kind == "shared":
                    add_shared(i, t)

            def experts(kind, count, first, i0, p0):
                if kind == "routed":
                    sorted_lo(0, 0)
                    sorted_lo(1, 1)
                mid(i0, p0)
                if kind == "shared":
                    for t in range(count):
                        tile(kind, i0 + t, first + t, (t + p0) % 2, t + 1 < count, t + 2 < count)
                        if first == 0:
                            routing(t)
                        elif t >= count - 2:
                            for n in range(4 * (t + 2 - count), 4 * (t + 3 - count)):
                                add_routed(n)
                else:
                    full = (count - 2) // 2
                    with dve.Fori(0, full) as j:
                        for n in range(2):
                            tile(kind, 2 * j + n + i0, 2 * j + n + first, (n + p0) % 2, True, True)
                    for t in range(2 * full, count):
                        tile(kind, i0 + t, first + t, (t + p0) % 2, t + 1 < count, t + 2 < count)
            experts("shared", FIRST, 0, 0, 0)
            experts("routed", NS, 0, FIRST, FIRST % 2)
            experts("shared", NT - FIRST, FIRST, FIRST + NS, (FIRST + NS) % 2)
            for t in range(8, NT):
                add_routed(t)


_INS = ['x', 'ctx_1024', 'g_xattn', 'g_ffn', 'L0_xattn_Wq', 'L0_xattn_Wk', 'L0_xattn_Wv', 'L0_xattn_Wo',
        'L0_xattn_gq', 'L0_xattn_gk', 'L0_ffn_router_w', 'L0_ffn_gate_up_proj', 'L0_ffn_down_proj',
        'L0_ffn_shared_gate_w', 'L0_ffn_shared_up_w', 'L0_ffn_shared_down_w']
_OUTS = [((8, 256, 256), 'float32')]


def kernel(**inputs):
    import numpy as _np
    import concourse.bacc as _bacc
    from concourse import mybir as _mybir
    from concourse.bass_utils import run_bass_kernel_spmd as _run

    nc = _bacc.Bacc("TRN2", target_bir_lowering=False, num_devices=1)
    arrays, args = {}, []
    for name in _INS:
        a = _np.ascontiguousarray(inputs[name])
        arrays[f"in_{name}_dram"] = a
        args.append(nc.dram_tensor(f"in_{name}_dram", a.shape, _mybir.dt.from_np(a.dtype), kind="ExternalInput").ap())
    for i, (shape, dtype) in enumerate(_OUTS):
        dt = _mybir.dt.from_np(_np.dtype(dtype))
        args.append(nc.dram_tensor(f"out_{i}_dram", shape, dt, kind="ExternalOutput").ap())
    flamingo_layer(nc, *args)
    r = _run(nc, [arrays], core_ids=[0])
    return r.results[0]["out_0_dram"]
```
